# Optimizing a Trainium2 kernel written in Bass

```python
import numpy as np
import jax
import jax.numpy as jnp

def _softmax(x, axis=-1):
    return jax.nn.softmax(x, axis=axis)

def _gelu(x):
    return jax.nn.gelu(x, approximate=True)

def _silu(x):
    return jax.nn.silu(x)

def _sigmoid(x):
    return jax.nn.sigmoid(x)

def _layernorm(x, axis=-1, eps=1e-05):
    m = jnp.mean(x, axis=axis, keepdims=True)
    v = jnp.var(x, axis=axis, keepdims=True)
    return (x - m) / jnp.sqrt(v + eps)

def _scatter_add(tgt, idx, src, axis=0):
    return tgt.at[idx].add(src)

def _segment_sum(src, seg, n):
    return jax.ops.segment_sum(src, seg, n)
kernel_name = 'mk_gnn_preln_d4_gnn_r8_7f565c'

def setup_inputs(seed: int=0):
    np.random.seed(seed)
    _w = jnp.asarray

    def _rec_inputs():
        import jax
        import jax.numpy as jnp
        _gk = jax.random.key(seed)
        x = -0.0005121 + 1.001 * jax.random.normal(jax.random.fold_in(_gk, 1), (6250, 64), jnp.float32)
        src = jax.random.randint(jax.random.fold_in(_gk, 2), (200000,), 0, 6250, jnp.int32)
        dst = jnp.minimum((6250 * jax.random.uniform(jax.random.fold_in(_gk, 3), (200000,)) ** 2.0).astype(jnp.int32), 49999)
        _o = jnp.argsort(dst, stable=True)
        src = src[_o]
        dst = dst[_o]
        edge_attr_32 = 0.000102155 + 1.00015 * jax.random.normal(jax.random.fold_in(_gk, 12), (200000, 32), jnp.float32)
        return (x, src, dst, edge_attr_32)
    x, src, dst, edge_attr_32 = _rec_inputs()

    def _L0_gnn_setup():
        import jax, jax.numpy as jnp
        import numpy as np
        N = 6250
        E = 100000
        IN = 64
        H = 4
        D = 16
        OH = H * D
        SCALE = float(np.sqrt(IN))
        LN_EPS = 1e-05
        key = jax.random.key(seed)
        ks = jax.random.split(key, 16)
        w = 0.05
        return {'feats': jax.random.normal(ks[0], (N, IN), jnp.float32), 'Wq': jax.random.normal(ks[1], (IN, OH), jnp.float32) * w, 'bq': jnp.zeros((OH,), jnp.float32), 'Wk': jax.random.normal(ks[2], (IN, OH), jnp.float32) * w, 'bk': jnp.zeros((OH,), jnp.float32), 'Wv': jax.random.normal(ks[3], (IN, OH), jnp.float32) * w, 'bv': jnp.zeros((OH,), jnp.float32), 'Wo': jax.random.normal(ks[4], (OH, OH), jnp.float32) * w, 'bo': jnp.zeros((OH,), jnp.float32), 'Wf': jax.random.normal(ks[5], (IN, OH), jnp.float32) * w, 'bf': jnp.zeros((OH,), jnp.float32), 'gamma': jnp.ones((OH,), jnp.float32), 'beta': jnp.zeros((OH,), jnp.float32), 'src': jax.random.randint(ks[6], (E,), 0, N, jnp.int32), 'dst': jax.random.randint(ks[7], (E,), 0, N, jnp.int32)}
    _L0_gnn_all = _L0_gnn_setup()
    _L0_gnn_in = {k: v for k, v in _L0_gnn_all.items() if k in ('Wq', 'bq', 'Wk', 'bk', 'Wv', 'bv', 'Wo', 'bo', 'Wf', 'bf', 'gamma', 'beta')}
    del _L0_gnn_all

    def _L1_gnn_setup():
        import jax, jax.numpy as jnp
        import numpy as np
        N_NODES = 12500
        N_EDGES = 200000
        IN_CH = 64
        OUT_CH = 64
        key = jax.random.key(seed)
        k1, k2, k3, k4 = jax.random.split(key, 4)
        x = jax.random.normal(k1, (N_NODES, IN_CH), dtype=jnp.float32)
        edge_index = jax.random.randint(k2, (2, N_EDGES), 0, N_NODES, dtype=jnp.int64)
        scale = float(np.sqrt(6.0 / (IN_CH + OUT_CH)))
        W = jax.random.uniform(k3, (IN_CH, OUT_CH), dtype=jnp.float32, minval=-scale, maxval=scale)
        b = jax.random.uniform(k4, (OUT_CH,), dtype=jnp.float32, minval=-0.1, maxval=0.1)
        return {'x': x, 'edge_index': edge_index, 'W': W, 'b': b}
    _L1_gnn_all = _L1_gnn_setup()
    _L1_gnn_in = {k: v for k, v in _L1_gnn_all.items() if k in ('W', 'b')}
    del _L1_gnn_all

    def _L2_gnn_setup():
        import jax, jax.numpy as jnp
        import numpy as np
        N_NODES = 12500
        N_EDGES = 125000
        NODE_DIM = 64
        EDGE_DIM = 32
        HIDDEN = 64

        def _unif(key, shape, fan_in):
            bound = 1.0 / np.sqrt(fan_in)
            return jax.random.uniform(key, shape, jnp.float32, -bound, bound)
        key = jax.random.key(seed)
        ks = jax.random.split(key, 11)
        node_features = jax.random.normal(ks[0], (N_NODES, NODE_DIM), jnp.float32)
        edge_index = jax.random.randint(ks[1], (2, N_EDGES), 0, N_NODES, dtype=jnp.int64)
        edge_features = jax.random.normal(ks[2], (N_EDGES, EDGE_DIM), jnp.float32)
        in_dim = 2 * NODE_DIM + EDGE_DIM
        W1 = _unif(ks[3], (HIDDEN, in_dim), in_dim)
        b1 = _unif(ks[4], (HIDDEN,), in_dim)
        W2 = _unif(ks[5], (HIDDEN, HIDDEN), HIDDEN)
        b2 = _unif(ks[6], (HIDDEN,), HIDDEN)
        w_ih = _unif(ks[7], (3 * NODE_DIM, HIDDEN), NODE_DIM)
        w_hh = _unif(ks[8], (3 * NODE_DIM, NODE_DIM), NODE_DIM)
        b_ih = _unif(ks[9], (3 * NODE_DIM,), NODE_DIM)
        b_hh = _unif(ks[10], (3 * NODE_DIM,), NODE_DIM)
        return {'node_features': node_features, 'edge_index': edge_index, 'edge_features': edge_features, 'W1': W1, 'b1': b1, 'W2': W2, 'b2': b2, 'w_ih': w_ih, 'w_hh': w_hh, 'b_ih': b_ih, 'b_hh': b_hh}
    _L2_gnn_all = _L2_gnn_setup()
    _L2_gnn_in = {k: v for k, v in _L2_gnn_all.items() if k in ('W1', 'b1', 'W2', 'b2', 'w_ih', 'w_hh', 'b_ih', 'b_hh')}
    del _L2_gnn_all

    def _L3_gnn_setup():
        import jax, jax.numpy as jnp
        import numpy as np
        N_NODES = 12500
        N_EDGES = 200000
        D_FEAT = 64
        key = jax.random.key(seed)
        k1, k2, k3 = jax.random.split(key, 3)
        embeddings = jax.random.normal(k1, (N_NODES, D_FEAT), dtype=jnp.float32)
        src = jax.random.randint(k2, (N_EDGES,), 0, N_NODES)
        dst = jax.random.randint(k3, (N_EDGES,), 0, N_NODES)
        return {'embeddings': embeddings, 'src': src, 'dst': dst, 'n_nodes': N_NODES}
    _L3_gnn_all = _L3_gnn_setup()
    _L3_gnn_in = {k: v for k, v in _L3_gnn_all.items() if k in ()}
    del _L3_gnn_all
    return {'x': x, 'src': src, 'dst': dst, 'edge_attr_32': edge_attr_32, 'L0_gnn_Wq': _L0_gnn_in['Wq'], 'L0_gnn_bq': _L0_gnn_in['bq'], 'L0_gnn_Wk': _L0_gnn_in['Wk'], 'L0_gnn_bk': _L0_gnn_in['bk'], 'L0_gnn_Wv': _L0_gnn_in['Wv'], 'L0_gnn_bv': _L0_gnn_in['bv'], 'L0_gnn_Wo': _L0_gnn_in['Wo'], 'L0_gnn_bo': _L0_gnn_in['bo'], 'L0_gnn_Wf': _L0_gnn_in['Wf'], 'L0_gnn_bf': _L0_gnn_in['bf'], 'L0_gnn_gamma': _L0_gnn_in['gamma'], 'L0_gnn_beta': _L0_gnn_in['beta'], 'L1_gnn_W': _L1_gnn_in['W'], 'L1_gnn_b': _L1_gnn_in['b'], 'L2_gnn_W1': _L2_gnn_in['W1'], 'L2_gnn_b1': _L2_gnn_in['b1'], 'L2_gnn_W2': _L2_gnn_in['W2'], 'L2_gnn_b2': _L2_gnn_in['b2'], 'L2_gnn_w_ih': _L2_gnn_in['w_ih'], 'L2_gnn_w_hh': _L2_gnn_in['w_hh'], 'L2_gnn_b_ih': _L2_gnn_in['b_ih'], 'L2_gnn_b_hh': _L2_gnn_in['b_hh']}

def reference(x, src, dst, edge_attr_32, L0_gnn_Wq, L0_gnn_bq, L0_gnn_Wk, L0_gnn_bk, L0_gnn_Wv, L0_gnn_bv, L0_gnn_Wo, L0_gnn_bo, L0_gnn_Wf, L0_gnn_bf, L0_gnn_gamma, L0_gnn_beta, L1_gnn_W, L1_gnn_b, L2_gnn_W1, L2_gnn_b1, L2_gnn_W2, L2_gnn_b2, L2_gnn_w_ih, L2_gnn_w_hh, L2_gnn_b_ih, L2_gnn_b_hh):
    import jax
    import jax.numpy as jnp

    def _L0_gnn_ref(feats, Wq, bq, Wk, bk, Wv, bv, Wo, bo, Wf, bf, gamma, beta, src, dst):
        import jax, jax.numpy as jnp
        import numpy as np
        N = 6250
        E = 100000
        IN = 64
        H = 4
        D = 16
        OH = H * D
        SCALE = float(np.sqrt(IN))
        LN_EPS = 1e-05
        n = feats.shape[0]
        q = (feats @ Wq + bq).reshape(n, H, D)
        k = (feats @ Wk + bk).reshape(n, H, D)
        v = (feats @ Wv + bv).reshape(n, H, D)
        score = jnp.sum(k[src] * q[dst], axis=-1)
        score = jnp.exp(jnp.clip(score / SCALE, -5.0, 5.0))
        wv = jax.ops.segment_sum(v[src] * score[..., None], dst, num_segments=n)
        z = jax.ops.segment_sum(score, dst, num_segments=n)
        wv = wv / (z[..., None] + 1.0)
        o = wv.reshape(n, OH) @ Wo + bo
        h = feats @ Wf + bf + o
        mu = jnp.mean(h, axis=-1, keepdims=True)
        var = jnp.var(h, axis=-1, keepdims=True)
        ln = (h - mu) * jax.lax.rsqrt(var + LN_EPS) * gamma + beta
        return h + ln

    def _L1_gnn_ref(x, edge_index, W, b):
        import jax, jax.numpy as jnp
        import numpy as np
        N_NODES = 12500
        N_EDGES = 200000
        IN_CH = 64
        OUT_CH = 64
        N = x.shape[0]
        loops = jnp.arange(N, dtype=edge_index.dtype)
        src = jnp.concatenate([edge_index[0], loops])
        dst = jnp.concatenate([edge_index[1], loops])
        ones = jnp.ones(src.shape[0], dtype=x.dtype)
        deg = jax.ops.segment_sum(ones, dst, num_segments=N)
        deg_inv_sqrt = jnp.where(deg > 0, jax.lax.rsqrt(deg), 0.0)
        norm = deg_inv_sqrt[src] * deg_inv_sqrt[dst]
        xw = x @ W
        msg = xw[src] * norm[:, None]
        out = jax.ops.segment_sum(msg, dst, num_segments=N) + b
        return jax.nn.relu(out)

    def _L2_gnn_ref(node_features, edge_index, edge_features, W1, b1, W2, b2, w_ih, w_hh, b_ih, b_hh):
        import jax, jax.numpy as jnp
        import numpy as np
        N_NODES = 12500
        N_EDGES = 125000
        NODE_DIM = 64
        EDGE_DIM = 32
        HIDDEN = 64

        def _unif(key, shape, fan_in):
            bound = 1.0 / np.sqrt(fan_in)
            return jax.random.uniform(key, shape, jnp.float32, -bound, bound)
        src, dst = (edge_index[0], edge_index[1])
        x = jnp.concatenate([node_features[src], node_features[dst], edge_features], axis=-1)
        h = jax.nn.relu(x @ W1.T + b1)
        messages = h @ W2.T + b2
        agg = jax.ops.segment_sum(messages, dst, num_segments=node_features.shape[0])
        gi = agg @ w_ih.T + b_ih
        gh = node_features @ w_hh.T + b_hh
        i_r, i_z, i_n = jnp.split(gi, 3, axis=-1)
        h_r, h_z, h_n = jnp.split(gh, 3, axis=-1)
        r = jax.nn.sigmoid(i_r + h_r)
        z = jax.nn.sigmoid(i_z + h_z)
        n = jnp.tanh(i_n + r * h_n)
        return (1.0 - z) * n + z * node_features

    def _L3_gnn_ref(embeddings, src, dst, n_nodes):
        import jax, jax.numpy as jnp
        import numpy as np
        N_NODES = 12500
        N_EDGES = 200000
        D_FEAT = 64
        ones = jnp.ones(src.shape[0], dtype=embeddings.dtype)
        out_deg = jnp.clip(jax.ops.segment_sum(ones, src, num_segments=n_nodes), 1.0)
        in_deg = jnp.clip(jax.ops.segment_sum(ones, dst, num_segments=n_nodes), 1.0)
        h = embeddings * (out_deg ** (-0.5))[:, None]
        agg = jax.ops.segment_sum(h[src], dst, num_segments=n_nodes)
        return agg * (in_deg ** (-0.5))[:, None]
    edge_index = jnp.stack([src, dst])
    h = jnp.maximum(_layernorm(x, axis=-1), 0.0)
    x = x + _L0_gnn_ref(h, L0_gnn_Wq, L0_gnn_bq, L0_gnn_Wk, L0_gnn_bk, L0_gnn_Wv, L0_gnn_bv, L0_gnn_Wo, L0_gnn_bo, L0_gnn_Wf, L0_gnn_bf, L0_gnn_gamma, L0_gnn_beta, src, dst)
    h = jnp.maximum(_layernorm(x, axis=-1), 0.0)
    x = x + _L1_gnn_ref(h, edge_index, L1_gnn_W, L1_gnn_b)
    h = jnp.maximum(_layernorm(x, axis=-1), 0.0)
    x = x + _L2_gnn_ref(h, edge_index, edge_attr_32, L2_gnn_W1, L2_gnn_b1, L2_gnn_W2, L2_gnn_b2, L2_gnn_w_ih, L2_gnn_w_hh, L2_gnn_b_ih, L2_gnn_b_hh)
    h = jnp.maximum(_layernorm(x, axis=-1), 0.0)
    x = x + _L3_gnn_ref(h, src, dst, 6250)
    return x

_drawn_inputs = setup_inputs


def setup_inputs(seed=0):
    import zlib

    import numpy as np

    out = dict(_drawn_inputs(seed))
    spreads = {'L0_gnn_bq': (0.0, 0.8),
     'L0_gnn_bk': (0.0, 2.0),
     'L0_gnn_bv': (0.0, 0.1),
     'L0_gnn_bo': (0.0, 0.1),
     'L0_gnn_bf': (0.0, 0.1),
     'L0_gnn_gamma': (1.0, 0.2),
     'L0_gnn_beta': (0.0, 0.1)}
    factors = {'L0_gnn_Wq': 8.0, 'L0_gnn_Wk': 8.0, 'L2_gnn_b_ih': 4.624, 'L2_gnn_b_hh': 7.098}
    for name, (base, spread) in spreads.items():
        noise = np.random.default_rng([zlib.crc32(name.encode()), seed]).standard_normal(out[name].shape)
        drawn = base * np.exp(spread * noise) if base else spread * noise
        out[name] = jnp.asarray(drawn.astype(out[name].dtype))
    for name, factor in factors.items():
        out[name] = (out[name] * factor).astype(out[name].dtype)
    return out
```

```python
from contextlib import ExitStack

import concourse.bass as bass
from concourse import mybir

ALU = mybir.AluOpType
ACT = mybir.ActivationFunctionType
AX = mybir.AxisListType
F32 = mybir.dt.float32
BF16 = mybir.dt.bfloat16
I32 = mybir.dt.int32

P = 128
NODES, EDGES, D, DE = 6250, 200000, 64, 32
HEADS, DH = 4, 16
TILES = -(-NODES // P)
NPAD = TILES * P
FULL = NODES // P
REST = NODES - FULL * P
CHUNKS = -(-EDGES // P)
EPAD = CHUNKS * P
U = 4
R = 4
STEPS = -(-(CHUNKS + TILES - 1) // (U * R)) * U * R
ROUNDS = STEPS // (U * R)
SB = -(-(STEPS + U * R) // P)
SPAD = SB * P
NTAB = 4 * -(-SB // 4)
N_WEIGHTS = 29
GT = 7
NR = TILES // GT
W0 = D + HEADS + 1
SCALE = float(D) ** -0.5
CLIP = 5.0 / SCALE
EPS = 1e-5
BIG = 1 << 16
OUTSIDE = 1000.0
TILE_BITS, CHUNK_BITS = 64, 2048
assert TILES % GT == 0 and TILES <= TILE_BITS and CHUNKS <= CHUNK_BITS and REST > 0


def build_gnn(nc, x, src, dst, attr, wq, bq, wk, bk, wv, bv, wo, bo, wf, bf, gamma, beta,
              w_gcn, b_gcn, w1t, b1, w2t, b2, wiht, whht, bih, bhh, out):
    with ExitStack() as ctx:
        def sb(name, shape, dt=F32):
            return ctx.enter_context(nc.sbuf_tensor(name, shape, dt))

        def sem(name):
            return ctx.enter_context(nc.semaphore(name))

        def dram(name, shape, dt=F32):
            return nc.dram_tensor(name, shape, dt).ap()

        dst_s, src_s, attr_s = dram("dst_s", [EPAD], I32), dram("src_s", [EPAD], I32), dram("attr_s", [EPAD, DE])
        kv_rows = dram("kv_rows", [NPAD, 2 * D])
        rows = [dram(f"rows{n}", [NPAD, D]) for n in range(3)]
        tiles_d, chunks_d = dram("tiles_d", [SPAD // U], I32), dram("chunks_d", [SPAD // 2], I32)

        xs = sb("xs", [P, TILES, D])
        h = sb("h", [P, TILES, D])
        q = sb("q", [P, TILES, D])
        y = sb("y", [P, TILES, D])
        stage = sb("stage", [P, 2, TILES * D])
        acc = sb("acc", [P, U, TILES * W0])
        cnt = sb("cnt", [P, TILES])
        outdeg = sb("outdeg", [P, TILES])
        small = sb("small", [P, 4, TILES])
        rd = sb("rd", [P, 3, TILES])
        z1 = sb("z1", [P, TILES, HEADS])
        dloc = sb("dloc", [P, SPAD])
        sidx = sb("sidx", [P, SPAD], I32)
        slo, shi = sb("slo", [P, SPAD]), sb("shi", [P, SPAD])
        tpk = sb("tpk", [1, 2 + SPAD // U], I32)
        cpk = sb("cpk", [1, SPAD // 2], I32)
        idx = sb("idx", [P, R, U], I32)
        gat = sb("gat", [P, R, U, 2 * D])
        oh = sb("oh", [P, R, U, P])
        oht = sb("oht", [P, 2, U, P])
        msg = sb("msg", [P, 2, U, W0])
        prod = sb("prod", [P, 2, U * D])
        sc = sb("sc", [P, 2, 2, U * HEADS])
        att = sb("att", [P, R, U, DE])
        attT = sb("attT", [P, 2, P])
        olo = oht[:, :, :, :].rearrange("p a u n -> p (a u n)").bitcast(BF16).rearrange("p (k u n) -> p k u n", k=R, u=U)
        ohi = prod[:, :, :].rearrange("p a n -> p (a n)").bitcast(BF16)[:, 0:R * U * TILES].rearrange("p (k u n) -> p k u n", k=R, u=U)
        hb = gat[:, :, :, :].rearrange("p k u d -> p (k u d)")[:, 0:2 * GT * D].rearrange("p (m t d) -> p m t d", m=2, t=GT)
        hT = sb("hT", [D + 1, 2, GT * P])
        ident = sb("ident", [P, P])
        iota_i, iota = sb("iota_i", [P, P], I32), sb("iota", [P, P])
        step_i, step = sb("step_i", [P, SB], I32), sb("step", [P, SB])
        zeros = sb("zeros", [P, U * W0])
        zerob = sb("zerob", [P, P], BF16)
        ones = sb("ones", [1, P])
        padi = sb("padi", [1, 2, P], I32)
        w_kvqf = sb("w_kvqf", [D + 1, 4 * D])
        w_o, w_g = sb("w_o", [D + 1, D]), sb("w_g", [D + 1, D])
        w_pq, w_m = sb("w_pq", [D + 1, 2 * D]), sb("w_m", [D + 1, D])
        w_i, w_h = sb("w_i", [D + 1, 4 * D]), sb("w_h", [D + 1, 4 * D])
        w_e = sb("w_e", [P, U * D])
        brow, bc = sb("brow", [1, 4 * D]), sb("bc", [P, 4 * D])
        CW = CHUNKS
        crow = stage[0:1, :, :].rearrange("p a n -> p (a n)")[:, 0:4 * CW].rearrange("p (a n) -> p a n", a=4)
        crow_i = h[0:1, :, :].rearrange("p t d -> p (t d)")[:, 0:2 * CW].bitcast(I32).rearrange("p (a n) -> p a n", a=2)
        chunk_no = q[0:1, :, :].rearrange("p t d -> p (t d)")[:, 0:CW]
        cs = sb("cs", [P, 6, SB])
        cs_i = sb("cs_i", [P, SB], I32)
        packf = prod[0:SB, :, :].rearrange("p a n -> p (a n)")[:, 0:3 * P].rearrange("p (a n) -> p a n", a=3)
        pack_i = attT[0:SB, 0, :].bitcast(I32)
        flat = acc[:, :, :].rearrange("p u n -> p (u n)")
        off_b, dw_b, mask_b = (flat[:, n * CW:(n + 1) * CW] for n in range(3))
        dg = flat[:, 3 * CW:3 * CW + SPAD].bitcast(I32)
        sg = flat[:, 3 * CW + SPAD:3 * CW + 2 * SPAD].bitcast(I32)
        df, vf = flat[:, 0:SPAD], flat[:, SPAD:2 * SPAD]
        sf = stage[:, 0, 0:SPAD]
        hi_i, lo_i = stage[:, 1, 0:SPAD].bitcast(I32), h[:, :, :].rearrange("p t d -> p (t d)")[:, 0:SPAD].bitcast(I32)
        hif = q[:, :, :].rearrange("p t d -> p (t d)")[:, 0:SPAD]
        lof = y[:, :, :].rearrange("p t d -> p (t d)")[:, 0:SPAD]

        ps = ctx.enter_context(nc.psum_tensor("ps", [P, 8, 512], F32))

        s_x, s_w, s_copy, s_pad = sem("x_loaded"), sem("weights_loaded"), sem("edges_copied"), sem("edges_padded")
        s_acopy = sem("attributes_copied_and_padded")
        s_ends = sem("chunk_ends_loaded")
        s_pool = sem("pool_constants")
        s_const = sem("constants_ready")
        s_rows = sem("rows_ready")
        s_bc = sem("broadcast_done")
        s_bcc = sem("table_block_copied")
        s_cidx = sem("chunk_numbers_ready")
        s_eg = sem("edge_rows_landed")
        s_eg2 = sem("source_rows_landed")
        s_tabs = sem("tables_ready_by_step")
        s_tabt = sem("table_block_turned")
        s_packt, s_packed, s_packd, s_packl = sem("steps_turned"), sem("steps_packed"), sem("packed_stored"), sem("packed_loaded")
        s_d = sem("vector_chain")
        s_var, s_sd = sem("variances_ready"), sem("deviations_ready")
        s_stage, s_table = sem("table_staged"), sem("table_stored")
        s_gates, s_gact = sem("gates_ready"), sem("gates_done")
        s_hist = sem("sources_counted")
        s_fin, s_out = sem("result_ready"), sem("result_stored")

        NPROD = 6
        PJ = [dict(ready=sem(f"proj{n}_input"), hb=sem(f"proj{n}_staged"), tr=sem(f"proj{n}_turned"),
                   ht=sem(f"proj{n}_turned_copied"), mm=sem(f"proj{n}_product"), ev=sem(f"proj{n}_taken"))
              for n in range(NPROD)]
        L = [dict(idx=sem(f"l{n}_indices"), land=[sem(f"l{n}_landed{k}") for k in range(R)],
                  oh=sem(f"l{n}_onehot"), t=sem(f"l{n}_onehot_turned"), oht=sem(f"l{n}_turned_copied"),
                  qe=sem(f"l{n}_dst_rows"), prod=sem(f"l{n}_combined"), red=sem(f"l{n}_reduced"),
                  clip=sem(f"l{n}_clipped"), exp=sem(f"l{n}_act"), used=sem(f"l{n}_rows_used"),
                  agg=sem(f"l{n}_summed"), acc=sem(f"l{n}_accumulated"))
             for n in range(4)]
        s_att = [sem(f"attr_landed{k}") for k in range(R)]
        s_atc = sem("attr_turned")

        block = ctx.enter_context(nc.Block())

        def proj_specs():
            flats = stage[:, :, :].rearrange("p a n -> p (a n)")
            kv = flats.rearrange("p (t c) -> p t c", c=2 * D)
            gates = flat[:, 0:TILES * 4 * D].rearrange("p (t c) -> p t c", c=4 * D)
            pst = stage[:, 0, :].rearrange("p (t c) -> p t c", c=D)
            return [
                ([(h, w_kvqf)], 4 * D, [(0, 2 * D, kv), (2 * D, 3 * D, q), (3 * D, 4 * D, y)]),
                ([(h, w_o)], D, [(0, D, pst)]),
                ([(h, w_g)], D, [(0, D, y)]),
                ([(h, w_pq)], 2 * D, [(0, D, pst), (D, 2 * D, q)]),
                ([(y, w_i), (h, w_h)], 4 * D, [(0, 4 * D, gates)]),
                ([(y, w_m)], D, [(0, D, pst)]),
            ]

        SPEC = proj_specs()
        outp = ps[:, 2:6, :].rearrange("p b (j c) -> p (b j) c", c=4 * D)

        def rounds(eng, body):
            body(0)
            with eng.Fori(1, NR) as i:
                body(i)

        def wait_last(eng, semaphore, count):
            if not isinstance(count, int) or count > 0:
                eng.wait_ge(semaphore, count)

        def round_tiles(a, i):
            return a[:, bass.ds(i * GT, GT), :]

        def proj_pool(pool, n):
            s, srcs = PJ[n], SPEC[n][0]
            M = len(srcs)

            def body(i):
                wait_last(pool, s["tr"], i * M)
                pool.wait_ge(s["ready"], 1)
                for m, (a, _) in enumerate(srcs):
                    nc.gpsimd.tensor_copy(hb[:, m, :, :], round_tiles(a, i)).then_inc(s["hb"], 1)

            rounds(pool, body)

        def proj_pe(pe, n):
            s, srcs, width = PJ[n], SPEC[n][0], SPEC[n][1]
            M = len(srcs)

            def body(i):
                for m in range(M):
                    staged, copied = i * M + m + 1, i * M + m
                    if not isinstance(i, int):
                        staged, copied = pe.to_reg(staged), pe.to_reg(copied)
                    pe.wait_ge(s_pool, 2)
                    pe.wait_ge(s["hb"], staged)
                    wait_last(pe, s["ht"], copied)
                    for t in range(GT):
                        mm = nc.tensor.transpose(ps[0:D, t // 4, (t % 4) * P:(t % 4 + 1) * P], hb[:, m, t, :], ident[:, :])
                    mm.then_inc(s["tr"], 1)
                pe.wait_ge(s["ht"], (i + 1) * M)
                wait_last(pe, s["ev"], i)
                for t in range(GT):
                    for m, (_, w) in enumerate(srcs):
                        mm = nc.tensor.matmul(outp[:, t, 0:width], hT[:, m, t * P:(t + 1) * P], w[:, 0:width],
                                              start=m == 0, stop=m == M - 1)
                mm.then_inc(s["mm"], 1)

            rounds(pe, body)

        def proj_act(act, n):
            s, M = PJ[n], len(SPEC[n][0])

            def body(i):
                for m in range(M):
                    wait_last(act, s["mm"], i)
                    act.wait_ge(s["tr"], i * M + m + 1)
                    nc.scalar.copy(hT[0:D, m, 0:4 * P], ps[0:D, 0, :])
                    nc.scalar.copy(hT[0:D, m, 4 * P:GT * P], ps[0:D, 1, 0:(GT - 4) * P]).then_inc(s["ht"], 1)

            rounds(act, body)

        def proj_dve(dve, n):
            s, dests = PJ[n], SPEC[n][2]

            def body(i):
                for k, (a, b, to) in enumerate(dests):
                    if k == 0:
                        dve.wait_ge(s["mm"], i + 1)
                        dve.wait_ge(s_const, 1)
                    ins = nc.vector.tensor_copy(round_tiles(to, i)[:, :, 0:b - a], outp[:, 0:GT, a:b])
                ins.then_inc(s["ev"], 1)

            rounds(dve, body)

        def edge_pool(pool, n, table, width, free):
            s = L[n]
            with pool.Fori(0, ROUNDS) as i:
                for k in range(R):
                    count = pool.to_reg(i * R + k + 1)
                    pool.wait_ge(s_table, 16 * (n + 1))
                    pool.wait_ge(s[free], count)
                    pool.wait_ge(s["idx"], count)
                    for u in range(U):
                        nc.gpsimd.indirect_dma_start(
                            gat[:, k, u, 0:width], None, table,
                            bass.IndirectOffsetOnAxis(ap=idx[:, k, u:u + 1], axis=0)).then_inc(s["land"][k], 16)

        def first_indices(act, n):
            act.wait_ge(s_bcc, NTAB)
            for k in range(R):
                nc.scalar.copy(idx[:, k, :], sidx[:, k * U:(k + 1) * U]).then_inc(L[n]["idx"], 1)

        def next_indices(act, n, i, k):
            act.wait_ge(L[n]["land"][k], (i + 1) * 16 * U)
            act.wait_ge(s_bcc, NTAB)
            nc.scalar.copy(idx[:, k, :], sidx[:, bass.ds((i * R + k + R) * U, U)]).then_inc(L[n]["idx"], 1)

        def one_hot(dve, n, i, k, extra=False):
            kk = k % R
            at = (i * R + k) * U
            ins = nc.vector.tensor_tensor(
                oh[:, kk, :, :], iota[:, :].unsqueeze(1).to_broadcast([P, U, P]),
                dloc[:, bass.ds(at, U)].unsqueeze(2).to_broadcast([P, U, P]), ALU.is_equal)
            if extra:
                nc.vector.tensor_tensor(
                    olo[:, kk, :, :], iota[:, :].unsqueeze(1).to_broadcast([P, U, P]),
                    slo[:, bass.ds(at, U)].unsqueeze(2).to_broadcast([P, U, P]), ALU.is_equal)
                ins = nc.vector.tensor_tensor(
                    ohi[:, kk, :, :], iota[:, 0:TILES].unsqueeze(1).to_broadcast([P, U, TILES]),
                    shi[:, bass.ds(at, U)].unsqueeze(2).to_broadcast([P, U, TILES]), ALU.is_equal)
            ins.then_inc(L[n]["oh"], 1)

        def tile_of(eng, packed, u):
            return nc.s_assert_within(eng.snap((packed >> (6 * u)) & (TILE_BITS - 1)), 0, TILES - 1,
                                      skip_runtime_bounds_check_because="tiles are clamped where they are packed")

        def load_tiles(eng, g):
            packed = eng.value_load(tpk[0:1, bass.ds(g + 2, 1)])
            return [tile_of(eng, packed, u) for u in range(U)]

        def accumulate(dve, n, g, k, lag, places, width):
            s, bank = L[n], (k + lag) % 2
            dve.wait_ge(s["agg"], g + R + 1 - lag)
            dve.wait_ge(s["acc"], g + 1)
            for u in range(U):
                a = acc[:, u, bass.ds(places[u] * width, width)]
                ins = nc.vector.tensor_tensor(a, a, ps[:, 4 + bank, u * width:(u + 1) * width], ALU.add)
            ins.then_inc(s["acc"], 1)

        def zero_acc(dve, n, width):
            nc.vector.memset(acc[:, :, 0:TILES * width], 0.0).then_inc(L[n]["acc"], 1)
            dve.wait_ge(L[n]["acc"], 1)

        def zero_sums(pe, n, lag, width):
            pe.wait_ge(L[n]["acc"], 1)
            nc.tensor.matmul(ps[:, 4 + lag % 2, 0:U * width], zeros[:, 0:P], zeros[:, 0:U * width],
                             start=True, stop=True).then_inc(L[n]["agg"], R + 1 - lag)

        def zero_group(dve, n):
            s = L[n]
            nc.vector.memset(oh[:, R - 1, :, :], 0.0)
            if n == 0:
                nc.vector.memset(gat[:, R - 1, :, :], 0.0)
            nc.vector.memset(msg[:, 1, :, 0:W0 - 1], 0.0).then_inc(s["exp"], 1)
            nc.vector.memset(small[:, 0, 0:1], 0.0).then_inc(s["used"], R - 1 if n == 0 else R)

        def sum_edges(pe, n, g, k, width, rhs):
            pe.wait_ge(L[n]["acc"], g + 1)
            for u in range(U):
                mm = nc.tensor.matmul(ps[:, 4 + k % 2, u * width:(u + 1) * width], oh[:, k, u, :], rhs(u),
                                      start=True, stop=True)
            return mm

        def sum_messages(pe, n, g, k1, width):
            s = L[n]
            if n == 0:
                pe.wait_ge(s["used"], g + R)
            else:
                pe.wait_ge(s["exp"], g + 1)
            sum_edges(pe, n, g, k1, width, lambda u: msg[:, k1 % 2, u, 0:width]).then_inc(s["agg"], 1)

        def turn_onehot(pe, n, at, kk, b):
            for u in range(U):
                mm = nc.tensor.transpose(ps[:, b, u * P:(u + 1) * P], oh[:, kk, u, :], ident[:, :])
            mm.then_inc(L[n]["t"], 1)

        def dst_rows(pe, n, i, k, first):
            b = k % 2
            places = load_tiles(pe, i * R + k)
            pe.wait_ge(L[n]["oht"], i * R + k + 1)
            if first is not None:
                first()
            qf = q[:, :, :].rearrange("p t d -> p (t d)")
            for u in range(U):
                mm = nc.tensor.matmul(ps[:, 2 + b, u * D:(u + 1) * D], oht[:, b, u, :],
                                      qf[:, bass.ds(places[u] * D, D)], start=first is None, stop=True,
                                      skip_group_check=True)
            mm.then_inc(L[n]["qe"], 1)

        @block.sync
        def _(sp):
            sp.wait_ge(s_const, 1)
            for t0, t1, r in ((0, FULL, P), (FULL, TILES, REST)):
                part = x[t0 * P:t0 * P + (t1 - t0 - 1) * P + r, :].rearrange("(t p) f -> p t f", p=r)
                sp.dma_start(xs[0:r, t0:t1, :], part).then_inc(s_x, 16)
            sp.dma_start(dst_s[0:EDGES].rearrange("(a b) -> a b", b=160), dst.rearrange("(a b) -> a b", b=160)).then_inc(s_copy, 16)
            sp.dma_start(src_s[0:EDGES].rearrange("(a b) -> a b", b=160), src.rearrange("(a b) -> a b", b=160)).then_inc(s_copy, 16)
            sp.dma_start(crow_i[0:1, 0, :], dst.rearrange("(a o) -> o a", a=EDGES)[:, 0:EDGES:P], allow_slow_non_contiguous=True).then_inc(s_ends, 16)
            sp.dma_start(crow_i[0:1, 1, 0:CHUNKS - 1], dst.rearrange("(a o) -> o a", a=EDGES)[:, P - 1:EDGES:P], allow_slow_non_contiguous=True).then_inc(s_ends, 16)
            sp.dma_start(crow_i[0:1, 1, CHUNKS - 1:CHUNKS], dst[EDGES - 1:EDGES].rearrange("(o a) -> o a", o=1)).then_inc(s_ends, 16)
            sp.dma_start(dst_s[EDGES:EPAD].rearrange("(o a) -> o a", o=1), padi[0:1, 0, 0:EPAD - EDGES]).then_inc(s_pad, 16)
            sp.dma_start(src_s[EDGES:EPAD].rearrange("(o a) -> o a", o=1), padi[0:1, 1, 0:EPAD - EDGES]).then_inc(s_pad, 16)
            wload = [(w_kvqf[0:D, 0:D], wk), (w_kvqf[0:D, D:2 * D], wv), (w_kvqf[0:D, 2 * D:3 * D], wq),
                     (w_kvqf[0:D, 3 * D:4 * D], wf), (w_o[0:D, :], wo), (w_g[0:D, :], w_gcn),
                     (w_pq[0:D, 0:D], w1t[0:D, :]), (w_pq[0:D, D:2 * D], w1t[D:2 * D, :]), (w_m[0:D, :], w2t),
                     (w_i[0:D, 0:3 * D], wiht), (w_h[0:D, 0:2 * D], whht[:, 0:2 * D]),
                     (w_h[0:D, 3 * D:4 * D], whht[:, 2 * D:3 * D])]
            row = lambda v: v.rearrange("(o a) -> o a", o=1)
            wload += [(w_kvqf[D:D + 1, 0:D], row(bk)), (w_kvqf[D:D + 1, D:2 * D], row(bv)),
                      (w_kvqf[D:D + 1, 2 * D:3 * D], row(bq)), (w_kvqf[D:D + 1, 3 * D:4 * D], row(bf)),
                      (w_o[D:D + 1, :], row(bo)), (w_pq[D:D + 1, 0:D], row(b1)), (w_i[D:D + 1, 0:3 * D], row(bih)),
                      (w_h[D:D + 1, 0:2 * D], row(bhh[0:2 * D])), (w_h[D:D + 1, 3 * D:4 * D], row(bhh[2 * D:3 * D]))]
            wload += [(brow[0:1, n * D:(n + 1) * D], row(v)) for n, v in enumerate((gamma, beta, b_gcn, b2))]
            wload += [(w_e[DE * u:DE * (u + 1), D * u:D * (u + 1)], w1t[2 * D:2 * D + DE, :]) for u in range(U)]
            for to, of in wload:
                sp.dma_start(to, of).then_inc(s_w, 16)
            assert len(wload) == N_WEIGHTS
            sp.wait_ge(s_packed, 2)
            sp.dma_start(tiles_d.rearrange("(a b) -> a b", b=P // U), pack_i[:, 0:P // U]).then_inc(s_packd, 16)
            sp.dma_start(chunks_d.rearrange("(a b) -> a b", b=P // 2), pack_i[:, P // U:P // U + P // 2]).then_inc(s_packd, 16)
            sp.wait_ge(s_packd, 32)
            sp.dma_start(tpk[0:1, 2:2 + SPAD // U], tiles_d.rearrange("(o a) -> o a", o=1)).then_inc(s_packl, 16)
            sp.dma_start(cpk[:, :], chunks_d.rearrange("(o a) -> o a", o=1)).then_inc(s_packl, 16)
            sp.dma_start(attr_s[0:EDGES, :].rearrange("(a b) f -> a (b f)", b=125), attr.rearrange("(a b) f -> a (b f)", b=125)).then_inc(s_acopy, 16)
            sp.dma_start(attr_s[EDGES:EPAD, :], zeros[0:EPAD - EDGES, 0:DE]).then_inc(s_acopy, 16)
            sp.wait_ge(PJ[0]["ev"], NR)
            sp.dma_start(kv_rows.rearrange("(t p) f -> p t f", p=P),
                         stage[:, :, :].rearrange("p a (t f) -> p (a t f)", f=D).rearrange("p (t f) -> p t f", f=2 * D)).then_inc(s_table, 16)
            for n in range(2):
                sp.wait_ge(*((s_stage, 1), (PJ[3]["ev"], NR))[n])
                sp.dma_start(rows[n].rearrange("(t p) f -> p t f", p=P), (y[:, :, :], stage[:, 0, :].rearrange("p (t f) -> p t f", f=D))[n]).then_inc(s_table, 16)
            sp.wait_ge(s_packl, 32)
            sp.wait_ge(s_acopy, 32)
            def load_attributes(g, k):
                sp.wait_ge(s_atc, g + 1)
                for half in range(U // 2):
                    at = g * (U // 2) + half
                    packed = sp.value_load(cpk[0:1, at:at + 1] if isinstance(at, int) else cpk[0:1, bass.ds(at, 1)])
                    for e in range(2):
                        c = nc.s_assert_within(sp.snap((packed >> (11 * e)) & (CHUNK_BITS - 1)), 0, CHUNKS - 1,
                                               skip_runtime_bounds_check_because="a count of chunks less one")
                        sp.dma_start(att[:, k, 2 * half + e, :], attr_s[bass.ds(c * P, P), :]).then_inc(s_att[k], 16)

            with sp.Fori(0, ROUNDS) as i:
                for k in range(R):
                    load_attributes(i * R + k, k)
            load_attributes(ROUNDS * R, 0)
            sp.wait_ge(s_stage, 2)
            sp.dma_start(rows[2].rearrange("(t p) f -> p t f", p=P), stage[:, 0, :].rearrange("p (t f) -> p t f", f=D)).then_inc(s_table, 16)
            sp.wait_ge(s_fin, 1)
            sp.dma_start(out[0:FULL * P, :].rearrange("(t p) f -> p t f", p=P), xs[:, 0:FULL, :]).then_inc(s_out, 16)
            sp.dma_start(out[FULL * P:NODES, :], xs[0:REST, FULL, :]).then_inc(s_out, 16)
            sp.wait_ge(s_out, 32)

        @block.gpsimd
        def _(pool):
            nc.gpsimd.memset(ident[:, :], 0.0).then_inc(s_pool, 1)
            pool.wait_ge(s_pool, 1)
            nc.gpsimd.affine_select(out=ident[:, :], in_=ident[:, :], compare_op=ALU.not_equal, fill=1.0, base=0,
                                    pattern=[[-1, P]], channel_multiplier=1).then_inc(s_pool, 1)
            nc.gpsimd.iota(iota_i[:, :], [[1, P]], base=0, channel_multiplier=0).then_inc(s_pool, 1)
            nc.gpsimd.iota(step_i[:, :], [[P, SB]], base=0, channel_multiplier=1).then_inc(s_pool, 1)
            nc.gpsimd.iota(chunk_no, [[1, CW]], base=0, channel_multiplier=0,
                           allow_small_or_imprecise_dtypes=True).then_inc(s_pool, 1)
            pool.wait_ge(s_copy, 32)
            pool.wait_ge(s_pad, 32)
            pool.wait_ge(s_cidx, 1)
            for j in range(SB):
                for to, of, landed in ((dg, dst_s, s_eg), (sg, src_s, s_eg2)):
                    nc.gpsimd.indirect_dma_start(
                        to[:, j * P:(j + 1) * P], None, of.rearrange("(c e) -> c e", e=P),
                        bass.IndirectOffsetOnAxis(ap=cs_i[:, j:j + 1], axis=0)).then_inc(landed, 16)
            proj_pool(pool, 0)
            edge_pool(pool, 0, kv_rows, 2 * D, "used")
            proj_pool(pool, 1)
            proj_pool(pool, 2)
            edge_pool(pool, 1, rows[0], D, "agg")
            proj_pool(pool, 3)
            edge_pool(pool, 2, rows[1], D, "used")
            proj_pool(pool, 4 + 1)
            proj_pool(pool, 4)
            edge_pool(pool, 3, rows[2], D, "agg")

        @block.scalar
        def _(act):
            roots = iter(range(8))

            def root():
                act.wait_ge(s_var, next(roots) + 1)
                nc.scalar.activation(small[:, 3, :], small[:, 2, :], ACT.Sqrt).then_inc(s_sd, 1)

            for t, to in enumerate((dloc, sidx, slo, shi)):
                for j in range(0, SB, 4):
                    m = min(4, SB - j)
                    n = t * (-(-SB // 4)) + j // 4
                    act.wait_ge(s_tabt, n + 1)
                    nc.scalar.copy(to[:, j * P:(j + m) * P], ps[:, n % 2, 0:m * P]).then_inc(s_bcc, 1)
            root()
            proj_act(act, 0)

            s = L[0]
            first_indices(act, 0)
            act.wait_ge(s["t"], 1)
            nc.scalar.copy(oht[:, 0, :, :], ps[:, 0, :]).then_inc(s["oht"], 1)
            with act.Fori(0, ROUNDS) as i:
                for k in range(R):
                    b = k % 2
                    act.wait_ge(s["t"], i * R + k + 2)
                    nc.scalar.copy(oht[:, 1 - b, :, :], ps[:, 1 - b, :]).then_inc(s["oht"], 1)
                    act.wait_ge(s["clip"], i * R + k + 1)
                    act.wait_ge(s["agg"], i * R + k + 3)
                    nc.scalar.activation(msg[:, b, :, D:D + HEADS],
                                         sc[:, b, 1, :].rearrange("p (u h) -> p u h", h=HEADS), ACT.Exp, scale=SCALE).then_inc(s["exp"], 1)
                    next_indices(act, 0, i, k)
            proj_act(act, 1)
            root()
            root()
            root()
            proj_act(act, 2)
            first_indices(act, 1)
            with act.Fori(0, ROUNDS) as i:
                for k in range(R):
                    next_indices(act, 1, i, k)
            root()
            proj_act(act, 3)

            s = L[2]
            first_indices(act, 2)
            act.wait_ge(s["t"], 1)
            nc.scalar.copy(oht[:, 0, :, :], ps[:, 0, :]).then_inc(s["oht"], 1)
            act.wait_ge(s_atc, R + 1)
            nc.scalar.copy(attT[:, 0, :], ps[:, 6, 0:P]).then_inc(s["clip"], 1)
            with act.Fori(0, ROUNDS) as i:
                for k in range(R):
                    b = k % 2
                    act.wait_ge(s["t"], i * R + k + 2)
                    nc.scalar.copy(oht[:, 1 - b, :, :], ps[:, 1 - b, :]).then_inc(s["oht"], 1)
                    act.wait_ge(s_atc, i * R + k + 2 + R)
                    nc.scalar.copy(attT[:, 1 - b, :], ps[:, 7 - b, 0:P]).then_inc(s["clip"], 1)
                    act.wait_ge(s["used"], i * R + k + 5)
                    act.wait_ge(s["agg"], i * R + k + 3)
                    nc.scalar.activation(msg[:, b, :, 0:D], prod[:, b, :].rearrange("p (u d) -> p u d", d=D), ACT.Relu).then_inc(s["exp"], 1)
                    next_indices(act, 2, i, k)
            proj_act(act, 5)
            proj_act(act, 4)
            gates = flat[:, 0:TILES * 4 * D].rearrange("p (t c) -> p t c", c=4 * D)
            act.wait_ge(s_gates, 1)
            nc.scalar.activation(gates[:, :, 0:2 * D], gates[:, :, 0:2 * D], ACT.Sigmoid).then_inc(s_gact, 1)
            act.wait_ge(s_gates, 2)
            nc.scalar.activation(gates[:, :, 2 * D:3 * D], gates[:, :, 2 * D:3 * D], ACT.Tanh).then_inc(s_gact, 1)
            root()
            root()
            root()
            first_indices(act, 3)
            with act.Fori(0, ROUNDS) as i:
                for k in range(R):
                    next_indices(act, 3, i, k)

        @block.tensor
        def _(pe):
            for n in range(2):
                pe.wait_ge(s_rows, n + 1)
                for j in range(4):
                    a, b = j * 512, min(CW, (j + 1) * 512)
                    mm = nc.tensor.matmul(ps[:, 4 * n + j, 0:b - a], ones[:, :], crow[0:1, 2 + n, a:b], start=True, stop=True)
                mm.then_inc(s_bc, 1)
            pe.wait_ge(s_w, 16 * N_WEIGHTS)
            pe.wait_ge(s_cidx, 1)
            nc.tensor.matmul(ps[:, 7, 0:4 * D], ones[:, :], brow[:, :], start=True, stop=True).then_inc(s_bc, 1)
            pe.wait_ge(s_pool, 5)
            nc.tensor.transpose(ps[0:SB, 2, 0:P], cs[:, 2, :], ident[:, :])
            nc.tensor.transpose(ps[0:SB, 2, P:2 * P], cs[:, 3, :], ident[:, :]).then_inc(s_packt, 1)
            for t, of in enumerate((df, sf, lof, hif)):
                pe.wait_ge(s_tabs, t + 1)
                for j in range(0, SB, 4):
                    m = min(4, SB - j)
                    n = t * (-(-SB // 4)) + j // 4
                    if n >= 2:
                        pe.wait_ge(s_bcc, n - 1)
                    for e in range(m):
                        mm = nc.tensor.transpose(ps[:, n % 2, e * P:(e + 1) * P], of[:, (j + e) * P:(j + e + 1) * P], ident[:, :])
                    mm.then_inc(s_tabt, 1)
            proj_pe(pe, 0)
            pe.wait_ge(s_packl, 32)

            s = L[0]
            zero_sums(pe, 0, 2, W0)

            pe.wait_ge(s["oh"], 1)
            turn_onehot(pe, 0, 0, 0, 0)
            with pe.Fori(0, ROUNDS) as i:
                for k in range(R):
                    b = k % 2
                    dst_rows(pe, 0, i, k, None)
                    pe.wait_ge(s["oh"], i * R + k + 2)
                    turn_onehot(pe, 0, None, (k + 1) % R, 1 - b)
                    sum_messages(pe, 0, i * R + k, (k - 1) % R, W0)
            sum_messages(pe, 0, ROUNDS * R, R - 1, W0)
            proj_pe(pe, 1)
            proj_pe(pe, 2)

            s = L[1]
            zero_sums(pe, 1, 1, D)
            nc.tensor.matmul(ps[:, 6, 0:TILES], zerob[:, :], zerob[:, 0:TILES], start=True, stop=False, skip_group_check=True)
            with pe.Fori(0, ROUNDS) as i:
                for k in range(R):
                    pe.wait_ge(s["oh"], i * R + k + 1)
                    pe.wait_ge(s["land"][k], (i + 1) * 16 * U)
                    mm = sum_edges(pe, 1, i * R + k, k, D, lambda u: gat[:, k, u, 0:D])
                    for u in range(U):
                        mm = nc.tensor.matmul(ps[:, 6, 0:TILES], olo[:, k, u, :], ohi[:, k, u, :], start=False, stop=False,
                                              skip_group_check=True)
                    mm.then_inc(s["agg"], 1)
            nc.tensor.matmul(ps[:, 6, 0:TILES], zerob[:, :], zerob[:, 0:TILES], start=False, stop=True,
                             skip_group_check=True).then_inc(s_hist, 1)
            proj_pe(pe, 3)

            s = L[2]
            zero_sums(pe, 2, 2, D)
            pe.wait_ge(s["oh"], 1)
            turn_onehot(pe, 2, 0, 0, 0)
            pe.wait_ge(s_att[0], 16 * U)
            nc.tensor.transpose(ps[:, 6, 0:P], att[:, 0, :, :], ident[:, :]).then_inc(s_atc, 1)
            with pe.Fori(0, ROUNDS) as i:
                for k in range(R):
                    b, k1 = k % 2, (k + 1) % R
                    pe.wait_ge(s["clip"], i * R + k + 1)
                    dst_rows(pe, 2, i, k, lambda: nc.tensor.matmul(
                        ps[:, 2 + b, 0:U * D], attT[:, b, :], w_e[:, :], start=True, stop=False, skip_group_check=True))
                    pe.wait_ge(s["oh"], i * R + k + 2)
                    turn_onehot(pe, 2, None, k1, 1 - b)
                    if k < R - 1:
                        pe.wait_ge(s_att[k1], (i + 1) * 16 * U)
                    else:
                        pe.wait_ge(s_att[k1], (i + 2) * 16 * U)
                    nc.tensor.transpose(ps[:, 7 - b, 0:P], att[:, k1, :, :], ident[:, :]).then_inc(s_atc, 1)
                    sum_messages(pe, 2, i * R + k, (k - 1) % R, D)
            sum_messages(pe, 2, ROUNDS * R, R - 1, D)
            proj_pe(pe, 5)
            proj_pe(pe, 4)

            s = L[3]
            zero_sums(pe, 3, 1, D)
            with pe.Fori(0, ROUNDS) as i:
                for k in range(R):
                    pe.wait_ge(s["oh"], i * R + k + 1)
                    pe.wait_ge(s["land"][k], (i + 1) * 16 * U)
                    sum_edges(pe, 3, i * R + k, k, D, lambda u: gat[:, k, u, 0:D]).then_inc(s["agg"], 1)

        @block.vector
        def _(dve):
            v = nc.vector
            links = [0]

            def link(ins):
                links[0] += 1
                ins.then_inc(s_d, 1)
                dve.wait_ge(s_d, links[0])

            v.memset(zeros[:, :], 0.0)
            v.memset(zerob[:, :], 0.0)
            v.memset(ones[:, :], 1.0)
            v.memset(padi[0:1, 0, :], BIG)
            v.memset(padi[0:1, 1, :], 0)
            v.memset(hT[D:D + 1, :, :], 1.0)
            for w in (w_g, w_m, w_pq):
                v.memset(w[D:D + 1, :], 0.0)
            for w in (w_i, w_h, w_e):
                v.memset(w[:, :], 0.0)
            v.memset(tpk[0:1, 0:2], 0)
            v.memset(msg[:, :, :, W0 - 1:W0], 1.0)
            v.memset(crow[0:1, 3, :], 0.0)
            v.memset(xs[:, FULL:TILES, :], 0.0).then_inc(s_const, 1)
            v.memset(small[:, :, :], 0.0).then_inc(s_atc, R)

            dve.wait_ge(s_ends, 48)
            link(v.tensor_scalar(crow_i[:, :, :], crow_i[:, :, :], 7, None, ALU.arith_shift_right))
            link(v.tensor_copy(crow[0:1, 0:2, :], crow_i[:, :, :]))
            link(v.tensor_tensor(crow[0:1, 1, :], crow[0:1, 1, :], crow[0:1, 0, :], ALU.subtract))
            link(v.tensor_tensor_scan(crow[0:1, 2, :], crow[0:1, 1, :], crow[0:1, 3, :], 0.0, ALU.add, ALU.add))
            link(v.tensor_tensor(crow[0:1, 2, :], crow[0:1, 2, :], crow[0:1, 1, :], ALU.subtract))
            dve.wait_ge(s_pool, 5)
            ins = v.tensor_tensor(crow[0:1, 2, :], crow[0:1, 2, :], chunk_no, ALU.add)
            ins.then_inc(s_rows, 1)
            dve.wait_ge(s_rows, 1)
            link(v.tensor_tensor(crow[0:1, 0, :], crow[0:1, 0, :], crow[0:1, 2, :], ALU.subtract))
            link(v.tensor_copy(crow[0:1, 3, 0:1], crow[0:1, 0, 0:1]))
            v.tensor_tensor(crow[0:1, 3, 1:CW], crow[0:1, 0, 1:CW], crow[0:1, 0, 0:CW - 1], ALU.subtract).then_inc(s_rows, 1)
            v.tensor_copy(iota[:, :], iota_i[:, :])
            link(v.tensor_copy(step[:, :], step_i[:, :]))
            dve.wait_ge(s_bc, 2)
            link(v.tensor_copy(off_b, ps[:, 0:4, :].rearrange("p b n -> p (b n)")[:, 0:CW]))
            link(v.tensor_copy(dw_b, ps[:, 4:8, :].rearrange("p b n -> p (b n)")[:, 0:CW]))
            for j in range(SB):
                link(v.tensor_scalar(mask_b, off_b, step[:, j:j + 1], None, ALU.is_le, ALU.add, accum_out=cs[:, 0, j:j + 1]))
                link(v.tensor_tensor_reduce(mask_b, mask_b, dw_b, 1.0, 0.0, ALU.mult, ALU.add, cs[:, 1, j:j + 1]))
            link(v.tensor_scalar(cs[:, 3, :], cs[:, 0, :], -1.0, None, ALU.add))
            link(v.tensor_tensor(cs[:, 4, :], cs[:, 1, :], step[:, :], ALU.add))
            link(v.tensor_scalar(cs[:, 2, :], cs[:, 4, :], float(TILES - 1), None, ALU.min))
            link(v.tensor_scalar(cs[:, 5, :], cs[:, 4, :], float(P), None, ALU.mult))
            v.tensor_copy(cs_i[:, :], cs[:, 3, :]).then_inc(s_cidx, 1)
            dve.wait_ge(s_bc, 3)
            link(v.tensor_copy(bc[:, :], ps[:, 7, 0:4 * D]))
            dve.wait_ge(s_packt, 1)
            link(v.tensor_copy(packf[:, 0:2, :], ps[0:SB, 2, 0:2 * P].rearrange("p (a b) -> p a b", b=P)))
            t4 = packf[:, 0, :].rearrange("p (g u) -> p g u", u=4)
            c2 = packf[:, 1, :].rearrange("p (g u) -> p g u", u=2)
            G4 = P // U
            for m in range(2):
                link(v.scalar_tensor_tensor(packf[:, 2, m * G4:(m + 1) * G4], t4[:, :, 2 * m + 1], float(TILE_BITS), t4[:, :, 2 * m],
                                            ALU.mult, ALU.add))
            v.scalar_tensor_tensor(pack_i[:, 0:G4], packf[:, 2, G4:2 * G4], float(TILE_BITS ** 2), packf[:, 2, 0:G4],
                                   ALU.mult, ALU.add).then_inc(s_packed, 1)
            v.scalar_tensor_tensor(pack_i[:, G4:G4 + P // 2], c2[:, :, 1], float(CHUNK_BITS), c2[:, :, 0],
                                   ALU.mult, ALU.add).then_inc(s_packed, 1)
            dve.wait_ge(s_eg, 16 * SB)
            link(v.tensor_copy(df, dg))
            by_step = lambda a: a.rearrange("p (j e) -> p j e", e=P)
            last = v.tensor_tensor(by_step(df), by_step(df), cs[:, 5, :].unsqueeze(2).to_broadcast([P, SB, P]), ALU.subtract)
            last.then_inc(s_tabs, 1)
            dve.wait_ge(s_tabs, 1)
            dve.wait_ge(s_eg2, 16 * SB)
            v.tensor_copy(sf, sg).then_inc(s_tabs, 1)
            link(v.tensor_scalar(lo_i, sg, P - 1, None, ALU.bitwise_and))
            v.tensor_copy(lof, lo_i).then_inc(s_tabs, 1)
            link(v.tensor_scalar(vf, df, 0.0, None, ALU.is_ge))
            link(v.scalar_tensor_tensor(vf, df, float(P), vf, ALU.is_lt, ALU.mult))
            link(v.tensor_scalar(vf, vf, -OUTSIDE, OUTSIDE, ALU.mult, ALU.add))
            link(v.tensor_scalar(hi_i, sg, 7, None, ALU.arith_shift_right))
            link(v.tensor_copy(hif, hi_i))
            v.tensor_tensor(hif, hif, vf, ALU.add).then_inc(s_tabs, 1)
            dve.wait_ge(s_bcc, NTAB)

            tmp0, tmp1 = (stage[:, n, :].rearrange("p (t d) -> p t d", d=D) for n in range(2))
            per_node = lambda a: a.unsqueeze(2).to_broadcast([P, TILES, D])
            per_feature = lambda n: bc[:, n * D:(n + 1) * D].unsqueeze(1).to_broadcast([P, TILES, D])
            nroot = [0]

            def inverse_root(to):
                nroot[0] += 1
                dve.wait_ge(s_sd, nroot[0])
                link(v.reciprocal(to, small[:, 3, :]))

            def center(a):
                link(v.tensor_reduce(small[:, 0, :], a[:, :, :], AX.X, ALU.add))
                link(v.tensor_scalar(small[:, 0, :], small[:, 0, :], 1.0 / D, None, ALU.mult))
                link(v.tensor_tensor(tmp0, a[:, :, :], per_node(small[:, 0, :]), ALU.subtract))
                link(v.tensor_tensor(tmp1, tmp0, tmp0, ALU.mult))
                link(v.tensor_reduce(small[:, 2, :], tmp1, AX.X, ALU.add))
                v.tensor_scalar(small[:, 2, :], small[:, 2, :], 1.0 / D, EPS, ALU.mult, ALU.add).then_inc(s_var, 1)
                inverse_root(small[:, 1, :])

            def root_of(a, op, c, to):
                v.tensor_scalar(small[:, 2, :], a, c, None, op).then_inc(s_var, 1)
                inverse_root(to)

            def norm_relu():
                return v.scalar_tensor_tensor(h[:, :, :], tmp0, 0.0, per_node(small[:, 1, :]), ALU.max, ALU.mult)

            def edge_sums(n, lag, width):
                for g in range(ROUNDS * R, ROUNDS * R + lag):
                    accumulate(dve, n, g, g % R, lag, load_tiles(dve, g - lag), width)
                dve.wait_ge(L[n]["acc"], ROUNDS * R + lag + 1)
                a = [acc[:, u, 0:TILES * width] for u in range(U)]
                link(v.tensor_tensor(a[0], a[0], a[1], ALU.add))
                link(v.tensor_tensor(a[2], a[2], a[3], ALU.add))
                link(v.tensor_tensor(a[0], a[0], a[2], ALU.add))
                return a[0].rearrange("p (t c) -> p t c", c=width)

            dve.wait_ge(s_x, 32)
            center(xs)
            norm_relu().then_inc(PJ[0]["ready"], 1)
            proj_dve(dve, 0)
            dve.wait_ge(s_packl, 32)

            s = L[0]
            zero_acc(dve, 0, W0)
            zero_group(dve, 0)
            one_hot(dve, 0, 0, 0)

            def weigh_values(g, k1):
                c = k1 % 2
                dve.wait_ge(s["exp"], g + 1)
                v.tensor_tensor(
                    msg[:, c, :, 0:D].rearrange("p u (h d) -> p u h d", d=DH),
                    gat[:, k1, :, D:2 * D].rearrange("p u (h d) -> p u h d", d=DH),
                    msg[:, c, :, D:D + HEADS].unsqueeze(3).to_broadcast([P, U, HEADS, DH]), ALU.mult).then_inc(s["used"], 1)

            with dve.Fori(0, ROUNDS) as i:
                for k in range(R):
                    g, b = i * R + k, k % 2
                    dve.wait_ge(s["agg"], g + 2)
                    one_hot(dve, 0, i, k + 1)
                    places = load_tiles(dve, g - 2)
                    dve.wait_ge(s["land"][k], (i + 1) * 16 * U)
                    dve.wait_ge(s["qe"], g + 1)
                    v.tensor_tensor(prod[:, b, :].rearrange("p (u d) -> p u d", d=D),
                                    ps[:, 2 + b, 0:U * D].rearrange("p (u d) -> p u d", d=D), gat[:, k, :, 0:D],
                                    ALU.mult).then_inc(s["prod"], 1)
                    dve.wait_ge(s["prod"], g + 1)
                    v.tensor_reduce(sc[:, b, 0, :], prod[:, b, :].rearrange("p (a d) -> p a d", d=DH), AX.X, ALU.add).then_inc(s["red"], 1)
                    dve.wait_ge(s["red"], g + 1)
                    v.tensor_scalar(sc[:, b, 1, :], sc[:, b, 0, :], -CLIP, CLIP, ALU.max, ALU.min).then_inc(s["clip"], 1)
                    weigh_values(g, (k - 1) % R)
                    accumulate(dve, 0, g, k, 2, places, W0)
            weigh_values(ROUNDS * R, R - 1)
            a0 = edge_sums(0, 2, W0)
            v.tensor_copy(cnt[:, :], a0[:, :, W0 - 1])
            link(v.tensor_scalar(z1[:, :, :], a0[:, :, D:D + HEADS], 1.0, None, ALU.add))
            link(v.reciprocal(z1[:, :, :], z1[:, :, :]))
            v.tensor_tensor(h[:, :, :].rearrange("p t (a d) -> p t a d", d=DH), a0[:, :, 0:D].rearrange("p t (a d) -> p t a d", d=DH),
                            z1[:, :, :].unsqueeze(3).to_broadcast([P, TILES, HEADS, DH]), ALU.mult).then_inc(PJ[1]["ready"], 1)
            proj_dve(dve, 1)
            dve.wait_ge(PJ[1]["ev"], NR)
            link(v.tensor_tensor(y[:, :, :], y[:, :, :], tmp0, ALU.add))
            center(y)
            link(v.tensor_tensor(tmp0, tmp0, per_node(small[:, 1, :]), ALU.mult))
            link(v.tensor_tensor(tmp0, tmp0, per_feature(0), ALU.mult))
            link(v.tensor_tensor(tmp0, tmp0, per_feature(1), ALU.add))
            link(v.tensor_tensor(tmp0, tmp0, y[:, :, :], ALU.add))
            link(v.tensor_tensor(xs[:, :, :], xs[:, :, :], tmp0, ALU.add))

            center(xs)
            link(norm_relu())
            root_of(cnt[:, :], ALU.add, 1.0, rd[:, 0, :])
            v.memset(small[:, 0, 0:1], 0.0).then_inc(PJ[2]["ready"], 1)
            proj_dve(dve, 2)
            dve.wait_ge(PJ[2]["ev"], NR)
            v.tensor_tensor(y[:, :, :], y[:, :, :], per_node(rd[:, 0, :]), ALU.mult).then_inc(s_stage, 1)
            s = L[1]
            zero_acc(dve, 1, D)
            one_hot(dve, 1, 0, 0, True)
            with dve.Fori(0, ROUNDS) as i:
                for k in range(R):
                    dve.wait_ge(s["agg"], i * R + k + 2)
                    one_hot(dve, 1, i, k + 1, True)
                    places = load_tiles(dve, i * R + k - 1)
                    accumulate(dve, 1, i * R + k, k, 1, places, D)
            a0 = edge_sums(1, 1, D)
            dve.wait_ge(s_hist, 1)
            link(v.tensor_copy(outdeg[:, :], ps[:, 6, 0:TILES]))
            link(v.tensor_tensor(tmp0, a0, y[:, :, :], ALU.add))
            link(v.tensor_tensor(tmp0, tmp0, per_node(rd[:, 0, :]), ALU.mult))
            link(v.tensor_tensor(tmp0, tmp0, per_feature(2), ALU.add))
            link(v.scalar_tensor_tensor(xs[:, :, :], tmp0, 0.0, xs[:, :, :], ALU.max, ALU.add))

            center(xs)
            norm_relu().then_inc(PJ[3]["ready"], 1)
            proj_dve(dve, 3)
            s = L[2]
            zero_acc(dve, 2, D)
            zero_group(dve, 2)
            one_hot(dve, 2, 0, 0)
            with dve.Fori(0, ROUNDS) as i:
                for k in range(R):
                    g, b = i * R + k, k % 2
                    dve.wait_ge(s["agg"], g + 2)
                    one_hot(dve, 2, i, k + 1)
                    places = load_tiles(dve, g - 2)
                    dve.wait_ge(s["agg"], g + 3)
                    dve.wait_ge(s["land"][k], (i + 1) * 16 * U)
                    dve.wait_ge(s["qe"], g + 1)
                    v.tensor_tensor(prod[:, b, :].rearrange("p (u d) -> p u d", d=D), ps[:, 2 + b, 0:U * D].rearrange("p (u d) -> p u d", d=D),
                                    gat[:, k, :, 0:D], ALU.add).then_inc(s["used"], 1)
                    accumulate(dve, 2, g, k, 2, places, D)
            a0 = edge_sums(2, 2, D)
            v.tensor_copy(y[:, :, :], a0).then_inc(PJ[5]["ready"], 1)
            proj_dve(dve, 5)
            dve.wait_ge(PJ[5]["ev"], NR)
            link(v.tensor_tensor(tmp1, per_node(cnt[:, :]), per_feature(3), ALU.mult))
            v.tensor_tensor(y[:, :, :], tmp0, tmp1, ALU.add).then_inc(PJ[4]["ready"], 1)
            proj_dve(dve, 4)
            dve.wait_ge(PJ[4]["ev"], NR)
            gates = flat[:, 0:TILES * 4 * D].rearrange("p (t c) -> p t c", c=4 * D)
            r, z, n_in, n_h = (gates[:, :, n * D:(n + 1) * D] for n in range(4))
            v.memset(small[:, 0, 0:1], 0.0).then_inc(s_gates, 1)
            dve.wait_ge(s_gact, 1)
            link(v.tensor_tensor(n_h, n_h, r, ALU.mult))
            v.tensor_tensor(n_in, n_in, n_h, ALU.add).then_inc(s_gates, 1)
            dve.wait_ge(s_gact, 2)
            link(v.tensor_tensor(tmp0, h[:, :, :], n_in, ALU.subtract))
            link(v.tensor_tensor(tmp0, tmp0, z, ALU.mult))
            link(v.tensor_tensor(tmp0, tmp0, n_in, ALU.add))
            link(v.tensor_tensor(xs[:, :, :], xs[:, :, :], tmp0, ALU.add))

            center(xs)
            link(norm_relu())
            root_of(outdeg[:, :], ALU.max, 1.0, rd[:, 1, :])
            root_of(cnt[:, :], ALU.max, 1.0, rd[:, 2, :])
            v.tensor_tensor(tmp0, h[:, :, :], per_node(rd[:, 1, :]), ALU.mult).then_inc(s_stage, 1)
            s = L[3]
            zero_acc(dve, 3, D)
            one_hot(dve, 3, 0, 0)
            with dve.Fori(0, ROUNDS) as i:
                for k in range(R):
                    dve.wait_ge(s["agg"], i * R + k + 2)
                    one_hot(dve, 3, i, k + 1)
                    places = load_tiles(dve, i * R + k - 1)
                    accumulate(dve, 3, i * R + k, k, 1, places, D)
            a0 = edge_sums(3, 1, D)
            link(v.tensor_tensor(tmp0, a0, per_node(rd[:, 2, :]), ALU.mult))
            v.tensor_tensor(xs[:, :, :], xs[:, :, :], tmp0, ALU.add).then_inc(s_fin, 1)


_L0 = ["Wq", "bq", "Wk", "bk", "Wv", "bv", "Wo", "bo", "Wf", "bf", "gamma", "beta"]


def kernel(**inputs):
    import numpy as _np
    import concourse.bacc as _bacc
    from concourse import mybir as _mybir
    from concourse.bass_utils import run_bass_kernel_spmd as _run

    arrays = {n: inputs[n] for n in ("x", "src", "dst", "edge_attr_32")}
    arrays |= {n: inputs["L0_gnn_" + n] for n in _L0}
    arrays |= {"W_gcn": inputs["L1_gnn_W"], "b_gcn": inputs["L1_gnn_b"]}
    for n in ("W1", "b1", "W2", "b2", "w_ih", "w_hh", "b_ih", "b_hh"):
        a = _np.asarray(inputs["L2_gnn_" + n])
        arrays["e_" + n] = a.T if a.ndim == 2 else a
    order = ["x", "src", "dst", "edge_attr_32", *_L0, "W_gcn", "b_gcn", "e_W1", "e_b1", "e_W2", "e_b2", "e_w_ih", "e_w_hh", "e_b_ih", "e_b_hh"]
    nc = _bacc.Bacc("TRN2", target_bir_lowering=False, num_devices=1)
    given, args = {}, []
    for n in order:
        a = _np.ascontiguousarray(arrays[n])
        given[f"in_{n}"] = a
        args.append(nc.dram_tensor(f"in_{n}", a.shape, _mybir.dt.from_np(a.dtype), kind="ExternalInput").ap())
    args.append(nc.dram_tensor("out_0", (NODES, D), F32, kind="ExternalOutput").ap())
    build_gnn(nc, *args)
    r = _run(nc, [given], core_ids=[0])
    return r.results[0]["out_0"]
```

```python
from contextlib import ExitStack

import concourse.bass as bass
from concourse import mybir

ALU = mybir.AluOpType
ACT = mybir.ActivationFunctionType
AX = mybir.AxisListType
F32 = mybir.dt.float32
BF16 = mybir.dt.bfloat16
I32 = mybir.dt.int32

P = 128
NODES, EDGES, D, DE = 6250, 200000, 64, 32
HEADS, DH = 4, 16
TILES = -(-NODES // P)
NPAD = TILES * P
FULL = NODES // P
REST = NODES - FULL * P
CHUNKS = -(-EDGES // P)
EPAD = CHUNKS * P
U = 4
R = 4
STEPS = -(-(CHUNKS + TILES - 1) // (U * R)) * U * R
ROUNDS = STEPS // (U * R)
SB = -(-(STEPS + U * R) // P)
SPAD = SB * P
NTAB = 4 * -(-SB // 4)
N_WEIGHTS = 29
GT = 7
NR = TILES // GT
W0 = D + HEADS + 1
SCALE = float(D) ** -0.5
CLIP = 5.0 / SCALE
EPS = 1e-5
BIG = 1 << 16
OUTSIDE = 1000.0
TILE_BITS, CHUNK_BITS = 64, 2048
OROWS = 125
OLEN = EDGES // OROWS
assert OROWS * OLEN == EDGES and OLEN <= TILES * W0
assert TILES % GT == 0 and TILES <= TILE_BITS and CHUNKS <= CHUNK_BITS and REST > 0


def build_gnn(nc, x, src, dst, attr, wq, bq, wk, bk, wv, bv, wo, bo, wf, bf, gamma, beta,
              w_gcn, b_gcn, w1t, b1, w2t, b2, wiht, whht, bih, bhh, out):
    with ExitStack() as ctx:
        def sb(name, shape, dt=F32):
            return ctx.enter_context(nc.sbuf_tensor(name, shape, dt))

        def sem(name):
            return ctx.enter_context(nc.semaphore(name))

        def dram(name, shape, dt=F32):
            return nc.dram_tensor(name, shape, dt).ap()

        dst_s, src_s, attr_s = dram("dst_s", [EPAD], I32), dram("src_s", [EPAD], I32), dram("attr_s", [EPAD, DE])
        kv_rows = dram("kv_rows", [NPAD, 2 * D])
        rows = [dram(f"rows{n}", [NPAD, D]) for n in range(3)]
        counts = dram("counts", [NPAD + P])
        tiles_d, chunks_d = dram("tiles_d", [SPAD // U], I32), dram("chunks_d", [SPAD // 2], I32)

        xs = sb("xs", [P, TILES, D])
        h = sb("h", [P, TILES, D])
        q = sb("q", [P, TILES, D])
        y = sb("y", [P, TILES, D])
        stage = sb("stage", [P, 2, TILES * D])
        acc = sb("acc", [P, U, TILES * W0])
        cnt = sb("cnt", [P, TILES])
        outdeg = sb("outdeg", [P, TILES])
        small = sb("small", [P, 4, TILES])
        rd = sb("rd", [P, 3, TILES])
        z1 = sb("z1", [P, TILES, HEADS])
        dloc = sb("dloc", [P, SPAD])
        sidx = sb("sidx", [P, SPAD], I32)
        slo, shi = sb("slo", [P, SPAD]), sb("shi", [P, SPAD])
        tpk = sb("tpk", [1, 2 + SPAD // U], I32)
        cpk = sb("cpk", [1, SPAD // 2], I32)
        idx = sb("idx", [P, R, U], I32)
        gat = sb("gat", [P, R, U, 2 * D])
        oh = sb("oh", [P, R, U, P])
        oht = sb("oht", [P, 2, U, P])
        msg = sb("msg", [P, 2, U, W0])
        prod = sb("prod", [P, 2, U * D])
        sc = sb("sc", [P, 2, 2, U * HEADS])
        att = sb("att", [P, R, U, DE])
        attT = sb("attT", [P, 2, P])
        olo = oht[:, :, :, :].rearrange("p a u n -> p (a u n)").bitcast(BF16).rearrange("p (k u n) -> p k u n", k=R, u=U)
        ohi = prod[:, :, :].rearrange("p a n -> p (a n)").bitcast(BF16)[:, 0:R * U * TILES].rearrange("p (k u n) -> p k u n", k=R, u=U)
        hb = gat[:, :, :, :].rearrange("p k u d -> p (k u d)")[:, 0:2 * GT * D].rearrange("p (m t d) -> p m t d", m=2, t=GT)
        hT = sb("hT", [D + 1, 2, GT * P])
        ident = sb("ident", [P, P])
        iota_i, iota = sb("iota_i", [P, P], I32), sb("iota", [P, P])
        step_i, step = sb("step_i", [P, SB], I32), sb("step", [P, SB])
        zeros = sb("zeros", [P, U * W0])
        zerob = sb("zerob", [P, P], BF16)
        ones = sb("ones", [1, P])
        padi = sb("padi", [1, 2, P], I32)
        w_kvqf = sb("w_kvqf", [D + 1, 4 * D])
        w_o, w_g = sb("w_o", [D + 1, D]), sb("w_g", [D + 1, D])
        w_pq, w_m = sb("w_pq", [D + 1, 2 * D]), sb("w_m", [D + 1, D])
        w_i, w_h = sb("w_i", [D + 1, 4 * D]), sb("w_h", [D + 1, 4 * D])
        w_e = sb("w_e", [P, U * D])
        brow, bc = sb("brow", [1, 4 * D]), sb("bc", [P, 4 * D])
        CW = CHUNKS
        crow = stage[0:1, :, :].rearrange("p a n -> p (a n)")[:, 0:4 * CW].rearrange("p (a n) -> p a n", a=4)
        crow_i = h[0:1, :, :].rearrange("p t d -> p (t d)")[:, 0:2 * CW].bitcast(I32).rearrange("p (a n) -> p a n", a=2)
        chunk_no = q[0:1, :, :].rearrange("p t d -> p (t d)")[:, 0:CW]
        cs = sb("cs", [P, 6, SB])
        cs_i = sb("cs_i", [P, SB], I32)
        packf = prod[0:SB, :, :].rearrange("p a n -> p (a n)")[:, 0:3 * P].rearrange("p (a n) -> p a n", a=3)
        pack_i = attT[0:SB, 0, :].bitcast(I32)
        flat = acc[:, :, :].rearrange("p u n -> p (u n)")
        off_b, dw_b, mask_b = (flat[:, n * CW:(n + 1) * CW] for n in range(3))
        dg = flat[:, 3 * CW:3 * CW + SPAD].bitcast(I32)
        sg = flat[:, 3 * CW + SPAD:3 * CW + 2 * SPAD].bitcast(I32)
        df, vf = flat[:, 0:SPAD], flat[:, SPAD:2 * SPAD]
        sf = stage[:, 0, 0:SPAD]
        hi_i, lo_i = stage[:, 1, 0:SPAD].bitcast(I32), h[:, :, :].rearrange("p t d -> p (t d)")[:, 0:SPAD].bitcast(I32)
        hif = q[:, :, :].rearrange("p t d -> p (t d)")[:, 0:SPAD]
        lof = y[:, :, :].rearrange("p t d -> p (t d)")[:, 0:SPAD]

        order_i = acc[0:OROWS, 0:1, 0:OLEN].rearrange("p u n -> p (u n)").bitcast(I32)
        next_i = acc[0:OROWS, 1:2, 0:1].rearrange("p u n -> p (u n)").bitcast(I32)
        falls = acc[0:OROWS, 2:3, 0:OLEN].rearrange("p u n -> p (u n)")
        fell = sb("fell", [P, 1])
        unsorted = sb("unsorted", [1, 1], I32)
        cell = lambda n: acc[:, 3, n:n + 1]
        key_i, src_i, idx_i, pos_i = (cell(n).bitcast(I32) for n in range(4))
        key, seen, total, rank, fresh, last, spare = (cell(n) for n in range(4, 11))
        keys_i = acc[:, 3, P:2 * P].bitcast(I32)
        keys, same, before, below = (acc[:, 3, n * P:(n + 1) * P] for n in range(2, 6))
        attr_c = acc[:, 3, 6 * P:6 * P + DE]
        ranks = y[:, :, :].rearrange("p t d -> p (t d)")[:, 0:CHUNKS]
        count_row = stage[0:1, :, :].rearrange("p a n -> p (a n)")
        start_row = acc[0:1, 0:2, :].rearrange("p u n -> p (u n)")[:, 0:NPAD]

        ps = ctx.enter_context(nc.psum_tensor("ps", [P, 8, 512], F32))

        s_order, s_fell, s_fellt, s_flag = sem("order_loaded"), sem("falls_found"), sem("falls_turned"), sem("order_known")
        s_tri, s_low = sem("ones_for_below"), sem("below_ready")
        S1 = dict(load=sem("count_loaded"), seen=sem("count_seen"), idx=sem("count_index"), new=sem("count_new"),
                  put=sem("count_stored"), row=sem("counts_in_a_row"), scan=sem("starts_ready"),
                  chain=sem("count_chain"), scanned=sem("start_chain"))
        S2 = dict(load=sem("place_loaded"), seen=sem("place_start"), pos=sem("place_ready"), put=[sem(f"edge_placed{n}") for n in range(3)], more=sem("place_rest_loaded"))
        s_x, s_w, s_copy, s_pad = sem("x_loaded"), sem("weights_loaded"), sem("edges_copied"), sem("edges_padded")
        s_acopy = sem("attributes_copied_and_padded")
        s_ends, s_ends2 = sem("chunk_ends_loaded"), sem("sorted_chunk_ends_loaded")
        s_pool = sem("pool_constants")
        s_const = sem("constants_ready")
        s_rows = sem("rows_ready")
        s_bc = sem("broadcast_done")
        s_bcc = sem("table_block_copied")
        s_cidx = sem("chunk_numbers_ready")
        s_eg = sem("edge_rows_landed")
        s_eg2 = sem("source_rows_landed")
        s_tabs = sem("tables_ready_by_step")
        s_tabt = sem("table_block_turned")
        s_packt, s_packed, s_packd, s_packl = sem("steps_turned"), sem("steps_packed"), sem("packed_stored"), sem("packed_loaded")
        s_d = sem("vector_chain")
        s_var, s_sd = sem("variances_ready"), sem("deviations_ready")
        s_stage, s_table = sem("table_staged"), sem("table_stored")
        s_gates, s_gact = sem("gates_ready"), sem("gates_done")
        s_hist = sem("sources_counted")
        s_fin, s_out = sem("result_ready"), sem("result_stored")

        NPROD = 6
        PJ = [dict(ready=sem(f"proj{n}_input"), hb=sem(f"proj{n}_staged"), tr=sem(f"proj{n}_turned"),
                   ht=sem(f"proj{n}_turned_copied"), mm=sem(f"proj{n}_product"), ev=sem(f"proj{n}_taken"))
              for n in range(NPROD)]
        sums = dict(idx="indices", oh="onehot", agg="summed", acc="accumulated")
        turned = dict(t="onehot_turned", oht="turned_copied", qe="dst_rows", exp="act", used="rows_used", clip="before_act")
        attention = dict(prod="combined", red="reduced")
        L = [dict({key: sem(f"l{n}_{name}") for key, name in names.items()}, land=[sem(f"l{n}_landed{k}") for k in range(R)])
             for n, names in enumerate((sums | turned | attention, sums, sums | turned, sums))]
        s_att = [sem(f"attr_landed{k}") for k in range(R)]
        s_atc = sem("attr_turned")

        block = ctx.enter_context(nc.Block())

        def proj_specs():
            flats = stage[:, :, :].rearrange("p a n -> p (a n)")
            kv = flats.rearrange("p (t c) -> p t c", c=2 * D)
            gates = flat[:, 0:TILES * 4 * D].rearrange("p (t c) -> p t c", c=4 * D)
            pst = stage[:, 0, :].rearrange("p (t c) -> p t c", c=D)
            return [
                ([(h, w_kvqf)], 4 * D, [(0, 2 * D, kv), (2 * D, 3 * D, q), (3 * D, 4 * D, y)]),
                ([(h, w_o)], D, [(0, D, pst)]),
                ([(h, w_g)], D, [(0, D, y)]),
                ([(h, w_pq)], 2 * D, [(0, D, pst), (D, 2 * D, q)]),
                ([(y, w_i), (h, w_h)], 4 * D, [(0, 4 * D, gates)]),
                ([(y, w_m)], D, [(0, D, pst)]),
            ]

        SPEC = proj_specs()
        outp = ps[:, 2:6, :].rearrange("p b (j c) -> p (b j) c", c=4 * D)

        def rounds(eng, body):
            body(0)
            with eng.Fori(1, NR) as i:
                body(i)

        def wait_last(eng, semaphore, count):
            if not isinstance(count, int) or count > 0:
                eng.wait_ge(semaphore, count)

        def round_tiles(a, i):
            return a[:, bass.ds(i * GT, GT), :]

        def proj_pool(pool, n):
            s, srcs = PJ[n], SPEC[n][0]
            M = len(srcs)

            def body(i):
                wait_last(pool, s["tr"], i * M)
                pool.wait_ge(s["ready"], 1)
                for m, (a, _) in enumerate(srcs):
                    nc.gpsimd.tensor_copy(hb[:, m, :, :], round_tiles(a, i)).then_inc(s["hb"], 1)

            rounds(pool, body)

        def proj_pe(pe, n):
            s, srcs, width = PJ[n], SPEC[n][0], SPEC[n][1]
            M = len(srcs)

            def body(i):
                for m in range(M):
                    staged, copied = i * M + m + 1, i * M + m
                    if not isinstance(i, int):
                        staged, copied = pe.to_reg(staged), pe.to_reg(copied)
                    pe.wait_ge(s_pool, 2)
                    pe.wait_ge(s["hb"], staged)
                    wait_last(pe, s["ht"], copied)
                    for t in range(GT):
                        mm = nc.tensor.transpose(ps[0:D, t // 4, (t % 4) * P:(t % 4 + 1) * P], hb[:, m, t, :], ident[:, :])
                    mm.then_inc(s["tr"], 1)
                pe.wait_ge(s["ht"], (i + 1) * M)
                wait_last(pe, s["ev"], i)
                for t in range(GT):
                    for m, (_, w) in enumerate(srcs):
                        mm = nc.tensor.matmul(outp[:, t, 0:width], hT[:, m, t * P:(t + 1) * P], w[:, 0:width],
                                              start=m == 0, stop=m == M - 1)
                mm.then_inc(s["mm"], 1)

            rounds(pe, body)

        def proj_act(act, n):
            s, M = PJ[n], len(SPEC[n][0])

            def body(i):
                for m in range(M):
                    wait_last(act, s["mm"], i)
                    act.wait_ge(s["tr"], i * M + m + 1)
                    nc.scalar.copy(hT[0:D, m, 0:4 * P], ps[0:D, 0, :])
                    nc.scalar.copy(hT[0:D, m, 4 * P:GT * P], ps[0:D, 1, 0:(GT - 4) * P]).then_inc(s["ht"], 1)

            rounds(act, body)

        def proj_dve(dve, n):
            s, dests = PJ[n], SPEC[n][2]

            def body(i):
                for k, (a, b, to) in enumerate(dests):
                    if k == 0:
                        dve.wait_ge(s["mm"], i + 1)
                        dve.wait_ge(s_const, 1)
                    ins = nc.vector.tensor_copy(round_tiles(to, i)[:, :, 0:b - a], outp[:, 0:GT, a:b])
                ins.then_inc(s["ev"], 1)

            rounds(dve, body)

        def edge_pool(pool, n, table, width, free):
            s = L[n]
            with pool.Fori(0, ROUNDS) as i:
                for k in range(R):
                    count = pool.to_reg(i * R + k + 1)
                    pool.wait_ge(s_table, 16 * (n + 1))
                    pool.wait_ge(s[free], count)
                    pool.wait_ge(s["idx"], count)
                    for u in range(U):
                        nc.gpsimd.indirect_dma_start(
                            gat[:, k, u, 0:width], None, table,
                            bass.IndirectOffsetOnAxis(ap=idx[:, k, u:u + 1], axis=0)).then_inc(s["land"][k], 16)

        def first_indices(act, n):
            act.wait_ge(s_bcc, NTAB)
            for k in range(R):
                nc.scalar.copy(idx[:, k, :], sidx[:, k * U:(k + 1) * U]).then_inc(L[n]["idx"], 1)

        def next_indices(act, n, i, k):
            act.wait_ge(L[n]["land"][k], (i + 1) * 16 * U)
            act.wait_ge(s_bcc, NTAB)
            nc.scalar.copy(idx[:, k, :], sidx[:, bass.ds((i * R + k + R) * U, U)]).then_inc(L[n]["idx"], 1)

        def one_hot(dve, n, i, k, extra=False):
            kk = k % R
            at = (i * R + k) * U
            ins = nc.vector.tensor_tensor(
                oh[:, kk, :, :], iota[:, :].unsqueeze(1).to_broadcast([P, U, P]),
                dloc[:, bass.ds(at, U)].unsqueeze(2).to_broadcast([P, U, P]), ALU.is_equal)
            if extra:
                nc.vector.tensor_tensor(
                    olo[:, kk, :, :], iota[:, :].unsqueeze(1).to_broadcast([P, U, P]),
                    slo[:, bass.ds(at, U)].unsqueeze(2).to_broadcast([P, U, P]), ALU.is_equal)
                ins = nc.vector.tensor_tensor(
                    ohi[:, kk, :, :], iota[:, 0:TILES].unsqueeze(1).to_broadcast([P, U, TILES]),
                    shi[:, bass.ds(at, U)].unsqueeze(2).to_broadcast([P, U, TILES]), ALU.is_equal)
            ins.then_inc(L[n]["oh"], 1)

        def tile_of(eng, packed, u):
            return nc.s_assert_within(eng.snap((packed >> (6 * u)) & (TILE_BITS - 1)), 0, TILES - 1,
                                      skip_runtime_bounds_check_because="tiles are clamped where they are packed")

        def load_tiles(eng, g):
            packed = eng.value_load(tpk[0:1, bass.ds(g + 2, 1)])
            return [tile_of(eng, packed, u) for u in range(U)]

        def accumulate(dve, n, g, k, lag, places, width, us=range(U)):
            s, bank = L[n], (k + lag) % 2
            if us[0] == 0:
                dve.wait_ge(s["agg"], g + R + 1 - lag)
                dve.wait_ge(s["acc"], g + 1)
            for u in us:
                a = acc[:, u, bass.ds(places[u] * width, width)]
                ins = nc.vector.tensor_tensor(a, a, ps[:, 4 + bank, u * width:(u + 1) * width], ALU.add)
            if us[-1] == U - 1:
                ins.then_inc(s["acc"], 1)

        def zero_acc(dve, n, width):
            nc.vector.memset(acc[:, :, 0:TILES * width], 0.0).then_inc(L[n]["acc"], 1)
            dve.wait_ge(L[n]["acc"], 1)

        def zero_sums(pe, n, lag, width):
            pe.wait_ge(L[n]["acc"], 1)
            nc.tensor.matmul(ps[:, 4 + lag % 2, 0:U * width], zeros[:, 0:P], zeros[:, 0:U * width],
                             start=True, stop=True).then_inc(L[n]["agg"], R + 1 - lag)

        def zero_group(dve, n):
            s = L[n]
            nc.vector.memset(oh[:, R - 1, :, :], 0.0)
            if n == 0:
                nc.vector.memset(gat[:, R - 1, :, :], 0.0)
            nc.vector.memset(msg[:, 1, :, 0:W0 - 1], 0.0).then_inc(s["exp"], 1)
            nc.vector.memset(small[:, 0, 0:1], 0.0).then_inc(s["used"], R - 1 if n == 0 else R)

        def sum_edges(pe, n, g, k, width, rhs):
            pe.wait_ge(L[n]["acc"], g + 1)
            for u in range(U):
                mm = nc.tensor.matmul(ps[:, 4 + k % 2, u * width:(u + 1) * width], oh[:, k, u, :], rhs(u),
                                      start=True, stop=True)
            return mm

        def sum_messages(pe, n, g, k1, width):
            s = L[n]
            if n == 0:
                pe.wait_ge(s["used"], g + R)
            else:
                pe.wait_ge(s["exp"], g + 1)
            sum_edges(pe, n, g, k1, width, lambda u: msg[:, k1 % 2, u, 0:width]).then_inc(s["agg"], 1)

        def turn_onehot(pe, n, at, kk, b):
            for u in range(U):
                mm = nc.tensor.transpose(ps[:, b, u * P:(u + 1) * P], oh[:, kk, u, :], ident[:, :])
            mm.then_inc(L[n]["t"], 1)

        def dst_rows(pe, n, i, k, first):
            b = k % 2
            places = load_tiles(pe, i * R + k)
            pe.wait_ge(L[n]["oht"], i * R + k + 1)
            if first is not None:
                first()
            qf = q[:, :, :].rearrange("p t d -> p (t d)")
            for u in range(U):
                mm = nc.tensor.matmul(ps[:, 2 + b, u * D:(u + 1) * D], oht[:, b, u, :],
                                      qf[:, bass.ds(places[u] * D, D)], start=first is None, stop=True,
                                      skip_group_check=True)
            mm.then_inc(L[n]["qe"], 1)

        col = lambda a: a.rearrange("(p o) -> p o", o=1)
        WHOLE = EDGES // P
        LEFT = EDGES - WHOLE * P

        def chunks_of(eng, body):
            body(0, P)
            with eng.Fori(1, WHOLE) as c:
                body(c, P)
            if LEFT:
                body(WHOLE, LEFT)

        def sort_sp(sp):
            def count(c, n):
                wait_last(sp, S1["put"], c * 16)
                sp.dma_start(key_i[0:n, :], col(dst[bass.ds(c * P, n)]), allow_slow_non_contiguous=True).then_inc(S1["load"], 16)
                sp.dma_start(keys_i[0:n, 0:n], dst[bass.ds(c * P, n)].rearrange("(o a) -> o a", o=1).to_broadcast([n, n])).then_inc(S1["load"], 16)

            sp.dma_start(counts.rearrange("(a b) -> a b", b=P), zeros[0:TILES + 1, 0:P]).then_inc(S1["row"], 16)
            sp.wait_ge(S1["row"], 16)
            chunks_of(sp, count)
            sp.wait_ge(S1["put"], 16 * CHUNKS)
            sp.dma_start(count_row, counts[0:NPAD].rearrange("(o a) -> o a", o=1)).then_inc(S1["row"], 16)
            sp.wait_ge(S1["scan"], 1)
            sp.dma_start(counts[0:NPAD].rearrange("(o a) -> o a", o=1), start_row).then_inc(S1["row"], 16)
            sp.wait_ge(S1["row"], 48)
            sp.wait_ge(s_copy, 32)
            sp.wait_ge(s_acopy, 32)

            def place(c, n):
                for put in S2["put"]:
                    wait_last(sp, put, c * 16)
                sp.dma_start(key_i[0:n, :], col(dst[bass.ds(c * P, n)]), allow_slow_non_contiguous=True).then_inc(S2["load"], 16)
                sp.dma_start(src_i[0:n, :], col(src[bass.ds(c * P, n)]), allow_slow_non_contiguous=True).then_inc(S2["more"], 16)
                sp.dma_start(attr_c[0:n, :], attr[bass.ds(c * P, n), :]).then_inc(S2["more"], 16)

            chunks_of(sp, place)
            for put in S2["put"]:
                sp.wait_ge(put, 16 * CHUNKS)
            sp.dma_start(crow_i[0:1, 0, :], dst_s.rearrange("(o a) -> o a", o=1)[:, 0:EDGES:P], allow_slow_non_contiguous=True).then_inc(s_ends2, 16)
            sp.dma_start(crow_i[0:1, 1, 0:CHUNKS - 1], dst_s.rearrange("(o a) -> o a", o=1)[:, P - 1:EDGES:P], allow_slow_non_contiguous=True).then_inc(s_ends2, 16)
            sp.dma_start(crow_i[0:1, 1, CHUNKS - 1:CHUNKS], dst_s[EDGES - 1:EDGES].rearrange("(o a) -> o a", o=1)).then_inc(s_ends2, 16)

        def sort_pool(pool):
            row = lambda a: a.rearrange("(n o) -> n o", o=1)
            at = lambda a: bass.IndirectOffsetOnAxis(ap=a, axis=0)

            def after(semaphore, count):
                count = count if isinstance(count, int) else pool.to_reg(count)
                pool.wait_ge(s_pool, 5)
                pool.wait_ge(semaphore, count)

            def count(c, n):
                after(S1["load"], (c + 1) * 32)
                nc.gpsimd.indirect_dma_start(seen[0:n, :], None, row(counts), at(key_i[0:n, :])).then_inc(S1["seen"], 16)
                after(S1["new"], c + 1)
                nc.gpsimd.indirect_dma_start(row(counts), at(idx_i[0:n, :]), fresh[0:n, :], None).then_inc(S1["put"], 16)

            def place(c, n):
                after(S2["load"], (c + 1) * 16)
                nc.gpsimd.indirect_dma_start(seen[0:n, :], None, row(counts), at(key_i[0:n, :])).then_inc(S2["seen"], 16)
                after(S2["more"], (c + 1) * 32)
                pool.wait_ge(S2["pos"], c + 1)
                for put, to, of in zip(S2["put"], (row(dst_s), row(src_s), attr_s), (key_i, src_i, attr_c)):
                    nc.gpsimd.indirect_dma_start(to, at(pos_i[0:n, :]), of[0:n, :], None).then_inc(put, 16)

            pool.wait_ge(s_tri, 1)
            nc.gpsimd.affine_select(out=below, in_=below, compare_op=ALU.is_gt, fill=0.0, base=0,
                                    pattern=[[-1, P]], channel_multiplier=1).then_inc(s_low, 1)
            chunks_of(pool, count)
            chunks_of(pool, place)
            for put in S2["put"]:
                pool.wait_ge(put, 16 * CHUNKS)

        def sort_dve(dve):
            v = nc.vector
            LINKS = 8

            def count(c, n):
                done = [0]

                def link(ins):
                    done[0] += 1
                    ins.then_inc(S1["chain"], 1)
                    dve.wait_ge(S1["chain"], c * LINKS + done[0])

                dve.wait_ge(S1["load"], (c + 1) * 32)
                v.tensor_copy(key[0:n, :], key_i[0:n, :])
                link(v.tensor_copy(keys[0:n, 0:n], keys_i[0:n, 0:n]))
                link(v.tensor_scalar(same[0:n, 0:n], keys[0:n, 0:n], key[0:n, :], None, ALU.is_equal))
                link(v.tensor_tensor(before[0:n, 0:n], same[0:n, 0:n], below[0:n, 0:n], ALU.mult))
                v.tensor_reduce(total[0:n, :], same[0:n, 0:n], AX.X, ALU.add)
                link(v.tensor_reduce(rank[0:n, :], before[0:n, 0:n], AX.X, ALU.add))
                link(v.scalar_tensor_tensor(last[0:n, :], rank[0:n, :], 1.0, total[0:n, :], ALU.add, ALU.is_equal))
                link(v.tensor_tensor(key[0:n, :], key[0:n, :], spare[0:n, :], ALU.subtract))
                link(v.tensor_tensor(key[0:n, :], key[0:n, :], last[0:n, :], ALU.mult))
                link(v.tensor_tensor(idx_i[0:n, :], key[0:n, :], spare[0:n, :], ALU.add))
                assert done[0] == LINKS
                dve.wait_ge(S1["seen"], (c + 1) * 16)
                v.tensor_tensor(ranks[0:n, bass.ds(c, 1)], rank[0:n, :], seen[0:n, :], ALU.add)
                v.tensor_tensor(fresh[0:n, :], total[0:n, :], seen[0:n, :], ALU.add).then_inc(S1["new"], 1)

            def place(c, n):
                dve.wait_ge(S2["seen"], (c + 1) * 16)
                v.tensor_tensor(pos_i[0:n, :], ranks[0:n, bass.ds(c, 1)], seen[0:n, :], ALU.add).then_inc(S2["pos"], 1)

            done = [0]

            def link(ins):
                done[0] += 1
                ins.then_inc(S1["scanned"], 1)
                dve.wait_ge(S1["scanned"], done[0])

            v.memset(below, 1.0).then_inc(s_tri, 1)
            link(v.tensor_scalar(spare, step[:, 0:1], float(NPAD), None, ALU.add))
            dve.wait_ge(s_low, 1)
            chunks_of(dve, count)
            dve.wait_ge(S1["row"], 32)
            zrow = h[0:1, :, :].rearrange("p t d -> p (t d)")
            link(v.memset(zrow, 0.0))
            half = TILES * D
            for m in range(2):
                part = slice(m * half, (m + 1) * half)
                link(v.tensor_tensor_scan(start_row[:, part], count_row[:, part], zrow, 0.0 if m == 0 else start_row[:, half - 1:half],
                                          ALU.add, ALU.add))
            v.tensor_tensor(start_row, start_row, count_row, ALU.subtract).then_inc(S1["scan"], 1)
            dve.wait_ge(S1["scan"], 1)
            link(v.memset(crow[0:1, 3, :], 0.0))
            chunks_of(dve, place)
            dve.wait_ge(s_ends2, 48)

        @block.sync
        def _(sp):
            sp.wait_ge(s_const, 1)
            sp.dma_start(order_i, dst.rearrange("(a b) -> a b", b=OLEN)).then_inc(s_order, 16)
            sp.dma_start(next_i[0:OROWS - 1, :], dst.rearrange("(a b) -> a b", b=OLEN)[1:OROWS, 0:1], allow_slow_non_contiguous=True).then_inc(s_order, 16)
            for t0, t1, r in ((0, FULL, P), (FULL, TILES, REST)):
                part = x[t0 * P:t0 * P + (t1 - t0 - 1) * P + r, :].rearrange("(t p) f -> p t f", p=r)
                sp.dma_start(xs[0:r, t0:t1, :], part).then_inc(s_x, 16)
            sp.dma_start(dst_s[0:EDGES].rearrange("(a b) -> a b", b=160), dst.rearrange("(a b) -> a b", b=160)).then_inc(s_copy, 16)
            sp.dma_start(src_s[0:EDGES].rearrange("(a b) -> a b", b=160), src.rearrange("(a b) -> a b", b=160)).then_inc(s_copy, 16)
            sp.dma_start(crow_i[0:1, 0, :], dst.rearrange("(a o) -> o a", a=EDGES)[:, 0:EDGES:P], allow_slow_non_contiguous=True).then_inc(s_ends, 16)
            sp.dma_start(crow_i[0:1, 1, 0:CHUNKS - 1], dst.rearrange("(a o) -> o a", a=EDGES)[:, P - 1:EDGES:P], allow_slow_non_contiguous=True).then_inc(s_ends, 16)
            sp.dma_start(crow_i[0:1, 1, CHUNKS - 1:CHUNKS], dst[EDGES - 1:EDGES].rearrange("(o a) -> o a", o=1)).then_inc(s_ends, 16)
            sp.dma_start(dst_s[EDGES:EPAD].rearrange("(o a) -> o a", o=1), padi[0:1, 0, 0:EPAD - EDGES]).then_inc(s_pad, 16)
            sp.dma_start(src_s[EDGES:EPAD].rearrange("(o a) -> o a", o=1), padi[0:1, 1, 0:EPAD - EDGES]).then_inc(s_pad, 16)
            wload = [(w_kvqf[0:D, 0:D], wk), (w_kvqf[0:D, D:2 * D], wv), (w_kvqf[0:D, 2 * D:3 * D], wq),
                     (w_kvqf[0:D, 3 * D:4 * D], wf), (w_o[0:D, :], wo), (w_g[0:D, :], w_gcn),
                     (w_pq[0:D, 0:D], w1t[0:D, :]), (w_pq[0:D, D:2 * D], w1t[D:2 * D, :]), (w_m[0:D, :], w2t),
                     (w_i[0:D, 0:3 * D], wiht), (w_h[0:D, 0:2 * D], whht[:, 0:2 * D]),
                     (w_h[0:D, 3 * D:4 * D], whht[:, 2 * D:3 * D])]
            row = lambda v: v.rearrange("(o a) -> o a", o=1)
            wload += [(w_kvqf[D:D + 1, 0:D], row(bk)), (w_kvqf[D:D + 1, D:2 * D], row(bv)),
                      (w_kvqf[D:D + 1, 2 * D:3 * D], row(bq)), (w_kvqf[D:D + 1, 3 * D:4 * D], row(bf)),
                      (w_o[D:D + 1, :], row(bo)), (w_pq[D:D + 1, 0:D], row(b1)), (w_i[D:D + 1, 0:3 * D], row(bih)),
                      (w_h[D:D + 1, 0:2 * D], row(bhh[0:2 * D])), (w_h[D:D + 1, 3 * D:4 * D], row(bhh[2 * D:3 * D]))]
            wload += [(brow[0:1, n * D:(n + 1) * D], row(v)) for n, v in enumerate((gamma, beta, b_gcn, b2))]
            wload += [(w_e[DE * u:DE * (u + 1), D * u:D * (u + 1)], w1t[2 * D:2 * D + DE, :]) for u in range(U)]
            for to, of in wload:
                sp.dma_start(to, of).then_inc(s_w, 16)
            assert len(wload) == N_WEIGHTS
            sp.dma_start(attr_s[0:EDGES, :].rearrange("(a b) f -> a (b f)", b=125), attr.rearrange("(a b) f -> a (b f)", b=125)).then_inc(s_acopy, 16)
            sp.dma_start(attr_s[EDGES:EPAD, :], zeros[0:EPAD - EDGES, 0:DE]).then_inc(s_acopy, 16)
            sp.wait_ge(s_flag, 1)
            with sp.If(sp.value_load(unsorted[0:1, 0:1]) > 0):
                sort_sp(sp)
            sp.wait_ge(s_packed, 2)
            sp.dma_start(tiles_d.rearrange("(a b) -> a b", b=P // U), pack_i[:, 0:P // U]).then_inc(s_packd, 16)
            sp.dma_start(chunks_d.rearrange("(a b) -> a b", b=P // 2), pack_i[:, P // U:P // U + P // 2]).then_inc(s_packd, 16)
            sp.wait_ge(s_packd, 32)
            sp.dma_start(tpk[0:1, 2:2 + SPAD // U], tiles_d.rearrange("(o a) -> o a", o=1)).then_inc(s_packl, 16)
            sp.dma_start(cpk[:, :], chunks_d.rearrange("(o a) -> o a", o=1)).then_inc(s_packl, 16)
            sp.wait_ge(PJ[0]["ev"], NR)
            sp.dma_start(kv_rows.rearrange("(t p) f -> p t f", p=P),
                         stage[:, :, :].rearrange("p a (t f) -> p (a t f)", f=D).rearrange("p (t f) -> p t f", f=2 * D)).then_inc(s_table, 16)
            for n in range(2):
                sp.wait_ge(*((s_stage, 1), (PJ[3]["ev"], NR))[n])
                sp.dma_start(rows[n].rearrange("(t p) f -> p t f", p=P), (y[:, :, :], stage[:, 0, :].rearrange("p (t f) -> p t f", f=D))[n]).then_inc(s_table, 16)
            sp.wait_ge(s_packl, 32)
            sp.wait_ge(s_acopy, 32)
            def load_attributes(g, k):
                sp.wait_ge(s_atc, g + 1)
                for half in range(U // 2):
                    at = g * (U // 2) + half
                    packed = sp.value_load(cpk[0:1, at:at + 1] if isinstance(at, int) else cpk[0:1, bass.ds(at, 1)])
                    for e in range(2):
                        c = nc.s_assert_within(sp.snap((packed >> (11 * e)) & (CHUNK_BITS - 1)), 0, CHUNKS - 1,
                                               skip_runtime_bounds_check_because="a count of chunks less one")
                        sp.dma_start(att[:, k, 2 * half + e, :], attr_s[bass.ds(c * P, P), :]).then_inc(s_att[k], 16)

            with sp.Fori(0, ROUNDS) as i:
                for k in range(R):
                    load_attributes(i * R + k, k)
            load_attributes(ROUNDS * R, 0)
            sp.wait_ge(s_stage, 2)
            sp.dma_start(rows[2].rearrange("(t p) f -> p t f", p=P), stage[:, 0, :].rearrange("p (t f) -> p t f", f=D)).then_inc(s_table, 16)
            sp.wait_ge(s_fin, 1)
            sp.dma_start(out[0:FULL * P, :].rearrange("(t p) f -> p t f", p=P), xs[:, 0:FULL, :]).then_inc(s_out, 16)
            sp.dma_start(out[FULL * P:NODES, :], xs[0:REST, FULL, :]).then_inc(s_out, 16)
            sp.wait_ge(s_out, 32)

        @block.gpsimd
        def _(pool):
            nc.gpsimd.memset(ident[:, :], 0.0).then_inc(s_pool, 1)
            pool.wait_ge(s_pool, 1)
            nc.gpsimd.affine_select(out=ident[:, :], in_=ident[:, :], compare_op=ALU.not_equal, fill=1.0, base=0,
                                    pattern=[[-1, P]], channel_multiplier=1).then_inc(s_pool, 1)
            nc.gpsimd.iota(iota_i[:, :], [[1, P]], base=0, channel_multiplier=0).then_inc(s_pool, 1)
            nc.gpsimd.iota(step_i[:, :], [[P, SB]], base=0, channel_multiplier=1).then_inc(s_pool, 1)
            nc.gpsimd.iota(chunk_no, [[1, CW]], base=0, channel_multiplier=0,
                           allow_small_or_imprecise_dtypes=True).then_inc(s_pool, 1)
            pool.wait_ge(s_flag, 1)
            with pool.If(pool.value_load(unsorted[0:1, 0:1]) > 0):
                sort_pool(pool)
            pool.wait_ge(s_copy, 32)
            pool.wait_ge(s_pad, 32)
            pool.wait_ge(s_cidx, 1)
            for j in range(SB):
                for to, of, landed in ((dg, dst_s, s_eg), (sg, src_s, s_eg2)):
                    nc.gpsimd.indirect_dma_start(
                        to[:, j * P:(j + 1) * P], None, of.rearrange("(c e) -> c e", e=P),
                        bass.IndirectOffsetOnAxis(ap=cs_i[:, j:j + 1], axis=0)).then_inc(landed, 16)
            proj_pool(pool, 0)
            edge_pool(pool, 0, kv_rows, 2 * D, "used")
            proj_pool(pool, 1)
            proj_pool(pool, 2)
            edge_pool(pool, 1, rows[0], D, "agg")
            proj_pool(pool, 3)
            edge_pool(pool, 2, rows[1], D, "used")
            proj_pool(pool, 4 + 1)
            proj_pool(pool, 4)
            edge_pool(pool, 3, rows[2], D, "agg")

        @block.scalar
        def _(act):
            roots = iter(range(8))

            def root():
                act.wait_ge(s_var, next(roots) + 1)
                nc.scalar.activation(small[:, 3, :], small[:, 2, :], ACT.Sqrt).then_inc(s_sd, 1)

            for t, to in enumerate((dloc, sidx, slo, shi)):
                for j in range(0, SB, 4):
                    m = min(4, SB - j)
                    n = t * (-(-SB // 4)) + j // 4
                    act.wait_ge(s_tabt, n + 1)
                    nc.scalar.copy(to[:, j * P:(j + m) * P], ps[:, n % 2, 0:m * P]).then_inc(s_bcc, 1)
            root()
            proj_act(act, 0)

            s = L[0]
            first_indices(act, 0)
            act.wait_ge(s["t"], 1)
            nc.scalar.copy(oht[:, 0, :, :], ps[:, 0, :]).then_inc(s["oht"], 1)
            with act.Fori(0, ROUNDS) as i:
                for k in range(R):
                    b = k % 2
                    act.wait_ge(s["t"], i * R + k + 2)
                    nc.scalar.copy(oht[:, 1 - b, :, :], ps[:, 1 - b, :]).then_inc(s["oht"], 1)
                    act.wait_ge(s["clip"], i * R + k + 1)
                    act.wait_ge(s["agg"], i * R + k + 3)
                    nc.scalar.activation(msg[:, b, :, D:D + HEADS],
                                         sc[:, b, 1, :].rearrange("p (u h) -> p u h", h=HEADS), ACT.Exp, scale=SCALE).then_inc(s["exp"], 1)
                    next_indices(act, 0, i, k)
            proj_act(act, 1)
            root()
            root()
            root()
            proj_act(act, 2)
            first_indices(act, 1)
            with act.Fori(0, ROUNDS) as i:
                for k in range(R):
                    next_indices(act, 1, i, k)
            root()
            proj_act(act, 3)

            s = L[2]
            first_indices(act, 2)
            act.wait_ge(s["t"], 1)
            nc.scalar.copy(oht[:, 0, :, :], ps[:, 0, :]).then_inc(s["oht"], 1)
            act.wait_ge(s_atc, R + 1)
            nc.scalar.copy(attT[:, 0, :], ps[:, 6, 0:P]).then_inc(s["clip"], 1)
            with act.Fori(0, ROUNDS) as i:
                for k in range(R):
                    b = k % 2
                    act.wait_ge(s["t"], i * R + k + 2)
                    nc.scalar.copy(oht[:, 1 - b, :, :], ps[:, 1 - b, :]).then_inc(s["oht"], 1)
                    act.wait_ge(s_atc, i * R + k + 2 + R)
                    nc.scalar.copy(attT[:, 1 - b, :], ps[:, 7 - b, 0:P]).then_inc(s["clip"], 1)
                    act.wait_ge(s["used"], i * R + k + 5)
                    act.wait_ge(s["agg"], i * R + k + 3)
                    nc.scalar.activation(msg[:, b, :, 0:D], prod[:, b, :].rearrange("p (u d) -> p u d", d=D), ACT.Relu).then_inc(s["exp"], 1)
                    next_indices(act, 2, i, k)
            proj_act(act, 5)
            proj_act(act, 4)
            gates = flat[:, 0:TILES * 4 * D].rearrange("p (t c) -> p t c", c=4 * D)
            act.wait_ge(s_gates, 1)
            nc.scalar.activation(gates[:, :, 0:2 * D], gates[:, :, 0:2 * D], ACT.Sigmoid).then_inc(s_gact, 1)
            act.wait_ge(s_gates, 2)
            nc.scalar.activation(gates[:, :, 2 * D:3 * D], gates[:, :, 2 * D:3 * D], ACT.Tanh).then_inc(s_gact, 1)
            root()
            root()
            root()
            first_indices(act, 3)
            with act.Fori(0, ROUNDS) as i:
                for k in range(R):
                    next_indices(act, 3, i, k)

        @block.tensor
        def _(pe):
            pe.wait_ge(s_pool, 2)
            pe.wait_ge(s_fell, 1)
            nc.tensor.transpose(ps[0:1, 0, 0:P], fell[:, :], ident[:, :]).then_inc(s_fellt, 1)
            for n in range(2):
                pe.wait_ge(s_rows, n + 1)
                for j in range(4):
                    a, b = j * 512, min(CW, (j + 1) * 512)
                    mm = nc.tensor.matmul(ps[:, 4 * n + j, 0:b - a], ones[:, :], crow[0:1, 2 + n, a:b], start=True, stop=True)
                mm.then_inc(s_bc, 1)
            pe.wait_ge(s_w, 16 * N_WEIGHTS)
            pe.wait_ge(s_cidx, 1)
            nc.tensor.matmul(ps[:, 7, 0:4 * D], ones[:, :], brow[:, :], start=True, stop=True).then_inc(s_bc, 1)
            pe.wait_ge(s_pool, 5)
            nc.tensor.transpose(ps[0:SB, 2, 0:P], cs[:, 2, :], ident[:, :])
            nc.tensor.transpose(ps[0:SB, 2, P:2 * P], cs[:, 3, :], ident[:, :]).then_inc(s_packt, 1)
            for t, of in enumerate((df, sf, lof, hif)):
                pe.wait_ge(s_tabs, t + 1)
                for j in range(0, SB, 4):
                    m = min(4, SB - j)
                    n = t * (-(-SB // 4)) + j // 4
                    if n >= 2:
                        pe.wait_ge(s_bcc, n - 1)
                    for e in range(m):
                        mm = nc.tensor.transpose(ps[:, n % 2, e * P:(e + 1) * P], of[:, (j + e) * P:(j + e + 1) * P], ident[:, :])
                    mm.then_inc(s_tabt, 1)
            proj_pe(pe, 0)
            pe.wait_ge(s_packl, 32)

            s = L[0]
            zero_sums(pe, 0, 2, W0)

            pe.wait_ge(s["oh"], 1)
            turn_onehot(pe, 0, 0, 0, 0)
            with pe.Fori(0, ROUNDS) as i:
                for k in range(R):
                    b = k % 2
                    dst_rows(pe, 0, i, k, None)
                    pe.wait_ge(s["oh"], i * R + k + 2)
                    turn_onehot(pe, 0, None, (k + 1) % R, 1 - b)
                    sum_messages(pe, 0, i * R + k, (k - 1) % R, W0)
            sum_messages(pe, 0, ROUNDS * R, R - 1, W0)
            proj_pe(pe, 1)
            proj_pe(pe, 2)

            s = L[1]
            zero_sums(pe, 1, 1, D)
            nc.tensor.matmul(ps[:, 6, 0:TILES], zerob[:, :], zerob[:, 0:TILES], start=True, stop=False, skip_group_check=True)
            with pe.Fori(0, ROUNDS) as i:
                for k in range(R):
                    pe.wait_ge(s["oh"], i * R + k + 1)
                    pe.wait_ge(s["land"][k], (i + 1) * 16 * U)
                    mm = sum_edges(pe, 1, i * R + k, k, D, lambda u: gat[:, k, u, 0:D])
                    for u in range(U):
                        mm = nc.tensor.matmul(ps[:, 6, 0:TILES], olo[:, k, u, :], ohi[:, k, u, :], start=False, stop=False,
                                              skip_group_check=True)
                    mm.then_inc(s["agg"], 1)
            nc.tensor.matmul(ps[:, 6, 0:TILES], zerob[:, :], zerob[:, 0:TILES], start=False, stop=True,
                             skip_group_check=True).then_inc(s_hist, 1)
            proj_pe(pe, 3)

            s = L[2]
            zero_sums(pe, 2, 2, D)
            pe.wait_ge(s["oh"], 1)
            turn_onehot(pe, 2, 0, 0, 0)
            pe.wait_ge(s_att[0], 16 * U)
            nc.tensor.transpose(ps[:, 6, 0:P], att[:, 0, :, :], ident[:, :]).then_inc(s_atc, 1)
            with pe.Fori(0, ROUNDS) as i:
                for k in range(R):
                    b, k1 = k % 2, (k + 1) % R
                    pe.wait_ge(s["clip"], i * R + k + 1)
                    dst_rows(pe, 2, i, k, lambda: nc.tensor.matmul(
                        ps[:, 2 + b, 0:U * D], attT[:, b, :], w_e[:, :], start=True, stop=False, skip_group_check=True))
                    pe.wait_ge(s["oh"], i * R + k + 2)
                    turn_onehot(pe, 2, None, k1, 1 - b)
                    if k < R - 1:
                        pe.wait_ge(s_att[k1], (i + 1) * 16 * U)
                    else:
                        pe.wait_ge(s_att[k1], (i + 2) * 16 * U)
                    nc.tensor.transpose(ps[:, 7 - b, 0:P], att[:, k1, :, :], ident[:, :]).then_inc(s_atc, 1)
                    sum_messages(pe, 2, i * R + k, (k - 1) % R, D)
            sum_messages(pe, 2, ROUNDS * R, R - 1, D)
            proj_pe(pe, 5)
            proj_pe(pe, 4)

            s = L[3]
            zero_sums(pe, 3, 1, D)
            with pe.Fori(0, ROUNDS) as i:
                for k in range(R):
                    pe.wait_ge(s["oh"], i * R + k + 1)
                    pe.wait_ge(s["land"][k], (i + 1) * 16 * U)
                    sum_edges(pe, 3, i * R + k, k, D, lambda u: gat[:, k, u, 0:D]).then_inc(s["agg"], 1)

        @block.vector
        def _(dve):
            v = nc.vector
            links = [0]

            def link(ins):
                links[0] += 1
                ins.then_inc(s_d, 1)
                dve.wait_ge(s_d, links[0])

            v.memset(zeros[:, :], 0.0)
            v.memset(zerob[:, :], 0.0)
            v.memset(ones[:, :], 1.0)
            v.memset(padi[0:1, 0, :], BIG)
            v.memset(padi[0:1, 1, :], 0)
            v.memset(hT[D:D + 1, :, :], 1.0)
            for w in (w_g, w_m, w_pq):
                v.memset(w[D:D + 1, :], 0.0)
            for w in (w_i, w_h, w_e):
                v.memset(w[:, :], 0.0)
            v.memset(tpk[0:1, 0:2], 0)
            v.memset(msg[:, :, :, W0 - 1:W0], 1.0)
            v.memset(crow[0:1, 3, :], 0.0)
            v.memset(xs[:, FULL:TILES, :], 0.0).then_inc(s_const, 1)
            v.memset(small[:, :, :], 0.0).then_inc(s_atc, R)

            v.memset(falls[:, OLEN - 1:OLEN], 0.0)
            link(v.memset(fell[:, :], 0.0))
            dve.wait_ge(s_order, 32)
            v.tensor_tensor(falls[:, 0:OLEN - 1], order_i[:, 0:OLEN - 1], order_i[:, 1:OLEN], ALU.is_gt)
            link(v.tensor_tensor(falls[0:OROWS - 1, OLEN - 1:OLEN], order_i[0:OROWS - 1, OLEN - 1:OLEN], next_i[0:OROWS - 1, :], ALU.is_gt))
            v.tensor_reduce(fell[0:OROWS, :], falls, AX.X, ALU.max).then_inc(s_fell, 1)
            dve.wait_ge(s_fellt, 1)
            v.tensor_reduce(unsorted[0:1, 0:1], ps[0:1, 0, 0:P], AX.X, ALU.max).then_inc(s_flag, 1)
            dve.wait_ge(s_flag, 1)
            dve.wait_ge(s_pool, 5)
            v.tensor_copy(iota[:, :], iota_i[:, :])
            link(v.tensor_copy(step[:, :], step_i[:, :]))
            dve.wait_ge(s_ends, 48)
            with dve.If(dve.value_load(unsorted[0:1, 0:1]) > 0):
                sort_dve(dve)

            dve.wait_ge(s_ends, 48)
            link(v.tensor_scalar(crow_i[:, :, :], crow_i[:, :, :], 7, None, ALU.arith_shift_right))
            link(v.tensor_copy(crow[0:1, 0:2, :], crow_i[:, :, :]))
            link(v.tensor_tensor(crow[0:1, 1, :], crow[0:1, 1, :], crow[0:1, 0, :], ALU.subtract))
            link(v.tensor_tensor_scan(crow[0:1, 2, :], crow[0:1, 1, :], crow[0:1, 3, :], 0.0, ALU.add, ALU.add))
            link(v.tensor_tensor(crow[0:1, 2, :], crow[0:1, 2, :], crow[0:1, 1, :], ALU.subtract))
            dve.wait_ge(s_pool, 5)
            ins = v.tensor_tensor(crow[0:1, 2, :], crow[0:1, 2, :], chunk_no, ALU.add)
            ins.then_inc(s_rows, 1)
            dve.wait_ge(s_rows, 1)
            link(v.tensor_tensor(crow[0:1, 0, :], crow[0:1, 0, :], crow[0:1, 2, :], ALU.subtract))
            link(v.tensor_copy(crow[0:1, 3, 0:1], crow[0:1, 0, 0:1]))
            v.tensor_tensor(crow[0:1, 3, 1:CW], crow[0:1, 0, 1:CW], crow[0:1, 0, 0:CW - 1], ALU.subtract).then_inc(s_rows, 1)
            dve.wait_ge(s_bc, 2)
            link(v.tensor_copy(off_b, ps[:, 0:4, :].rearrange("p b n -> p (b n)")[:, 0:CW]))
            link(v.tensor_copy(dw_b, ps[:, 4:8, :].rearrange("p b n -> p (b n)")[:, 0:CW]))
            for j in range(SB):
                link(v.tensor_scalar(mask_b, off_b, step[:, j:j + 1], None, ALU.is_le, ALU.add, accum_out=cs[:, 0, j:j + 1]))
                link(v.tensor_tensor_reduce(mask_b, mask_b, dw_b, 1.0, 0.0, ALU.mult, ALU.add, cs[:, 1, j:j + 1]))
            link(v.tensor_scalar(cs[:, 3, :], cs[:, 0, :], -1.0, None, ALU.add))
            link(v.tensor_tensor(cs[:, 4, :], cs[:, 1, :], step[:, :], ALU.add))
            link(v.tensor_scalar(cs[:, 2, :], cs[:, 4, :], float(TILES - 1), None, ALU.min))
            link(v.tensor_scalar(cs[:, 5, :], cs[:, 4, :], float(P), None, ALU.mult))
            v.tensor_copy(cs_i[:, :], cs[:, 3, :]).then_inc(s_cidx, 1)
            dve.wait_ge(s_bc, 3)
            link(v.tensor_copy(bc[:, :], ps[:, 7, 0:4 * D]))
            dve.wait_ge(s_packt, 1)
            link(v.tensor_copy(packf[:, 0:2, :], ps[0:SB, 2, 0:2 * P].rearrange("p (a b) -> p a b", b=P)))
            t4 = packf[:, 0, :].rearrange("p (g u) -> p g u", u=4)
            c2 = packf[:, 1, :].rearrange("p (g u) -> p g u", u=2)
            G4 = P // U
            for m in range(2):
                link(v.scalar_tensor_tensor(packf[:, 2, m * G4:(m + 1) * G4], t4[:, :, 2 * m + 1], float(TILE_BITS), t4[:, :, 2 * m],
                                            ALU.mult, ALU.add))
            v.scalar_tensor_tensor(pack_i[:, 0:G4], packf[:, 2, G4:2 * G4], float(TILE_BITS ** 2), packf[:, 2, 0:G4],
                                   ALU.mult, ALU.add).then_inc(s_packed, 1)
            v.scalar_tensor_tensor(pack_i[:, G4:G4 + P // 2], c2[:, :, 1], float(CHUNK_BITS), c2[:, :, 0],
                                   ALU.mult, ALU.add).then_inc(s_packed, 1)
            dve.wait_ge(s_eg, 16 * SB)
            link(v.tensor_copy(df, dg))
            by_step = lambda a: a.rearrange("p (j e) -> p j e", e=P)
            last = v.tensor_tensor(by_step(df), by_step(df), cs[:, 5, :].unsqueeze(2).to_broadcast([P, SB, P]), ALU.subtract)
            last.then_inc(s_tabs, 1)
            dve.wait_ge(s_tabs, 1)
            dve.wait_ge(s_eg2, 16 * SB)
            v.tensor_copy(sf, sg).then_inc(s_tabs, 1)
            link(v.tensor_scalar(lo_i, sg, P - 1, None, ALU.bitwise_and))
            v.tensor_copy(lof, lo_i).then_inc(s_tabs, 1)
            link(v.tensor_scalar(vf, df, 0.0, None, ALU.is_ge))
            link(v.scalar_tensor_tensor(vf, df, float(P), vf, ALU.is_lt, ALU.mult))
            link(v.tensor_scalar(vf, vf, -OUTSIDE, OUTSIDE, ALU.mult, ALU.add))
            link(v.tensor_scalar(hi_i, sg, 7, None, ALU.arith_shift_right))
            link(v.tensor_copy(hif, hi_i))
            v.tensor_tensor(hif, hif, vf, ALU.add).then_inc(s_tabs, 1)
            dve.wait_ge(s_bcc, NTAB)

            tmp0, tmp1 = (stage[:, n, :].rearrange("p (t d) -> p t d", d=D) for n in range(2))
            per_node = lambda a: a.unsqueeze(2).to_broadcast([P, TILES, D])
            per_feature = lambda n: bc[:, n * D:(n + 1) * D].unsqueeze(1).to_broadcast([P, TILES, D])
            nroot = [0]

            def inverse_root(to):
                nroot[0] += 1
                dve.wait_ge(s_sd, nroot[0])
                link(v.reciprocal(to, small[:, 3, :]))

            def center(a):
                link(v.tensor_reduce(small[:, 0, :], a[:, :, :], AX.X, ALU.add))
                link(v.tensor_scalar(small[:, 0, :], small[:, 0, :], 1.0 / D, None, ALU.mult))
                link(v.tensor_tensor(tmp0, a[:, :, :], per_node(small[:, 0, :]), ALU.subtract))
                link(v.tensor_tensor(tmp1, tmp0, tmp0, ALU.mult))
                link(v.tensor_reduce(small[:, 2, :], tmp1, AX.X, ALU.add))
                v.tensor_scalar(small[:, 2, :], small[:, 2, :], 1.0 / D, EPS, ALU.mult, ALU.add).then_inc(s_var, 1)
                inverse_root(small[:, 1, :])

            def root_of(a, op, c, to):
                v.tensor_scalar(small[:, 2, :], a, c, None, op).then_inc(s_var, 1)
                inverse_root(to)

            def norm_relu():
                return v.scalar_tensor_tensor(h[:, :, :], tmp0, 0.0, per_node(small[:, 1, :]), ALU.max, ALU.mult)

            def edge_sums(n, lag, width):
                for g in range(ROUNDS * R, ROUNDS * R + lag):
                    accumulate(dve, n, g, g % R, lag, load_tiles(dve, g - lag), width)
                dve.wait_ge(L[n]["acc"], ROUNDS * R + lag + 1)
                a = [acc[:, u, 0:TILES * width] for u in range(U)]
                link(v.tensor_tensor(a[0], a[0], a[1], ALU.add))
                link(v.tensor_tensor(a[2], a[2], a[3], ALU.add))
                link(v.tensor_tensor(a[0], a[0], a[2], ALU.add))
                return a[0].rearrange("p (t c) -> p t c", c=width)

            dve.wait_ge(s_x, 32)
            center(xs)
            norm_relu().then_inc(PJ[0]["ready"], 1)
            proj_dve(dve, 0)
            dve.wait_ge(s_packl, 32)

            s = L[0]
            zero_acc(dve, 0, W0)
            zero_group(dve, 0)
            one_hot(dve, 0, 0, 0)

            def weigh_values(g, k1):
                c = k1 % 2
                dve.wait_ge(s["exp"], g + 1)
                v.tensor_tensor(
                    msg[:, c, :, 0:D].rearrange("p u (h d) -> p u h d", d=DH),
                    gat[:, k1, :, D:2 * D].rearrange("p u (h d) -> p u h d", d=DH),
                    msg[:, c, :, D:D + HEADS].unsqueeze(3).to_broadcast([P, U, HEADS, DH]), ALU.mult).then_inc(s["used"], 1)

            with dve.Fori(0, ROUNDS) as i:
                for k in range(R):
                    g, b = i * R + k, k % 2
                    dve.wait_ge(s["agg"], g + 2)
                    one_hot(dve, 0, i, k + 1)
                    weigh_values(g, (k - 1) % R)
                    places = load_tiles(dve, g - 2)
                    dve.wait_ge(s["land"][k], (i + 1) * 16 * U)
                    dve.wait_ge(s["qe"], g + 1)
                    v.tensor_tensor(prod[:, b, :].rearrange("p (u d) -> p u d", d=D),
                                    ps[:, 2 + b, 0:U * D].rearrange("p (u d) -> p u d", d=D), gat[:, k, :, 0:D],
                                    ALU.mult).then_inc(s["prod"], 1)
                    accumulate(dve, 0, g, k, 2, places, W0, range(U // 2))
                    dve.wait_ge(s["prod"], g + 1)
                    v.tensor_reduce(sc[:, b, 0, :], prod[:, b, :].rearrange("p (a d) -> p a d", d=DH), AX.X, ALU.add).then_inc(s["red"], 1)
                    accumulate(dve, 0, g, k, 2, places, W0, range(U // 2, U))
                    dve.wait_ge(s["red"], g + 1)
                    v.tensor_scalar(sc[:, b, 1, :], sc[:, b, 0, :], -CLIP, CLIP, ALU.max, ALU.min).then_inc(s["clip"], 1)
            weigh_values(ROUNDS * R, R - 1)
            a0 = edge_sums(0, 2, W0)
            v.tensor_copy(cnt[:, :], a0[:, :, W0 - 1])
            link(v.tensor_scalar(z1[:, :, :], a0[:, :, D:D + HEADS], 1.0, None, ALU.add))
            link(v.reciprocal(z1[:, :, :], z1[:, :, :]))
            v.tensor_tensor(h[:, :, :].rearrange("p t (a d) -> p t a d", d=DH), a0[:, :, 0:D].rearrange("p t (a d) -> p t a d", d=DH),
                            z1[:, :, :].unsqueeze(3).to_broadcast([P, TILES, HEADS, DH]), ALU.mult).then_inc(PJ[1]["ready"], 1)
            proj_dve(dve, 1)
            dve.wait_ge(PJ[1]["ev"], NR)
            link(v.tensor_tensor(y[:, :, :], y[:, :, :], tmp0, ALU.add))
            center(y)
            link(v.tensor_tensor(tmp0, tmp0, per_node(small[:, 1, :]), ALU.mult))
            link(v.tensor_tensor(tmp0, tmp0, per_feature(0), ALU.mult))
            link(v.tensor_tensor(tmp0, tmp0, per_feature(1), ALU.add))
            link(v.tensor_tensor(tmp0, tmp0, y[:, :, :], ALU.add))
            link(v.tensor_tensor(xs[:, :, :], xs[:, :, :], tmp0, ALU.add))

            center(xs)
            link(norm_relu())
            root_of(cnt[:, :], ALU.add, 1.0, rd[:, 0, :])
            v.memset(small[:, 0, 0:1], 0.0).then_inc(PJ[2]["ready"], 1)
            proj_dve(dve, 2)
            dve.wait_ge(PJ[2]["ev"], NR)
            v.tensor_tensor(y[:, :, :], y[:, :, :], per_node(rd[:, 0, :]), ALU.mult).then_inc(s_stage, 1)
            s = L[1]
            zero_acc(dve, 1, D)
            one_hot(dve, 1, 0, 0, True)
            with dve.Fori(0, ROUNDS) as i:
                for k in range(R):
                    dve.wait_ge(s["agg"], i * R + k + 2)
                    one_hot(dve, 1, i, k + 1, True)
                    places = load_tiles(dve, i * R + k - 1)
                    accumulate(dve, 1, i * R + k, k, 1, places, D)
            a0 = edge_sums(1, 1, D)
            dve.wait_ge(s_hist, 1)
            link(v.tensor_copy(outdeg[:, :], ps[:, 6, 0:TILES]))
            link(v.tensor_tensor(tmp0, a0, y[:, :, :], ALU.add))
            link(v.tensor_tensor(tmp0, tmp0, per_node(rd[:, 0, :]), ALU.mult))
            link(v.tensor_tensor(tmp0, tmp0, per_feature(2), ALU.add))
            link(v.scalar_tensor_tensor(xs[:, :, :], tmp0, 0.0, xs[:, :, :], ALU.max, ALU.add))

            center(xs)
            norm_relu().then_inc(PJ[3]["ready"], 1)
            proj_dve(dve, 3)
            s = L[2]
            zero_acc(dve, 2, D)
            zero_group(dve, 2)
            one_hot(dve, 2, 0, 0)
            with dve.Fori(0, ROUNDS) as i:
                for k in range(R):
                    g, b = i * R + k, k % 2
                    dve.wait_ge(s["agg"], g + 2)
                    one_hot(dve, 2, i, k + 1)
                    places = load_tiles(dve, g - 2)
                    dve.wait_ge(s["agg"], g + 3)
                    dve.wait_ge(s["land"][k], (i + 1) * 16 * U)
                    dve.wait_ge(s["qe"], g + 1)
                    v.tensor_tensor(prod[:, b, :].rearrange("p (u d) -> p u d", d=D), ps[:, 2 + b, 0:U * D].rearrange("p (u d) -> p u d", d=D),
                                    gat[:, k, :, 0:D], ALU.add).then_inc(s["used"], 1)
                    accumulate(dve, 2, g, k, 2, places, D)
            a0 = edge_sums(2, 2, D)
            v.tensor_copy(y[:, :, :], a0).then_inc(PJ[5]["ready"], 1)
            proj_dve(dve, 5)
            dve.wait_ge(PJ[5]["ev"], NR)
            link(v.tensor_tensor(tmp1, per_node(cnt[:, :]), per_feature(3), ALU.mult))
            v.tensor_tensor(y[:, :, :], tmp0, tmp1, ALU.add).then_inc(PJ[4]["ready"], 1)
            proj_dve(dve, 4)
            dve.wait_ge(PJ[4]["ev"], NR)
            gates = flat[:, 0:TILES * 4 * D].rearrange("p (t c) -> p t c", c=4 * D)
            r, z, n_in, n_h = (gates[:, :, n * D:(n + 1) * D] for n in range(4))
            v.memset(small[:, 0, 0:1], 0.0).then_inc(s_gates, 1)
            dve.wait_ge(s_gact, 1)
            link(v.tensor_tensor(n_h, n_h, r, ALU.mult))
            v.tensor_tensor(n_in, n_in, n_h, ALU.add).then_inc(s_gates, 1)
            dve.wait_ge(s_gact, 2)
            link(v.tensor_tensor(tmp0, h[:, :, :], n_in, ALU.subtract))
            link(v.tensor_tensor(tmp0, tmp0, z, ALU.mult))
            link(v.tensor_tensor(tmp0, tmp0, n_in, ALU.add))
            link(v.tensor_tensor(xs[:, :, :], xs[:, :, :], tmp0, ALU.add))

            center(xs)
            link(norm_relu())
            root_of(outdeg[:, :], ALU.max, 1.0, rd[:, 1, :])
            root_of(cnt[:, :], ALU.max, 1.0, rd[:, 2, :])
            v.tensor_tensor(tmp0, h[:, :, :], per_node(rd[:, 1, :]), ALU.mult).then_inc(s_stage, 1)
            s = L[3]
            zero_acc(dve, 3, D)
            one_hot(dve, 3, 0, 0)
            with dve.Fori(0, ROUNDS) as i:
                for k in range(R):
                    dve.wait_ge(s["agg"], i * R + k + 2)
                    one_hot(dve, 3, i, k + 1)
                    places = load_tiles(dve, i * R + k - 1)
                    accumulate(dve, 3, i * R + k, k, 1, places, D)
            a0 = edge_sums(3, 1, D)
            link(v.tensor_tensor(tmp0, a0, per_node(rd[:, 2, :]), ALU.mult))
            v.tensor_tensor(xs[:, :, :], xs[:, :, :], tmp0, ALU.add).then_inc(s_fin, 1)


_L0 = ["Wq", "bq", "Wk", "bk", "Wv", "bv", "Wo", "bo", "Wf", "bf", "gamma", "beta"]


def kernel(**inputs):
    import numpy as _np
    import concourse.bacc as _bacc
    from concourse import mybir as _mybir
    from concourse.bass_utils import run_bass_kernel_spmd as _run

    arrays = {n: inputs[n] for n in ("x", "src", "dst", "edge_attr_32")}
    arrays |= {n: inputs["L0_gnn_" + n] for n in _L0}
    arrays |= {"W_gcn": inputs["L1_gnn_W"], "b_gcn": inputs["L1_gnn_b"]}
    for n in ("W1", "b1", "W2", "b2", "w_ih", "w_hh", "b_ih", "b_hh"):
        a = _np.asarray(inputs["L2_gnn_" + n])
        arrays["e_" + n] = a.T if a.ndim == 2 else a
    order = ["x", "src", "dst", "edge_attr_32", *_L0, "W_gcn", "b_gcn", "e_W1", "e_b1", "e_W2", "e_b2", "e_w_ih", "e_w_hh", "e_b_ih", "e_b_hh"]
    nc = _bacc.Bacc("TRN2", target_bir_lowering=False, num_devices=1)
    given, args = {}, []
    for n in order:
        a = _np.ascontiguousarray(arrays[n])
        given[f"in_{n}"] = a
        args.append(nc.dram_tensor(f"in_{n}", a.shape, _mybir.dt.from_np(a.dtype), kind="ExternalInput").ap())
    args.append(nc.dram_tensor("out_0", (NODES, D), F32, kind="ExternalOutput").ap())
    build_gnn(nc, *args)
    r = _run(nc, [given], core_ids=[0])
    return r.results[0]["out_0"]
```

```python
from contextlib import ExitStack

import concourse.bass as bass
from concourse import mybir

ALU = mybir.AluOpType
ACT = mybir.ActivationFunctionType
AX = mybir.AxisListType
F32 = mybir.dt.float32
BF16 = mybir.dt.bfloat16
I32 = mybir.dt.int32

P = 128
NODES, EDGES, D, DE = 6250, 200000, 64, 32
HEADS, DH = 4, 16
TILES = -(-NODES // P)
NPAD = TILES * P
FULL = NODES // P
REST = NODES - FULL * P
CHUNKS = -(-EDGES // P)
EPAD = CHUNKS * P
U = 4
R = 4
STEPS = -(-(CHUNKS + TILES - 1) // (U * R)) * U * R
ROUNDS = STEPS // (U * R)
SB = -(-(STEPS + U * R) // P)
SPAD = SB * P
NTAB = 4 * -(-SB // 4)
N_WEIGHTS = 29
GT = 7
NR = TILES // GT
PARTS = ((0, 4), (4, NR))
PART_TILES = [slice(a * GT, b * GT) for a, b in PARTS]
LAG = TILES - 1
W0 = D + HEADS + 1
SCALE = float(D) ** -0.5
CLIP = 5.0 / SCALE
EPS = 1e-5
BIG = 1 << 16
OUTSIDE = 1000.0
TILE_BITS, CHUNK_BITS = 64, 2048
OROWS = 125
OLEN = EDGES // OROWS
assert OROWS * OLEN == EDGES and OLEN <= TILES * W0
assert TILES % GT == 0 and TILES <= TILE_BITS and CHUNKS <= CHUNK_BITS and REST > 0


def build_gnn(nc, x, src, dst, attr, wq, bq, wk, bk, wv, bv, wo, bo, wf, bf, gamma, beta,
              w_gcn, b_gcn, w1t, b1, w2, b2, wiht, whht, bih, bhh, out):
    with ExitStack() as ctx:
        def sb(name, shape, dt=F32):
            return ctx.enter_context(nc.sbuf_tensor(name, shape, dt))

        def sem(name):
            return ctx.enter_context(nc.semaphore(name))

        def dram(name, shape, dt=F32):
            return nc.dram_tensor(name, shape, dt).ap()

        dst_s, src_s, attr_s = dram("dst_s", [EPAD], I32), dram("src_s", [EPAD], I32), dram("attr_s", [EPAD, DE])
        kv_rows = dram("kv_rows", [NPAD, 2 * D])
        rows = [dram(f"rows{n}", [NPAD, D]) for n in range(3)]
        counts = dram("counts", [NPAD + P])
        tiles_d, chunks_d = dram("tiles_d", [SPAD // U], I32), dram("chunks_d", [SPAD // 2], I32)

        xs = sb("xs", [P, TILES, D])
        h = sb("h", [P, TILES, D])
        q = sb("q", [P, TILES, D])
        y = sb("y", [P, TILES, D])
        stage = sb("stage", [P, 2, TILES * D])
        acc = sb("acc", [P, U, TILES * W0])
        cnt = sb("cnt", [P, TILES])
        outdeg = sb("outdeg", [P, TILES])
        small = sb("small", [P, 4, TILES])
        rd = sb("rd", [P, 3, TILES])
        z1 = sb("z1", [P, TILES, HEADS])
        dloc = sb("dloc", [P, SPAD])
        sidx = sb("sidx", [P, SPAD], I32)
        slo, shi = sb("slo", [P, SPAD]), sb("shi", [P, SPAD])
        tpk = sb("tpk", [1, 2 + SPAD // U], I32)
        cpk = sb("cpk", [1, SPAD // 2], I32)
        idx = sb("idx", [P, R, U], I32)
        gat = sb("gat", [P, R, U, 2 * D])
        oh = sb("oh", [P, R, U, P])
        oht = sb("oht", [P, 2, U, P])
        msg = sb("msg", [P, 2, U, W0])
        prod = sb("prod", [P, 2, U * D])
        sc = sb("sc", [P, 2, 2, U * HEADS])
        att = sb("att", [P, R, U, DE])
        attT = sb("attT", [P, 2, P])
        olo = oht[:, :, :, :].rearrange("p a u n -> p (a u n)").bitcast(BF16).rearrange("p (k u n) -> p k u n", k=R, u=U)
        ohi = prod[:, :, :].rearrange("p a n -> p (a n)").bitcast(BF16)[:, 0:R * U * TILES].rearrange("p (k u n) -> p k u n", k=R, u=U)
        tiles_at = lambda at, width: gat[:, :, :, :].rearrange("p k u d -> p (k u d)")[:, at:at + GT * width].rearrange("p (t d) -> p t d", d=width)
        hb, hb_sums = tiles_at(0, D), tiles_at(GT * D, D + 2)
        hT = sb("hT", [D + 2, 2, GT * P])
        ident = sb("ident", [P, P])
        iota_i, iota = sb("iota_i", [P, P], I32), sb("iota", [P, P])
        step_i, step = sb("step_i", [P, SB], I32), sb("step", [P, SB])
        zeros = sb("zeros", [P, U * W0])
        zerob = sb("zerob", [P, P], BF16)
        ones = sb("ones", [1, P])
        padi = sb("padi", [1, 2, P], I32)
        w_kvqf = sb("w_kvqf", [D + 1, 4 * D])
        w_o, w_g = sb("w_o", [D + 1, D]), sb("w_g", [D + 1, D])
        w_pq, w_h = sb("w_pq", [D + 1, 2 * D]), sb("w_h", [D + 1, 4 * D])
        w_2, w_i, w_s = sb("w_2", [D, D + 1]), sb("w_i", [D, 3 * D]), sb("w_s", [D + 2, 3 * D])
        w_e = sb("w_e", [P, U * D])
        brow, bc = sb("brow", [1, 3 * D]), sb("bc", [P, 3 * D])
        CW = CHUNKS
        flat = acc[:, :, :].rearrange("p u n -> p (u n)")
        WIN = LAG + P
        off_p, w_p = (flat[:, n * (P + SPAD):(n + 1) * (P + SPAD)] for n in range(2))
        at_mask = 2 * (P + SPAD)
        mask = flat[:, at_mask:at_mask + SB * WIN].rearrange("p (j e) -> p j e", e=WIN)
        at_rows = at_mask + SB * WIN
        crow = flat[0:1, at_rows:at_rows + 4 * CW].rearrange("p (a n) -> p a n", a=4)
        crow_i = h[0:1, :, :].rearrange("p t d -> p (t d)")[:, 0:2 * CW].bitcast(I32).rearrange("p (a n) -> p a n", a=2)
        chunk_no = q[0:1, :, :].rearrange("p t d -> p (t d)")[:, 0:CW]
        cs = sb("cs", [P, 6, SB])
        cs_i = sb("cs_i", [P, SB], I32)
        packf = prod[0:SB, :, :].rearrange("p a n -> p (a n)")[:, 0:3 * P].rearrange("p (a n) -> p a n", a=3)
        pack_i = attT[0:SB, 0, :].bitcast(I32)
        df, sf, lof, hif, vf, sraw = (flat[:, n * SPAD:(n + 1) * SPAD] for n in range(6))
        dg, sg, lo_i, hi_i = (a.bitcast(I32) for a in (df, sraw, lof, hif))

        order_i = acc[0:OROWS, 0:1, 0:OLEN].rearrange("p u n -> p (u n)").bitcast(I32)
        next_i = acc[0:OROWS, 1:2, 0:1].rearrange("p u n -> p (u n)").bitcast(I32)
        falls = acc[0:OROWS, 2:3, 0:OLEN].rearrange("p u n -> p (u n)")
        fell = sb("fell", [P, 1])
        unsorted = sb("unsorted", [1, 1], I32)
        cell = lambda n: acc[:, 3, n:n + 1]
        key_i, src_i, idx_i, pos_i = (cell(n).bitcast(I32) for n in range(4))
        key, seen, total, rank, fresh, last, spare = (cell(n) for n in range(4, 11))
        keys_i = acc[:, 3, P:2 * P].bitcast(I32)
        keys, same, before, below = (acc[:, 3, n * P:(n + 1) * P] for n in range(2, 6))
        attr_c = acc[:, 3, 6 * P:6 * P + DE]
        ranks = y[:, :, :].rearrange("p t d -> p (t d)")[:, 0:CHUNKS]
        count_row = stage[0:1, :, :].rearrange("p a n -> p (a n)")
        start_row = acc[0:1, 0:2, :].rearrange("p u n -> p (u n)")[:, 0:NPAD]

        ps = ctx.enter_context(nc.psum_tensor("ps", [P, 8, 512], F32))

        s_order, s_fell, s_fellt, s_flag = sem("order_loaded"), sem("falls_found"), sem("falls_turned"), sem("order_known")
        s_tri, s_low = sem("ones_for_below"), sem("below_ready")
        S1 = dict(load=sem("count_loaded"), seen=sem("count_seen"), idx=sem("count_index"), new=sem("count_new"),
                  put=sem("count_stored"), row=sem("counts_in_a_row"), scan=sem("starts_ready"),
                  chain=sem("count_chain"), scanned=sem("start_chain"))
        S2 = dict(load=sem("place_loaded"), seen=sem("place_start"), pos=sem("place_ready"), put=[sem(f"edge_placed{n}") for n in range(3)], more=sem("place_rest_loaded"))
        s_x, s_w, s_copy, s_pad = sem("x_loaded"), sem("weights_loaded"), sem("edges_copied"), sem("edges_padded")
        s_acopy = sem("attributes_copied_and_padded")
        s_ends, s_ends2 = sem("chunk_ends_loaded"), sem("sorted_chunk_ends_loaded")
        s_pool = sem("pool_constants")
        s_const = sem("constants_ready")
        s_rows = sem("rows_ready")
        s_bc = sem("broadcast_done")
        s_bcc = sem("table_block_copied")
        s_bcs = sem("broadcast_rows_copied")
        s_half, s_free = sem("half_of_sums_zeroed"), sem("gates_used")
        s_cidx = sem("chunk_numbers_ready")
        s_eg = sem("edge_rows_landed")
        s_eg2 = sem("source_rows_landed")
        s_tabs = sem("tables_ready_by_step")
        s_tabt = sem("table_block_turned")
        s_packt, s_packed, s_packd, s_packl = sem("steps_turned"), sem("steps_packed"), sem("packed_stored"), sem("packed_loaded")
        s_d = sem("vector_chain")
        s_var, s_sd = sem("variances_ready"), sem("deviations_ready")
        s_stage, s_table = sem("table_staged"), sem("table_stored")
        s_gates, s_gact = sem("gates_ready"), sem("gates_done")
        s_hist = sem("sources_counted")
        s_fin, s_out = sem("result_ready"), sem("result_stored")

        NPROD = 5
        PJ = [dict(ready=sem(f"proj{n}_input"), hb=sem(f"proj{n}_staged"), tr=sem(f"proj{n}_turned"),
                   ht=sem(f"proj{n}_turned_copied"), mm=sem(f"proj{n}_product"), ev=sem(f"proj{n}_taken"))
              for n in range(NPROD)]
        sums = dict(idx="indices", oh="onehot", agg="summed", acc="accumulated")
        turned = dict(t="onehot_turned", oht="turned_copied", qe="dst_rows", exp="act", used="rows_used", clip="before_act")
        attention = dict(prod="combined", red="reduced")
        L = [dict({key: sem(f"l{n}_{name}") for key, name in names.items()}, land=[sem(f"l{n}_landed{k}") for k in range(R)])
             for n, names in enumerate((sums | turned | attention, sums, sums | turned, sums))]
        s_att = [sem(f"attr_landed{k}") for k in range(R)]
        s_atc = sem("attr_turned")

        block = ctx.enter_context(nc.Block())

        def proj_specs():
            flats = stage[:, :, :].rearrange("p a n -> p (a n)")
            kv = flats.rearrange("p (t c) -> p t c", c=2 * D)
            gates = flat[:, 0:TILES * 4 * D].rearrange("p (t c) -> p t c", c=4 * D)
            pst = stage[:, 0, :].rearrange("p (t c) -> p t c", c=D)
            one = lambda a, w, width: [(a, hb, D, D + 1, w, [(0, width, True, True)])]
            both = [(y, hb_sums, D + 2, D + 2, w_s, [(0, 3 * D, True, False)]),
                    (h, hb, D, D + 1, w_h, [(0, 2 * D, False, True), (3 * D, 4 * D, False, True)])]
            return [
                (one(h, w_kvqf, 4 * D), 4 * D, [(0, 2 * D, kv), (2 * D, 3 * D, q), (3 * D, 4 * D, y)]),
                (one(h, w_o, D), D, [(0, D, pst)]),
                (one(h, w_g, D), D, [(0, D, y)]),
                (one(h, w_pq, 2 * D), 2 * D, [(0, D, pst), (D, 2 * D, q)]),
                (both, 4 * D, [(0, 4 * D, gates)]),
            ]

        SPEC = proj_specs()
        outp = ps[:, 2:6, :].rearrange("p b (j c) -> p (b j) c", c=4 * D)

        def wait_last(eng, semaphore, count):
            if not isinstance(count, int) or count > 0:
                eng.wait_ge(semaphore, count)

        def round_tiles(a, i):
            return a[:, bass.ds(i * GT, GT), :]

        def proj_pe(pe, n, part):
            s, srcs = PJ[n], SPEC[n][0]
            M = len(srcs)
            with pe.Fori(*PARTS[part]) as i:
                for m, (_, to, width, _, _, _) in enumerate(srcs):
                    staged, copied = pe.to_reg(i * M + m + 1), pe.to_reg(i * M + m)
                    pe.wait_ge(s_pool, 2)
                    pe.wait_ge(s["hb"], staged)
                    if m > 0:
                        pe.wait_ge(s["ht"], copied)
                    for t in range(GT):
                        mm = nc.tensor.transpose(ps[0:width, t // 4, (t % 4) * P:(t % 4 + 1) * P], to[:, t, :], ident[:, :])
                    mm.then_inc(s["tr"], 1)
                pe.wait_ge(s["ht"], (i + 1) * M)
                for t in range(GT):
                    for m, (_, _, _, k, w, spans) in enumerate(srcs):
                        for a, b, start, stop in spans:
                            mm = nc.tensor.matmul(outp[:, t, a:b], hT[0:k, m, t * P:(t + 1) * P], w[:, a:b],
                                                  start=start, stop=stop, skip_group_check=M > 1)
                mm.then_inc(s["mm"], 1)

        def proj_act(act, n, part):
            s, srcs, _, dests = PJ[n], *SPEC[n]
            M = len(srcs)

            def stage_tiles(i):
                for a, to, width, _, _, _ in srcs:
                    if width > D:
                        nc.scalar.copy(to[:, :, D:D + 1], cnt[:, bass.ds(i * GT, GT)].unsqueeze(2))
                    nc.scalar.copy(to[:, :, 0:D], round_tiles(a, i)).then_inc(s["hb"], 1)

            def body(i, more):
                for m, (_, _, width, _, _, _) in enumerate(srcs):
                    act.wait_ge(s["tr"], i * M + m + 1)
                    nc.scalar.copy(hT[0:width, m, 0:4 * P], ps[0:width, 0, :])
                    nc.scalar.copy(hT[0:width, m, 4 * P:GT * P], ps[0:width, 1, 0:(GT - 4) * P]).then_inc(s["ht"], 1)
                if more:
                    stage_tiles(i + 1)
                act.wait_ge(s["mm"], i + 1)
                if M > 1:
                    act.wait_ge(s["ready"], 2)
                for a, b, to in dests:
                    ins = nc.scalar.copy(round_tiles(to, i)[:, :, 0:b - a], outp[:, 0:GT, a:b])
                ins.then_inc(s["ev"], 1)

            first, end = PARTS[part]
            act.wait_ge(s["ready"], part + 1)
            stage_tiles(first)
            with act.Fori(first, end - 1) as i:
                body(i, True)
            body(end - 1, False)

        def edge_pool(pool, n, table, width, free):
            s = L[n]
            with pool.Fori(0, ROUNDS) as i:
                for k in range(R):
                    count = pool.to_reg(i * R + k + 1)
                    pool.wait_ge(s_table, 32 * (n + 1))
                    pool.wait_ge(s[free], count)
                    pool.wait_ge(s["idx"], count)
                    for u in range(U):
                        nc.gpsimd.indirect_dma_start(
                            gat[:, k, u, 0:width], None, table,
                            bass.IndirectOffsetOnAxis(ap=idx[:, k, u:u + 1], axis=0)).then_inc(s["land"][k], 16)

        def first_indices(act, n):
            act.wait_ge(s_bcc, NTAB // 4)
            for k in range(R):
                nc.scalar.copy(idx[:, k, :], sidx[:, k * U:(k + 1) * U]).then_inc(L[n]["idx"], 1)

        def next_indices(act, n, i, k):
            act.wait_ge(L[n]["land"][k], (i + 1) * 16 * U)
            act.wait_ge(s_bcc, NTAB)
            nc.scalar.copy(idx[:, k, :], sidx[:, bass.ds((i * R + k + R) * U, U)]).then_inc(L[n]["idx"], 1)

        def one_hot(dve, n, i, k, extra=False):
            kk = k % R
            at = (i * R + k) * U
            ins = nc.vector.tensor_tensor(
                oh[:, kk, :, :], iota[:, :].unsqueeze(1).to_broadcast([P, U, P]),
                dloc[:, bass.ds(at, U)].unsqueeze(2).to_broadcast([P, U, P]), ALU.is_equal)
            if extra:
                nc.vector.tensor_tensor(
                    olo[:, kk, :, :], iota[:, :].unsqueeze(1).to_broadcast([P, U, P]),
                    slo[:, bass.ds(at, U)].unsqueeze(2).to_broadcast([P, U, P]), ALU.is_equal)
                ins = nc.vector.tensor_tensor(
                    ohi[:, kk, :, :], iota[:, 0:TILES].unsqueeze(1).to_broadcast([P, U, TILES]),
                    shi[:, bass.ds(at, U)].unsqueeze(2).to_broadcast([P, U, TILES]), ALU.is_equal)
            ins.then_inc(L[n]["oh"], 1)

        def tile_of(eng, packed, u):
            return nc.s_assert_within(eng.snap((packed >> (6 * u)) & (TILE_BITS - 1)), 0, TILES - 1,
                                      skip_runtime_bounds_check_because="tiles are clamped where they are packed")

        def load_tiles(eng, g):
            packed = eng.value_load(tpk[0:1, bass.ds(g + 2, 1)])
            return [tile_of(eng, packed, u) for u in range(U)]

        def accumulate(dve, n, g, k, lag, places, width, us=range(U)):
            s, bank = L[n], (k + lag) % 2
            if us[0] == 0:
                dve.wait_ge(s["agg"], g + R + 1 - lag)
                dve.wait_ge(s["acc"], g + 1)
            for u in us:
                a = acc[:, u, bass.ds(places[u] * width, width)]
                ins = nc.vector.tensor_tensor(a, a, ps[:, 4 + bank, u * width:(u + 1) * width], ALU.add)
            if us[-1] == U - 1:
                ins.then_inc(s["acc"], 1)

        def zero_acc(dve, n, width, us=U):
            nc.vector.memset(acc[:, 0:us, 0:TILES * width], 0.0).then_inc(L[n]["acc"], 1)

        def zero_acc_act(act, us, width):
            return nc.scalar.copy(acc[:, us, 0:TILES * width], zeros[:, 0:1].unsqueeze(2).to_broadcast([P, us.stop - us.start, TILES * width]))

        def zero_sums(pe, n, lag, width):
            pe.wait_ge(L[n]["acc"], 1)
            nc.tensor.matmul(ps[:, 4 + lag % 2, 0:U * width], zeros[:, 0:P], zeros[:, 0:U * width],
                             start=True, stop=True).then_inc(L[n]["agg"], R + 1 - lag)

        def zero_group(dve, n):
            s = L[n]
            nc.vector.memset(oh[:, R - 1, :, :], 0.0)
            if n == 0:
                nc.vector.memset(gat[:, R - 1, :, :], 0.0)
            nc.vector.memset(msg[:, 1, :, 0:W0 - 1], 0.0).then_inc(s["exp"], 1)
            nc.vector.memset(small[:, 0, 0:1], 0.0).then_inc(s["used"], R - 1 if n == 0 else R)

        def sum_edges(pe, n, g, k, width, rhs):
            pe.wait_ge(L[n]["acc"], g + 1)
            for u in range(U):
                mm = nc.tensor.matmul(ps[:, 4 + k % 2, u * width:(u + 1) * width], oh[:, k, u, :], rhs(u),
                                      start=True, stop=True)
            return mm

        def sum_messages(pe, n, g, k1, width):
            s = L[n]
            if n == 0:
                pe.wait_ge(s["used"], g + R)
            else:
                pe.wait_ge(s["exp"], g + 1)
            sum_edges(pe, n, g, k1, width, lambda u: msg[:, k1 % 2, u, 0:width]).then_inc(s["agg"], 1)

        def turn_onehot(pe, n, at, kk, b):
            for u in range(U):
                mm = nc.tensor.transpose(ps[:, b, u * P:(u + 1) * P], oh[:, kk, u, :], ident[:, :])
            mm.then_inc(L[n]["t"], 1)

        def dst_rows(pe, n, i, k, first):
            b = k % 2
            places = load_tiles(pe, i * R + k)
            pe.wait_ge(L[n]["oht"], i * R + k + 1)
            if first is not None:
                first()
            qf = q[:, :, :].rearrange("p t d -> p (t d)")
            for u in range(U):
                mm = nc.tensor.matmul(ps[:, 2 + b, u * D:(u + 1) * D], oht[:, b, u, :],
                                      qf[:, bass.ds(places[u] * D, D)], start=first is None, stop=True,
                                      skip_group_check=True)
            mm.then_inc(L[n]["qe"], 1)

        col = lambda a: a.rearrange("(p o) -> p o", o=1)
        WHOLE = EDGES // P
        LEFT = EDGES - WHOLE * P

        def chunks_of(eng, body):
            body(0, P)
            with eng.Fori(1, WHOLE) as c:
                body(c, P)
            if LEFT:
                body(WHOLE, LEFT)

        def sort_sp(sp):
            def count(c, n):
                wait_last(sp, S1["put"], c * 16)
                sp.dma_start(key_i[0:n, :], col(dst[bass.ds(c * P, n)]), allow_slow_non_contiguous=True).then_inc(S1["load"], 16)
                sp.dma_start(keys_i[0:n, 0:n], dst[bass.ds(c * P, n)].rearrange("(o a) -> o a", o=1).to_broadcast([n, n])).then_inc(S1["load"], 16)

            sp.dma_start(counts.rearrange("(a b) -> a b", b=P), zeros[0:TILES + 1, 0:P]).then_inc(S1["row"], 16)
            sp.wait_ge(S1["row"], 16)
            chunks_of(sp, count)
            sp.wait_ge(S1["put"], 16 * CHUNKS)
            sp.dma_start(count_row, counts[0:NPAD].rearrange("(o a) -> o a", o=1)).then_inc(S1["row"], 16)
            sp.wait_ge(S1["scan"], 1)
            sp.dma_start(counts[0:NPAD].rearrange("(o a) -> o a", o=1), start_row).then_inc(S1["row"], 16)
            sp.wait_ge(S1["row"], 48)
            sp.wait_ge(s_copy, 32)
            sp.wait_ge(s_acopy, 32)

            def place(c, n):
                for put in S2["put"]:
                    wait_last(sp, put, c * 16)
                sp.dma_start(key_i[0:n, :], col(dst[bass.ds(c * P, n)]), allow_slow_non_contiguous=True).then_inc(S2["load"], 16)
                sp.dma_start(src_i[0:n, :], col(src[bass.ds(c * P, n)]), allow_slow_non_contiguous=True).then_inc(S2["more"], 16)
                sp.dma_start(attr_c[0:n, :], attr[bass.ds(c * P, n), :]).then_inc(S2["more"], 16)

            chunks_of(sp, place)
            for put in S2["put"]:
                sp.wait_ge(put, 16 * CHUNKS)
            sp.dma_start(crow_i[0:1, 0, :], dst_s.rearrange("(o a) -> o a", o=1)[:, 0:EDGES:P], allow_slow_non_contiguous=True).then_inc(s_ends2, 16)
            sp.dma_start(crow_i[0:1, 1, 0:CHUNKS - 1], dst_s.rearrange("(o a) -> o a", o=1)[:, P - 1:EDGES:P], allow_slow_non_contiguous=True).then_inc(s_ends2, 16)
            sp.dma_start(crow_i[0:1, 1, CHUNKS - 1:CHUNKS], dst_s[EDGES - 1:EDGES].rearrange("(o a) -> o a", o=1)).then_inc(s_ends2, 16)

        def sort_pool(pool):
            row = lambda a: a.rearrange("(n o) -> n o", o=1)
            at = lambda a: bass.IndirectOffsetOnAxis(ap=a, axis=0)

            def after(semaphore, count):
                count = count if isinstance(count, int) else pool.to_reg(count)
                pool.wait_ge(s_pool, 5)
                pool.wait_ge(semaphore, count)

            def count(c, n):
                after(S1["load"], (c + 1) * 32)
                nc.gpsimd.indirect_dma_start(seen[0:n, :], None, row(counts), at(key_i[0:n, :])).then_inc(S1["seen"], 16)
                after(S1["new"], c + 1)
                nc.gpsimd.indirect_dma_start(row(counts), at(idx_i[0:n, :]), fresh[0:n, :], None).then_inc(S1["put"], 16)

            def place(c, n):
                after(S2["load"], (c + 1) * 16)
                nc.gpsimd.indirect_dma_start(seen[0:n, :], None, row(counts), at(key_i[0:n, :])).then_inc(S2["seen"], 16)
                after(S2["more"], (c + 1) * 32)
                pool.wait_ge(S2["pos"], c + 1)
                for put, to, of in zip(S2["put"], (row(dst_s), row(src_s), attr_s), (key_i, src_i, attr_c)):
                    nc.gpsimd.indirect_dma_start(to, at(pos_i[0:n, :]), of[0:n, :], None).then_inc(put, 16)

            pool.wait_ge(s_tri, 1)
            nc.gpsimd.affine_select(out=below, in_=below, compare_op=ALU.is_gt, fill=0.0, base=0,
                                    pattern=[[-1, P]], channel_multiplier=1).then_inc(s_low, 1)
            chunks_of(pool, count)
            chunks_of(pool, place)
            for put in S2["put"]:
                pool.wait_ge(put, 16 * CHUNKS)

        def sort_dve(dve):
            v = nc.vector
            LINKS = 8

            def count(c, n):
                done = [0]

                def link(ins):
                    done[0] += 1
                    ins.then_inc(S1["chain"], 1)
                    dve.wait_ge(S1["chain"], c * LINKS + done[0])

                dve.wait_ge(S1["load"], (c + 1) * 32)
                v.tensor_copy(key[0:n, :], key_i[0:n, :])
                link(v.tensor_copy(keys[0:n, 0:n], keys_i[0:n, 0:n]))
                link(v.tensor_scalar(same[0:n, 0:n], keys[0:n, 0:n], key[0:n, :], None, ALU.is_equal))
                link(v.tensor_tensor(before[0:n, 0:n], same[0:n, 0:n], below[0:n, 0:n], ALU.mult))
                v.tensor_reduce(total[0:n, :], same[0:n, 0:n], AX.X, ALU.add)
                link(v.tensor_reduce(rank[0:n, :], before[0:n, 0:n], AX.X, ALU.add))
                link(v.scalar_tensor_tensor(last[0:n, :], rank[0:n, :], 1.0, total[0:n, :], ALU.add, ALU.is_equal))
                link(v.tensor_tensor(key[0:n, :], key[0:n, :], spare[0:n, :], ALU.subtract))
                link(v.tensor_tensor(key[0:n, :], key[0:n, :], last[0:n, :], ALU.mult))
                link(v.tensor_tensor(idx_i[0:n, :], key[0:n, :], spare[0:n, :], ALU.add))
                assert done[0] == LINKS
                dve.wait_ge(S1["seen"], (c + 1) * 16)
                v.tensor_tensor(ranks[0:n, bass.ds(c, 1)], rank[0:n, :], seen[0:n, :], ALU.add)
                v.tensor_tensor(fresh[0:n, :], total[0:n, :], seen[0:n, :], ALU.add).then_inc(S1["new"], 1)

            def place(c, n):
                dve.wait_ge(S2["seen"], (c + 1) * 16)
                v.tensor_tensor(pos_i[0:n, :], ranks[0:n, bass.ds(c, 1)], seen[0:n, :], ALU.add).then_inc(S2["pos"], 1)

            done = [0]

            def link(ins):
                done[0] += 1
                ins.then_inc(S1["scanned"], 1)
                dve.wait_ge(S1["scanned"], done[0])

            v.memset(below, 1.0).then_inc(s_tri, 1)
            link(v.tensor_scalar(spare, step[:, 0:1], float(NPAD), None, ALU.add))
            dve.wait_ge(s_low, 1)
            chunks_of(dve, count)
            dve.wait_ge(S1["row"], 32)
            zrow = h[0:1, :, :].rearrange("p t d -> p (t d)")
            link(v.memset(zrow, 0.0))
            half = TILES * D
            for m in range(2):
                part = slice(m * half, (m + 1) * half)
                link(v.tensor_tensor_scan(start_row[:, part], count_row[:, part], zrow, 0.0 if m == 0 else start_row[:, half - 1:half],
                                          ALU.add, ALU.add))
            v.tensor_tensor(start_row, start_row, count_row, ALU.subtract).then_inc(S1["scan"], 1)
            dve.wait_ge(S1["scan"], 1)
            chunks_of(dve, place)
            dve.wait_ge(s_ends2, 48)

        @block.sync
        def _(sp):
            sp.wait_ge(s_const, 1)
            sp.dma_start(crow_i[0:1, 0, :], dst.rearrange("(a o) -> o a", a=EDGES)[:, 0:EDGES:P], allow_slow_non_contiguous=True).then_inc(s_ends, 16)
            sp.dma_start(crow_i[0:1, 1, 0:CHUNKS - 1], dst.rearrange("(a o) -> o a", a=EDGES)[:, P - 1:EDGES:P], allow_slow_non_contiguous=True).then_inc(s_ends, 16)
            sp.dma_start(crow_i[0:1, 1, CHUNKS - 1:CHUNKS], dst[EDGES - 1:EDGES].rearrange("(o a) -> o a", o=1)).then_inc(s_ends, 16)
            sp.dma_start(order_i, dst.rearrange("(a b) -> a b", b=OLEN)).then_inc(s_order, 16)
            sp.dma_start(next_i[0:OROWS - 1, :], dst.rearrange("(a b) -> a b", b=OLEN)[1:OROWS, 0:1], allow_slow_non_contiguous=True).then_inc(s_order, 16)
            for t0, t1, r in ((0, FULL, P), (FULL, TILES, REST)):
                part = x[t0 * P:t0 * P + (t1 - t0 - 1) * P + r, :].rearrange("(t p) f -> p t f", p=r)
                sp.dma_start(xs[0:r, t0:t1, :], part).then_inc(s_x, 16)
            sp.dma_start(dst_s[0:EDGES].rearrange("(a b) -> a b", b=160), dst.rearrange("(a b) -> a b", b=160)).then_inc(s_copy, 16)
            sp.dma_start(src_s[0:EDGES].rearrange("(a b) -> a b", b=160), src.rearrange("(a b) -> a b", b=160)).then_inc(s_copy, 16)
            sp.dma_start(dst_s[EDGES:EPAD].rearrange("(o a) -> o a", o=1), padi[0:1, 0, 0:EPAD - EDGES]).then_inc(s_pad, 16)
            sp.dma_start(src_s[EDGES:EPAD].rearrange("(o a) -> o a", o=1), padi[0:1, 1, 0:EPAD - EDGES]).then_inc(s_pad, 16)
            wload = [(w_kvqf[0:D, 0:D], wk), (w_kvqf[0:D, D:2 * D], wv), (w_kvqf[0:D, 2 * D:3 * D], wq),
                     (w_kvqf[0:D, 3 * D:4 * D], wf), (w_o[0:D, :], wo), (w_g[0:D, :], w_gcn),
                     (w_pq[0:D, 0:D], w1t[0:D, :]), (w_pq[0:D, D:2 * D], w1t[D:2 * D, :]), (w_2[:, 0:D], w2),
                     (w_i[:, :], wiht), (w_h[0:D, 0:2 * D], whht[:, 0:2 * D]),
                     (w_h[0:D, 3 * D:4 * D], whht[:, 2 * D:3 * D])]
            row = lambda v: v.rearrange("(o a) -> o a", o=1)
            wload += [(w_kvqf[D:D + 1, 0:D], row(bk)), (w_kvqf[D:D + 1, D:2 * D], row(bv)),
                      (w_kvqf[D:D + 1, 2 * D:3 * D], row(bq)), (w_kvqf[D:D + 1, 3 * D:4 * D], row(bf)),
                      (w_o[D:D + 1, :], row(bo)), (w_pq[D:D + 1, 0:D], row(b1)), (w_s[D + 1:D + 2, :], row(bih)),
                      (w_h[D:D + 1, 0:2 * D], row(bhh[0:2 * D])), (w_h[D:D + 1, 3 * D:4 * D], row(bhh[2 * D:3 * D]))]
            wload += [(brow[0:1, n * D:(n + 1) * D], row(v)) for n, v in enumerate((gamma, beta, b_gcn))]
            wload += [(w_e[DE * u:DE * (u + 1), D * u:D * (u + 1)], w1t[2 * D:2 * D + DE, :]) for u in range(U)]
            for to, of in wload:
                sp.dma_start(to, of).then_inc(s_w, 16)
            sp.dma_start(w_2[:, D:D + 1], b2.rearrange("(a o) -> a o", o=1), allow_slow_non_contiguous=True).then_inc(s_w, 16)
            assert len(wload) + 1 == N_WEIGHTS
            sp.dma_start(attr_s[0:EDGES, :].rearrange("(a b) f -> a (b f)", b=125), attr.rearrange("(a b) f -> a (b f)", b=125)).then_inc(s_acopy, 16)
            sp.dma_start(attr_s[EDGES:EPAD, :], zeros[0:EPAD - EDGES, 0:DE]).then_inc(s_acopy, 16)
            sp.wait_ge(s_flag, 1)
            with sp.If(sp.value_load(unsorted[0:1, 0:1]) > 0):
                sort_sp(sp)
            sp.wait_ge(s_packed, 2)
            sp.dma_start(tiles_d.rearrange("(a b) -> a b", b=P // U), pack_i[:, 0:P // U]).then_inc(s_packd, 16)
            sp.dma_start(chunks_d.rearrange("(a b) -> a b", b=P // 2), pack_i[:, P // U:P // U + P // 2]).then_inc(s_packd, 16)
            sp.wait_ge(s_packd, 32)
            sp.dma_start(tpk[0:1, 2:2 + SPAD // U], tiles_d.rearrange("(o a) -> o a", o=1)).then_inc(s_packl, 16)
            sp.dma_start(cpk[:, :], chunks_d.rearrange("(o a) -> o a", o=1)).then_inc(s_packl, 16)
            def store_rows(table, of, part):
                tiles = PART_TILES[part]
                sp.dma_start(table.rearrange("(t p) f -> p t f", p=P)[:, tiles, :], of[:, tiles, :]).then_inc(s_table, 16)

            staged = stage[:, 0, :].rearrange("p (t f) -> p t f", f=D)
            kv = stage[:, :, :].rearrange("p a n -> p (a n)").rearrange("p (t f) -> p t f", f=2 * D)
            for part, (_, end) in enumerate(PARTS):
                sp.wait_ge(PJ[0]["ev"], end)
                store_rows(kv_rows, kv, part)
            for part in range(2):
                sp.wait_ge(s_stage, part + 1)
                store_rows(rows[0], y, part)
            for part, (_, end) in enumerate(PARTS):
                sp.wait_ge(PJ[3]["ev"], end)
                store_rows(rows[1], staged, part)
            sp.wait_ge(s_packl, 32)
            sp.wait_ge(s_acopy, 32)
            def load_attributes(g, k):
                sp.wait_ge(s_atc, g + 1)
                for half in range(U // 2):
                    at = g * (U // 2) + half
                    packed = sp.value_load(cpk[0:1, at:at + 1] if isinstance(at, int) else cpk[0:1, bass.ds(at, 1)])
                    for e in range(2):
                        c = nc.s_assert_within(sp.snap((packed >> (11 * e)) & (CHUNK_BITS - 1)), 0, CHUNKS - 1,
                                               skip_runtime_bounds_check_because="a count of chunks less one")
                        sp.dma_start(att[:, k, 2 * half + e, :], attr_s[bass.ds(c * P, P), :]).then_inc(s_att[k], 16)

            with sp.Fori(0, ROUNDS) as i:
                for k in range(R):
                    load_attributes(i * R + k, k)
            load_attributes(ROUNDS * R, 0)
            for part in range(2):
                sp.wait_ge(s_stage, part + 3)
                store_rows(rows[2], staged, part)
            cut = PART_TILES[1].start
            sp.wait_ge(s_fin, 1)
            sp.dma_start(out[0:cut * P, :].rearrange("(t p) f -> p t f", p=P), xs[:, 0:cut, :]).then_inc(s_out, 16)
            sp.wait_ge(s_fin, 2)
            sp.dma_start(out[cut * P:FULL * P, :].rearrange("(t p) f -> p t f", p=P), xs[:, cut:FULL, :]).then_inc(s_out, 16)
            sp.dma_start(out[FULL * P:NODES, :], xs[0:REST, FULL, :]).then_inc(s_out, 16)
            sp.wait_ge(s_out, 48)

        @block.gpsimd
        def _(pool):
            nc.gpsimd.memset(ident[:, :], 0.0).then_inc(s_pool, 1)
            pool.wait_ge(s_pool, 1)
            nc.gpsimd.affine_select(out=ident[:, :], in_=ident[:, :], compare_op=ALU.not_equal, fill=1.0, base=0,
                                    pattern=[[-1, P]], channel_multiplier=1).then_inc(s_pool, 1)
            nc.gpsimd.iota(iota_i[:, :], [[1, P]], base=0, channel_multiplier=0).then_inc(s_pool, 1)
            nc.gpsimd.iota(step_i[:, :], [[P, SB]], base=0, channel_multiplier=1).then_inc(s_pool, 1)
            nc.gpsimd.iota(chunk_no, [[1, CW]], base=0, channel_multiplier=0,
                           allow_small_or_imprecise_dtypes=True).then_inc(s_pool, 1)
            pool.wait_ge(s_flag, 1)
            with pool.If(pool.value_load(unsorted[0:1, 0:1]) > 0):
                sort_pool(pool)
            pool.wait_ge(s_copy, 32)
            pool.wait_ge(s_pad, 32)
            pool.wait_ge(s_cidx, 1)
            for j in range(SB):
                for to, of, landed in ((dg, dst_s, s_eg), (sg, src_s, s_eg2)):
                    nc.gpsimd.indirect_dma_start(
                        to[:, j * P:(j + 1) * P], None, of.rearrange("(c e) -> c e", e=P),
                        bass.IndirectOffsetOnAxis(ap=cs_i[:, j:j + 1], axis=0)).then_inc(landed, 16)
            edge_pool(pool, 0, kv_rows, 2 * D, "used")
            edge_pool(pool, 1, rows[0], D, "agg")
            edge_pool(pool, 2, rows[1], D, "used")
            edge_pool(pool, 3, rows[2], D, "agg")

        @block.scalar
        def _(act):
            roots = iter(range(12))

            def root(part):
                act.wait_ge(s_var, next(roots) + 1)
                nc.scalar.activation(small[:, 3, PART_TILES[part]], small[:, 2, PART_TILES[part]], ACT.Sqrt).then_inc(s_sd, 1)

            def root_of_degrees(rows):
                act.wait_ge(s_var, next(roots) + 1)
                nc.scalar.activation(rd[:, rows, :], rd[:, rows, :], ACT.Sqrt).then_inc(s_sd, 1)

            root(0)
            for n, to in enumerate((off_p, w_p)):
                act.wait_ge(s_bc, n + 1)
                nc.scalar.copy(to[:, P:P + CW], ps[:, 4 * n:4 * n + 4, :].rearrange("p b n -> p (b n)")[:, 0:CW]).then_inc(s_bcs, 1)
            act.wait_ge(s_bc, 3)
            nc.scalar.copy(w_s[0:D + 1, :], ps[0:D + 1, 7, 3 * D:6 * D])
            nc.scalar.copy(bc[:, :], ps[:, 7, 0:3 * D]).then_inc(s_bcs, 1)
            proj_act(act, 0, 0)
            root(1)
            proj_act(act, 0, 1)
            for t, to in enumerate((sidx, dloc, slo, shi)):
                for j in range(0, SB, 4):
                    m = min(4, SB - j)
                    n = t * (-(-SB // 4)) + j // 4
                    act.wait_ge(s_tabt, n + 1)
                    nc.scalar.copy(to[:, j * P:(j + m) * P], ps[:, n % 2, 0:m * P]).then_inc(s_bcc, 1)
                if t == 0:
                    first_indices(act, 0)
            zero_acc_act(act, slice(U // 2, U), W0).then_inc(s_half, 1)

            s = L[0]
            act.wait_ge(s["t"], 1)
            nc.scalar.copy(oht[:, 0, :, :], ps[:, 0, :]).then_inc(s["oht"], 1)
            with act.Fori(0, ROUNDS) as i:
                for k in range(R):
                    b = k % 2
                    act.wait_ge(s["t"], i * R + k + 2)
                    nc.scalar.copy(oht[:, 1 - b, :, :], ps[:, 1 - b, :]).then_inc(s["oht"], 1)
                    act.wait_ge(s["clip"], i * R + k + 1)
                    act.wait_ge(s["agg"], i * R + k + 3)
                    nc.scalar.activation(msg[:, b, :, D:D + HEADS],
                                         sc[:, b, 1, :].rearrange("p (u h) -> p u h", h=HEADS), ACT.Exp, scale=SCALE).then_inc(s["exp"], 1)
                    next_indices(act, 0, i, k)
            for part in range(2):
                proj_act(act, 1, part)
            root_of_degrees(slice(0, 2))
            root(0)
            root(1)
            root(0)
            proj_act(act, 2, 0)
            root(1)
            proj_act(act, 2, 1)
            first_indices(act, 1)
            with act.Fori(0, ROUNDS) as i:
                for k in range(R):
                    next_indices(act, 1, i, k)
            root_of_degrees(slice(2, 3))
            root(0)
            proj_act(act, 3, 0)
            root(1)
            proj_act(act, 3, 1)

            s = L[2]
            first_indices(act, 2)
            act.wait_ge(s["t"], 1)
            nc.scalar.copy(oht[:, 0, :, :], ps[:, 0, :]).then_inc(s["oht"], 1)
            act.wait_ge(s_atc, R + 1)
            nc.scalar.copy(attT[:, 0, :], ps[:, 6, 0:P]).then_inc(s["clip"], 1)
            with act.Fori(0, ROUNDS) as i:
                for k in range(R):
                    b = k % 2
                    act.wait_ge(s["t"], i * R + k + 2)
                    nc.scalar.copy(oht[:, 1 - b, :, :], ps[:, 1 - b, :]).then_inc(s["oht"], 1)
                    act.wait_ge(s_atc, i * R + k + 2 + R)
                    nc.scalar.copy(attT[:, 1 - b, :], ps[:, 7 - b, 0:P]).then_inc(s["clip"], 1)
                    act.wait_ge(s["used"], i * R + k + 5)
                    act.wait_ge(s["agg"], i * R + k + 3)
                    nc.scalar.activation(msg[:, b, :, 0:D], prod[:, b, :].rearrange("p (u d) -> p u d", d=D), ACT.Relu).then_inc(s["exp"], 1)
                    next_indices(act, 2, i, k)
            gates = flat[:, 0:TILES * 4 * D].rearrange("p (t c) -> p t c", c=4 * D)

            def sigmoids(part):
                act.wait_ge(PJ[4]["ev"], PARTS[part][1])
                a = gates[:, PART_TILES[part], 0:2 * D]
                nc.scalar.activation(a, a, ACT.Sigmoid).then_inc(s_gact, 1)

            def tanhs(part):
                act.wait_ge(s_gates, part + 1)
                a = gates[:, PART_TILES[part], 2 * D:3 * D]
                nc.scalar.activation(a, a, ACT.Tanh).then_inc(s_gact, 1)

            proj_act(act, 4, 0)
            sigmoids(0)
            proj_act(act, 4, 1)
            tanhs(0)
            sigmoids(1)
            tanhs(1)
            act.wait_ge(s_free, 1)
            zero_acc_act(act, slice(0, U // 2), D)
            root(0)
            zero_acc_act(act, slice(U // 2, U), D).then_inc(L[3]["acc"], 1)
            root(1)
            first_indices(act, 3)
            with act.Fori(0, ROUNDS) as i:
                for k in range(R):
                    next_indices(act, 3, i, k)

        @block.tensor
        def _(pe):
            pe.wait_ge(s_pool, 2)
            pe.wait_ge(s_fell, 1)
            nc.tensor.transpose(ps[0:1, 0, 0:P], fell[:, :], ident[:, :]).then_inc(s_fellt, 1)
            for n in range(2):
                pe.wait_ge(s_rows, n + 1)
                for j in range(4):
                    a, b = j * 512, min(CW, (j + 1) * 512)
                    mm = nc.tensor.matmul(ps[:, 4 * n + j, 0:b - a], ones[:, :], crow[0:1, 2 + n, a:b], start=True, stop=True)
                mm.then_inc(s_bc, 1)
            pe.wait_ge(s_w, 16 * N_WEIGHTS)
            pe.wait_ge(s_bcs, 2)
            nc.tensor.matmul(ps[:, 7, 0:3 * D], ones[:, :], brow[:, :], start=True, stop=True)
            nc.tensor.matmul(ps[0:D + 1, 7, 3 * D:6 * D], w_2[:, :], w_i[:, :], start=True, stop=True, skip_group_check=True).then_inc(s_bc, 1)
            proj_pe(pe, 0, 0)
            pe.wait_ge(s_pool, 5)
            pe.wait_ge(s_cidx, 1)
            nc.tensor.transpose(ps[0:SB, 6, 0:P], cs[:, 2, :], ident[:, :])
            nc.tensor.transpose(ps[0:SB, 6, P:2 * P], cs[:, 3, :], ident[:, :]).then_inc(s_packt, 1)
            proj_pe(pe, 0, 1)
            for t, of in enumerate((sf, df, lof, hif)):
                pe.wait_ge(s_tabs, t + 1)
                for j in range(0, SB, 4):
                    m = min(4, SB - j)
                    n = t * (-(-SB // 4)) + j // 4
                    if n >= 2:
                        pe.wait_ge(s_bcc, n - 1)
                    for e in range(m):
                        mm = nc.tensor.transpose(ps[:, n % 2, e * P:(e + 1) * P], of[:, (j + e) * P:(j + e + 1) * P], ident[:, :])
                    mm.then_inc(s_tabt, 1)
            pe.wait_ge(PJ[0]["ev"], NR)
            pe.wait_ge(s_bcc, NTAB)
            pe.wait_ge(s_packl, 32)

            s = L[0]
            zero_sums(pe, 0, 2, W0)

            pe.wait_ge(s["oh"], 1)
            turn_onehot(pe, 0, 0, 0, 0)
            with pe.Fori(0, ROUNDS) as i:
                for k in range(R):
                    b = k % 2
                    dst_rows(pe, 0, i, k, None)
                    pe.wait_ge(s["oh"], i * R + k + 2)
                    turn_onehot(pe, 0, None, (k + 1) % R, 1 - b)
                    sum_messages(pe, 0, i * R + k, (k - 1) % R, W0)
            sum_messages(pe, 0, ROUNDS * R, R - 1, W0)
            for part in range(2):
                proj_pe(pe, 1, part)
            for part in range(2):
                proj_pe(pe, 2, part)
            pe.wait_ge(PJ[2]["ev"], NR)

            s = L[1]
            zero_sums(pe, 1, 1, D)
            nc.tensor.matmul(ps[:, 6, 0:TILES], zerob[:, :], zerob[:, 0:TILES], start=True, stop=False, skip_group_check=True)
            with pe.Fori(0, ROUNDS) as i:
                for k in range(R):
                    pe.wait_ge(s["oh"], i * R + k + 1)
                    pe.wait_ge(s["land"][k], (i + 1) * 16 * U)
                    mm = sum_edges(pe, 1, i * R + k, k, D, lambda u: gat[:, k, u, 0:D])
                    for u in range(U):
                        mm = nc.tensor.matmul(ps[:, 6, 0:TILES], olo[:, k, u, :], ohi[:, k, u, :], start=False, stop=False,
                                              skip_group_check=True)
                    mm.then_inc(s["agg"], 1)
            nc.tensor.matmul(ps[:, 6, 0:TILES], zerob[:, :], zerob[:, 0:TILES], start=False, stop=True,
                             skip_group_check=True).then_inc(s_hist, 1)
            for part in range(2):
                proj_pe(pe, 3, part)
            pe.wait_ge(PJ[3]["ev"], NR)

            s = L[2]
            zero_sums(pe, 2, 2, D)
            pe.wait_ge(s["oh"], 1)
            turn_onehot(pe, 2, 0, 0, 0)
            pe.wait_ge(s_att[0], 16 * U)
            nc.tensor.transpose(ps[:, 6, 0:P], att[:, 0, :, :], ident[:, :]).then_inc(s_atc, 1)
            with pe.Fori(0, ROUNDS) as i:
                for k in range(R):
                    b, k1 = k % 2, (k + 1) % R
                    pe.wait_ge(s["clip"], i * R + k + 1)
                    dst_rows(pe, 2, i, k, lambda: nc.tensor.matmul(
                        ps[:, 2 + b, 0:U * D], attT[:, b, :], w_e[:, :], start=True, stop=False, skip_group_check=True))
                    pe.wait_ge(s["oh"], i * R + k + 2)
                    turn_onehot(pe, 2, None, k1, 1 - b)
                    if k < R - 1:
                        pe.wait_ge(s_att[k1], (i + 1) * 16 * U)
                    else:
                        pe.wait_ge(s_att[k1], (i + 2) * 16 * U)
                    nc.tensor.transpose(ps[:, 7 - b, 0:P], att[:, k1, :, :], ident[:, :]).then_inc(s_atc, 1)
                    sum_messages(pe, 2, i * R + k, (k - 1) % R, D)
            sum_messages(pe, 2, ROUNDS * R, R - 1, D)
            for part in range(2):
                proj_pe(pe, 4, part)
            pe.wait_ge(PJ[4]["ev"], NR)

            s = L[3]
            zero_sums(pe, 3, 1, D)
            with pe.Fori(0, ROUNDS) as i:
                for k in range(R):
                    pe.wait_ge(s["oh"], i * R + k + 1)
                    pe.wait_ge(s["land"][k], (i + 1) * 16 * U)
                    sum_edges(pe, 3, i * R + k, k, D, lambda u: gat[:, k, u, 0:D]).then_inc(s["agg"], 1)

        @block.vector
        def _(dve):
            v = nc.vector
            links = [0]

            def link(ins):
                links[0] += 1
                ins.then_inc(s_d, 1)
                dve.wait_ge(s_d, links[0])

            v.memset(zeros[:, :], 0.0)
            v.memset(zerob[:, :], 0.0)
            v.memset(ones[:, :], 1.0)
            v.memset(padi[0:1, 0, :], BIG)
            v.memset(padi[0:1, 1, :], 0)
            v.memset(hT[D:D + 1, :, :], 1.0)
            for w in (w_g, w_pq):
                v.memset(w[D:D + 1, :], 0.0)
            for w in (w_h, w_e):
                v.memset(w[:, :], 0.0)
            v.memset(tpk[0:1, 0:2], 0)
            v.memset(msg[:, :, :, W0 - 1:W0], 1.0)
            v.memset(xs[:, FULL:TILES, :], 0.0).then_inc(s_const, 1)
            v.memset(small[:, :, :], 0.0).then_inc(s_atc, R)

            v.memset(falls[:, OLEN - 1:OLEN], 0.0)
            link(v.memset(fell[:, :], 0.0))
            dve.wait_ge(s_order, 32)
            v.tensor_tensor(falls[:, 0:OLEN - 1], order_i[:, 0:OLEN - 1], order_i[:, 1:OLEN], ALU.is_gt)
            link(v.tensor_tensor(falls[0:OROWS - 1, OLEN - 1:OLEN], order_i[0:OROWS - 1, OLEN - 1:OLEN], next_i[0:OROWS - 1, :], ALU.is_gt))
            v.tensor_reduce(fell[0:OROWS, :], falls, AX.X, ALU.max).then_inc(s_fell, 1)
            dve.wait_ge(s_fellt, 1)
            v.tensor_reduce(unsorted[0:1, 0:1], ps[0:1, 0, 0:P], AX.X, ALU.max).then_inc(s_flag, 1)
            dve.wait_ge(s_flag, 1)
            dve.wait_ge(s_pool, 5)
            v.tensor_copy(iota[:, :], iota_i[:, :])
            link(v.tensor_copy(step[:, :], step_i[:, :]))
            dve.wait_ge(s_ends, 48)
            with dve.If(dve.value_load(unsorted[0:1, 0:1]) > 0):
                sort_dve(dve)

            dve.wait_ge(s_ends, 48)
            for a, low, high in ((off_p, -float(BIG), float(BIG)), (w_p, 0.0, 0.0)):
                v.memset(a[:, 0:P], low)
                v.memset(a[:, P + CW:P + SPAD], high)
            v.memset(crow[0:1, 3, :], 0.0)
            link(v.tensor_scalar(crow_i[:, :, :], crow_i[:, :, :], 7, None, ALU.arith_shift_right))
            link(v.tensor_copy(crow[0:1, 0:2, :], crow_i[:, :, :]))
            link(v.tensor_tensor(crow[0:1, 1, :], crow[0:1, 1, :], crow[0:1, 0, :], ALU.subtract))
            link(v.tensor_tensor_scan(crow[0:1, 2, :], crow[0:1, 1, :], crow[0:1, 3, :], 0.0, ALU.add, ALU.add))
            link(v.tensor_tensor(crow[0:1, 1, :], crow[0:1, 2, :], crow[0:1, 1, :], ALU.subtract))
            dve.wait_ge(s_pool, 5)
            v.tensor_tensor(crow[0:1, 2, :], crow[0:1, 1, :], chunk_no, ALU.add).then_inc(s_rows, 1)
            v.tensor_tensor(crow[0:1, 3, :], crow[0:1, 0, :], crow[0:1, 1, :], ALU.subtract).then_inc(s_rows, 1)

            per_node = lambda a, part: a[:, PART_TILES[part]].unsqueeze(2).to_broadcast([P, tiles_in(part), D])
            per_feature = lambda n, part: bc[:, n * D:(n + 1) * D].unsqueeze(1).to_broadcast([P, tiles_in(part), D])
            tiles_in = lambda part: PART_TILES[part].stop - PART_TILES[part].start
            cut = lambda a, part: a[:, PART_TILES[part], :]
            tmp0, tmp1 = (stage[:, n, :].rearrange("p (t d) -> p t d", d=D) for n in range(2))
            asked = [0]

            def center(a, part, t0, t1):
                sm = lambda n: small[:, n, PART_TILES[part]]
                link(v.tensor_reduce(sm(0), cut(a, part), AX.X, ALU.add))
                link(v.tensor_scalar(sm(0), sm(0), 1.0 / D, None, ALU.mult))
                link(v.tensor_tensor(cut(t0, part), cut(a, part), per_node(small[:, 0, :], part), ALU.subtract))
                link(v.tensor_tensor(cut(t1, part), cut(t0, part), cut(t0, part), ALU.mult))
                link(v.tensor_reduce(sm(2), cut(t1, part), AX.X, ALU.add))
                v.tensor_scalar(sm(2), sm(2), 1.0 / D, EPS, ALU.mult, ALU.add).then_inc(s_var, 1)
                asked[0] += 1
                return asked[0]

            def inverse(part, n):
                dve.wait_ge(s_sd, n)
                link(v.reciprocal(small[:, 1, PART_TILES[part]], small[:, 3, PART_TILES[part]]))

            def norm_relu(part, t0):
                return v.scalar_tensor_tensor(cut(h, part), cut(t0, part), 0.0, per_node(small[:, 1, :], part), ALU.max, ALU.mult)

            def last_sums(n, lag, width):
                for g in range(ROUNDS * R, ROUNDS * R + lag):
                    accumulate(dve, n, g, g % R, lag, load_tiles(dve, g - lag), width)
                dve.wait_ge(L[n]["acc"], ROUNDS * R + lag + 1)

            def edge_sums(part, width, to=None):
                a = [cut(acc[:, u, 0:TILES * width].rearrange("p (t c) -> p t c", c=width), part) for u in range(U)]
                link(v.tensor_tensor(a[0], a[0], a[1], ALU.add))
                link(v.tensor_tensor(a[2], a[2], a[3], ALU.add))
                link(v.tensor_tensor(a[0] if to is None else cut(to, part), a[0], a[2], ALU.add))
                return a[0]

            dve.wait_ge(s_rows, 2)
            dve.wait_ge(s_x, 32)
            inverse(0, center(xs, 0, y, q))
            norm_relu(0, y).then_inc(PJ[0]["ready"], 1)
            second = center(xs, 1, y, q)
            dve.wait_ge(s_bcs, 2)
            blocks = lambda a: a.rearrange("p (j e) -> p j e", e=P)
            own, before = (lambda a: blocks(a[:, P:P + SPAD])), (lambda a: blocks(a[:, 0:SPAD])[:, :, P - LAG:P])
            by_step = lambda n: step[:, :].unsqueeze(2).to_broadcast([P, SB, n])
            v.tensor_tensor(mask[:, :, 0:LAG], before(off_p), by_step(LAG), ALU.is_le)
            link(v.tensor_tensor(mask[:, :, LAG:WIN], own(off_p), by_step(P), ALU.is_le))
            link(v.tensor_reduce(cs[:, 0, :], mask, AX.X, ALU.add))
            v.tensor_tensor(mask[:, :, 0:LAG], mask[:, :, 0:LAG], before(w_p), ALU.mult)
            link(v.tensor_tensor(mask[:, :, LAG:WIN], mask[:, :, LAG:WIN], own(w_p), ALU.mult))
            link(v.tensor_reduce(cs[:, 1, :], mask, AX.X, ALU.max))
            link(v.tensor_tensor(cs[:, 0, :], cs[:, 0, :], step[:, :], ALU.add))
            link(v.tensor_scalar(cs[:, 3, :], cs[:, 0, :], step[:, 0:1], -float(LAG + 1), ALU.subtract, ALU.add))
            link(v.tensor_tensor(cs[:, 4, :], cs[:, 1, :], step[:, :], ALU.add))
            link(v.tensor_tensor(cs[:, 4, :], cs[:, 4, :], cs[:, 3, :], ALU.subtract))
            link(v.tensor_scalar(cs[:, 2, :], cs[:, 4, :], float(TILES - 1), None, ALU.min))
            link(v.tensor_scalar(cs[:, 5, :], cs[:, 4, :], float(P), None, ALU.mult))
            v.tensor_copy(cs_i[:, :], cs[:, 3, :]).then_inc(s_cidx, 1)
            inverse(1, second)
            norm_relu(1, y).then_inc(PJ[0]["ready"], 1)
            dve.wait_ge(s_packt, 1)
            link(v.tensor_copy(packf[:, 0:2, :], ps[0:SB, 6, 0:2 * P].rearrange("p (a b) -> p a b", b=P)))
            t4 = packf[:, 0, :].rearrange("p (g u) -> p g u", u=4)
            c2 = packf[:, 1, :].rearrange("p (g u) -> p g u", u=2)
            G4 = P // U
            for m in range(2):
                link(v.scalar_tensor_tensor(packf[:, 2, m * G4:(m + 1) * G4], t4[:, :, 2 * m + 1], float(TILE_BITS), t4[:, :, 2 * m],
                                            ALU.mult, ALU.add))
            v.scalar_tensor_tensor(pack_i[:, 0:G4], packf[:, 2, G4:2 * G4], float(TILE_BITS ** 2), packf[:, 2, 0:G4],
                                   ALU.mult, ALU.add).then_inc(s_packed, 1)
            v.scalar_tensor_tensor(pack_i[:, G4:G4 + P // 2], c2[:, :, 1], float(CHUNK_BITS), c2[:, :, 0],
                                   ALU.mult, ALU.add).then_inc(s_packed, 1)
            dve.wait_ge(s_eg, 16 * SB)
            dve.wait_ge(s_eg2, 16 * SB)
            v.tensor_copy(sf, sg).then_inc(s_tabs, 1)
            link(v.tensor_copy(df, dg))
            v.tensor_tensor(blocks(df), blocks(df), cs[:, 5, :].unsqueeze(2).to_broadcast([P, SB, P]), ALU.subtract).then_inc(s_tabs, 1)
            link(v.tensor_scalar(lo_i, sg, P - 1, None, ALU.bitwise_and))
            v.tensor_copy(lof, lo_i).then_inc(s_tabs, 1)
            dve.wait_ge(s_tabs, 3)
            link(v.tensor_scalar(vf, df, 0.0, None, ALU.is_ge))
            link(v.scalar_tensor_tensor(vf, df, float(P), vf, ALU.is_lt, ALU.mult))
            link(v.tensor_scalar(vf, vf, -OUTSIDE, OUTSIDE, ALU.mult, ALU.add))
            link(v.tensor_scalar(hi_i, sg, 7, None, ALU.arith_shift_right))
            link(v.tensor_copy(hif, hi_i))
            v.tensor_tensor(hif, hif, vf, ALU.add).then_inc(s_tabs, 1)

            s = L[0]
            dve.wait_ge(PJ[0]["ev"], NR)
            zero_group(dve, 0)
            dve.wait_ge(s_bcc, NTAB)
            one_hot(dve, 0, 0, 0)
            zero_acc(dve, 0, W0, U // 2)
            dve.wait_ge(L[0]["acc"], 1)
            dve.wait_ge(s_half, 1)
            dve.wait_ge(s_packl, 32)

            def weigh_values(g, k1):
                c = k1 % 2
                dve.wait_ge(s["exp"], g + 1)
                v.tensor_tensor(
                    msg[:, c, :, 0:D].rearrange("p u (h d) -> p u h d", d=DH),
                    gat[:, k1, :, D:2 * D].rearrange("p u (h d) -> p u h d", d=DH),
                    msg[:, c, :, D:D + HEADS].unsqueeze(3).to_broadcast([P, U, HEADS, DH]), ALU.mult).then_inc(s["used"], 1)

            with dve.Fori(0, ROUNDS) as i:
                for k in range(R):
                    g, b = i * R + k, k % 2
                    dve.wait_ge(s["agg"], g + 2)
                    one_hot(dve, 0, i, k + 1)
                    weigh_values(g, (k - 1) % R)
                    places = load_tiles(dve, g - 2)
                    dve.wait_ge(s["land"][k], (i + 1) * 16 * U)
                    dve.wait_ge(s["qe"], g + 1)
                    v.tensor_tensor(prod[:, b, :].rearrange("p (u d) -> p u d", d=D),
                                    ps[:, 2 + b, 0:U * D].rearrange("p (u d) -> p u d", d=D), gat[:, k, :, 0:D],
                                    ALU.mult).then_inc(s["prod"], 1)
                    accumulate(dve, 0, g, k, 2, places, W0, range(U // 2))
                    dve.wait_ge(s["prod"], g + 1)
                    v.tensor_reduce(sc[:, b, 0, :], prod[:, b, :].rearrange("p (a d) -> p a d", d=DH), AX.X, ALU.add).then_inc(s["red"], 1)
                    accumulate(dve, 0, g, k, 2, places, W0, range(U // 2, U))
                    dve.wait_ge(s["red"], g + 1)
                    v.tensor_scalar(sc[:, b, 1, :], sc[:, b, 0, :], -CLIP, CLIP, ALU.max, ALU.min).then_inc(s["clip"], 1)
            weigh_values(ROUNDS * R, R - 1)
            last_sums(0, 2, W0)
            for part in range(2):
                a0, tiles, n = edge_sums(part, W0), PART_TILES[part], tiles_in(part)
                v.tensor_copy(cnt[:, tiles], a0[:, :, W0 - 1])
                link(v.tensor_scalar(z1[:, tiles, :], a0[:, :, D:D + HEADS], 1.0, None, ALU.add))
                link(v.reciprocal(z1[:, tiles, :], z1[:, tiles, :]))
                v.tensor_tensor(cut(h, part).rearrange("p t (a d) -> p t a d", d=DH), a0[:, :, 0:D].rearrange("p t (a d) -> p t a d", d=DH),
                                z1[:, tiles, :].unsqueeze(3).to_broadcast([P, n, HEADS, DH]), ALU.mult).then_inc(PJ[1]["ready"], 1)
            dve.wait_ge(PJ[1]["ready"], 2)
            zero_acc(dve, 1, D)
            v.tensor_scalar(rd[:, 0, :], cnt[:, :], 1.0, None, ALU.add)
            v.tensor_scalar(rd[:, 1, :], cnt[:, :], 1.0, None, ALU.max).then_inc(s_var, 1)
            asked[0] += 1
            degrees, n = asked[0], []
            for part, (_, end) in enumerate(PARTS):
                dve.wait_ge(PJ[1]["ev"], end)
                link(v.tensor_tensor(cut(y, part), cut(y, part), cut(tmp0, part), ALU.add))
                n.append(center(y, part, tmp0, tmp1))
            dve.wait_ge(s_bcs, 3)
            dve.wait_ge(s_sd, degrees)
            link(v.reciprocal(rd[:, 0:2, :], rd[:, 0:2, :]))
            for part in range(2):
                t0 = cut(tmp0, part)
                inverse(part, n[part])
                link(v.tensor_tensor(t0, t0, per_node(small[:, 1, :], part), ALU.mult))
                link(v.tensor_tensor(t0, t0, per_feature(0, part), ALU.mult))
                link(v.tensor_tensor(t0, t0, per_feature(1, part), ALU.add))
                link(v.tensor_tensor(t0, t0, cut(y, part), ALU.add))
                link(v.tensor_tensor(cut(xs, part), cut(xs, part), t0, ALU.add))
                inverse(part, center(xs, part, tmp0, tmp1))
                norm_relu(part, tmp0).then_inc(PJ[2]["ready"], 1)

            for part, (_, end) in enumerate(PARTS):
                dve.wait_ge(PJ[2]["ev"], end)
                v.tensor_tensor(cut(y, part), cut(y, part), per_node(rd[:, 0, :], part), ALU.mult).then_inc(s_stage, 1)
            s = L[1]
            dve.wait_ge(s["acc"], 1)
            one_hot(dve, 1, 0, 0, True)
            with dve.Fori(0, ROUNDS) as i:
                for k in range(R):
                    dve.wait_ge(s["agg"], i * R + k + 2)
                    one_hot(dve, 1, i, k + 1, True)
                    places = load_tiles(dve, i * R + k - 1)
                    accumulate(dve, 1, i * R + k, k, 1, places, D)
            last_sums(1, 1, D)
            dve.wait_ge(s_hist, 1)
            v.tensor_scalar(rd[:, 2, :], ps[:, 6, 0:TILES], 1.0, None, ALU.max).then_inc(s_var, 1)
            asked[0] += 1
            degrees = asked[0]
            dve.wait_ge(s_stage, 2)
            for part in range(2):
                t0 = cut(tmp0, part)
                a0 = edge_sums(part, D)
                link(v.tensor_tensor(t0, a0, cut(y, part), ALU.add))
                link(v.tensor_tensor(t0, t0, per_node(rd[:, 0, :], part), ALU.mult))
                link(v.tensor_tensor(t0, t0, per_feature(2, part), ALU.add))
                link(v.scalar_tensor_tensor(cut(xs, part), t0, 0.0, cut(xs, part), ALU.max, ALU.add))
                n = center(xs, part, tmp0, tmp1)
                if part == 1:
                    zero_acc(dve, 2, D)
                inverse(part, n)
                norm_relu(part, tmp0).then_inc(PJ[3]["ready"], 1)

            s = L[2]
            dve.wait_ge(s_sd, degrees)
            v.reciprocal(rd[:, 2, :], rd[:, 2, :])
            zero_group(dve, 2)
            one_hot(dve, 2, 0, 0)
            dve.wait_ge(s["acc"], 1)
            with dve.Fori(0, ROUNDS) as i:
                for k in range(R):
                    g, b = i * R + k, k % 2
                    dve.wait_ge(s["agg"], g + 2)
                    one_hot(dve, 2, i, k + 1)
                    places = load_tiles(dve, g - 2)
                    dve.wait_ge(s["agg"], g + 3)
                    dve.wait_ge(s["land"][k], (i + 1) * 16 * U)
                    dve.wait_ge(s["qe"], g + 1)
                    v.tensor_tensor(prod[:, b, :].rearrange("p (u d) -> p u d", d=D), ps[:, 2 + b, 0:U * D].rearrange("p (u d) -> p u d", d=D),
                                    gat[:, k, :, 0:D], ALU.add).then_inc(s["used"], 1)
                    accumulate(dve, 2, g, k, 2, places, D)
            last_sums(2, 2, D)
            link(v.memset(hb_sums[:, :, D + 1:D + 2], 1.0))
            for part in range(2):
                edge_sums(part, D, y)
                v.memset(fell[:, :], 0.0).then_inc(PJ[4]["ready"], 1)
                dve.wait_ge(PJ[4]["ready"], part + 1)
            gates = flat[:, 0:TILES * 4 * D].rearrange("p (t c) -> p t c", c=4 * D)
            gate = lambda n, part: cut(gates[:, :, n * D:(n + 1) * D], part)

            def blend(part):
                dve.wait_ge(s_gact, (2, 4)[part])
                t0 = cut(tmp0, part)
                link(v.tensor_tensor(t0, cut(h, part), gate(2, part), ALU.subtract))
                link(v.tensor_tensor(t0, t0, gate(1, part), ALU.mult))
                link(v.tensor_tensor(t0, t0, gate(2, part), ALU.add))
                link(v.tensor_tensor(cut(xs, part), cut(xs, part), t0, ALU.add))

            for part in range(2):
                dve.wait_ge(s_gact, 1 + 2 * part)
                link(v.tensor_tensor(gate(3, part), gate(3, part), gate(0, part), ALU.mult))
                v.tensor_tensor(gate(2, part), gate(2, part), gate(3, part), ALU.add).then_inc(s_gates, 1)
                if part == 1:
                    blend(0)
            blend(1)
            v.memset(fell[:, :], 0.0).then_inc(s_free, 1)

            for part in range(2):
                inverse(part, center(xs, part, tmp0, tmp1))
                link(norm_relu(part, tmp0))
                v.tensor_tensor(cut(tmp0, part), cut(h, part), per_node(rd[:, 2, :], part), ALU.mult).then_inc(s_stage, 1)
            s = L[3]
            one_hot(dve, 3, 0, 0)
            dve.wait_ge(s["acc"], 1)
            with dve.Fori(0, ROUNDS) as i:
                for k in range(R):
                    dve.wait_ge(s["agg"], i * R + k + 2)
                    one_hot(dve, 3, i, k + 1)
                    places = load_tiles(dve, i * R + k - 1)
                    accumulate(dve, 3, i * R + k, k, 1, places, D)
            last_sums(3, 1, D)
            for part in range(2):
                a0, t0 = edge_sums(part, D), cut(tmp1, part)
                link(v.tensor_tensor(t0, a0, per_node(rd[:, 1, :], part), ALU.mult))
                v.tensor_tensor(cut(xs, part), cut(xs, part), t0, ALU.add).then_inc(s_fin, 1)


_L0 = ["Wq", "bq", "Wk", "bk", "Wv", "bv", "Wo", "bo", "Wf", "bf", "gamma", "beta"]


def kernel(**inputs):
    import numpy as _np
    import concourse.bacc as _bacc
    from concourse import mybir as _mybir
    from concourse.bass_utils import run_bass_kernel_spmd as _run

    arrays = {n: inputs[n] for n in ("x", "src", "dst", "edge_attr_32")}
    arrays |= {n: inputs["L0_gnn_" + n] for n in _L0}
    arrays |= {"W_gcn": inputs["L1_gnn_W"], "b_gcn": inputs["L1_gnn_b"]}
    for n in ("W1", "b1", "W2", "b2", "w_ih", "w_hh", "b_ih", "b_hh"):
        a = _np.asarray(inputs["L2_gnn_" + n])
        arrays["e_" + n] = a.T if a.ndim == 2 and n != "W2" else a
    order = ["x", "src", "dst", "edge_attr_32", *_L0, "W_gcn", "b_gcn", "e_W1", "e_b1", "e_W2", "e_b2", "e_w_ih", "e_w_hh", "e_b_ih", "e_b_hh"]
    nc = _bacc.Bacc("TRN2", target_bir_lowering=False, num_devices=1)
    given, args = {}, []
    for n in order:
        a = _np.ascontiguousarray(arrays[n])
        given[f"in_{n}"] = a
        args.append(nc.dram_tensor(f"in_{n}", a.shape, _mybir.dt.from_np(a.dtype), kind="ExternalInput").ap())
    args.append(nc.dram_tensor("out_0", (NODES, D), F32, kind="ExternalOutput").ap())
    build_gnn(nc, *args)
    r = _run(nc, [given], core_ids=[0])
    return r.results[0]["out_0"]
```
